# Optimizing a Trainium2 kernel written in Bass

```python
import numpy as np
import jax
import jax.numpy as jnp

def _softmax(x, axis=-1):
    return jax.nn.softmax(x, axis=axis)

def _gelu(x):
    return jax.nn.gelu(x, approximate=True)

def _silu(x):
    return jax.nn.silu(x)

def _sigmoid(x):
    return jax.nn.sigmoid(x)

def _layernorm(x, axis=-1, eps=1e-05):
    m = jnp.mean(x, axis=axis, keepdims=True)
    v = jnp.var(x, axis=axis, keepdims=True)
    return (x - m) / jnp.sqrt(v + eps)

def _scatter_add(tgt, idx, src, axis=0):
    return tgt.at[idx].add(src)

def _segment_sum(src, seg, n):
    return jax.ops.segment_sum(src, seg, n)
kernel_name = 'mk_conv_preact_d4_conv_nchw512_r2_067964'

def setup_inputs(seed: int=0):
    np.random.seed(seed)
    _w = jnp.asarray

    def _rec_inputs():
        import jax
        import jax.numpy as jnp
        _gk = jax.random.key(seed)
        x = -0.0003957 + 1 * jax.random.normal(jax.random.fold_in(_gk, 1), (256, 256, 7, 7), jnp.float32)
        return x
    x = _rec_inputs()

    def _L0_conv_setup():
        import jax, jax.numpy as jnp
        from jax import lax
        import numpy as np
        NUM_CLASSES = 42871
        C = 256
        KH = KW = 1
        B = 256
        H = W = 7
        key = jax.random.key(seed)
        kx, kw = jax.random.split(key)
        x = jax.random.normal(kx, (B, C, H, W), dtype=jnp.float32)
        labels = jnp.arange(B, dtype=jnp.int64)
        weight = jax.random.normal(kw, (NUM_CLASSES, C, KH, KW), dtype=jnp.float32) * 0.02
        bias = jnp.zeros((NUM_CLASSES,), dtype=jnp.float32)
        return {'x': x, 'labels': labels, 'weight': weight, 'bias': bias}
    _L0_conv_all = _L0_conv_setup()
    _L0_conv_in = {k: v for k, v in _L0_conv_all.items() if k in ('labels', 'weight', 'bias')}
    del _L0_conv_all

    def _L1_conv_setup():
        import jax, jax.numpy as jnp
        import numpy as np
        DIM = 16
        EPS = 1e-15
        BN_EPS = 1e-05

        def _conv(x, w, groups=1):
            return jax.lax.conv_general_dilated(x, w, window_strides=(1, 1), padding='SAME', feature_group_count=groups, dimension_numbers=('NCHW', 'OIHW', 'NCHW'))
        key = jax.random.key(seed)
        ks = jax.random.split(key, 5)
        B, Cin, H, W = (8, 256, 32, 32)
        total_dim = 256
        C3 = 3 * total_dim
        x = jax.random.normal(ks[0], (B, Cin, H, W), dtype=jnp.float32)
        w_qkv = jax.random.normal(ks[1], (C3, Cin, 1, 1), dtype=jnp.float32) * 0.02
        w_dw = jax.random.normal(ks[2], (C3, 1, 5, 5), dtype=jnp.float32) * 0.02
        w_pw = jax.random.normal(ks[3], (C3, C3 // (3 * DIM), 1, 1), dtype=jnp.float32) * 0.02
        w_proj = jax.random.normal(ks[4], (256, 2 * total_dim, 1, 1), dtype=jnp.float32) * 0.02
        bn_gamma = jnp.ones((256,), jnp.float32)
        bn_beta = jnp.zeros((256,), jnp.float32)
        bn_mean = jnp.zeros((256,), jnp.float32)
        bn_var = jnp.ones((256,), jnp.float32)
        return {'x': x, 'w_qkv': w_qkv, 'w_dw': w_dw, 'w_pw': w_pw, 'w_proj': w_proj, 'bn_gamma': bn_gamma, 'bn_beta': bn_beta, 'bn_mean': bn_mean, 'bn_var': bn_var}
    _L1_conv_all = _L1_conv_setup()
    _L1_conv_in = {k: v for k, v in _L1_conv_all.items() if k in ('w_qkv', 'w_dw', 'w_pw', 'w_proj', 'bn_gamma', 'bn_beta', 'bn_mean', 'bn_var')}
    del _L1_conv_all

    def _L2_conv_setup():
        import jax, jax.numpy as jnp
        import numpy as np
        GROUPS = 32
        LOG_2PI = float(np.log(2.0 * np.pi))
        key = jax.random.key(seed)
        ks = jax.random.split(key, 5)
        b, c, h, w = (32, 256, 56, 56)
        g = GROUPS
        return {'x': jax.random.normal(ks[0], (b, c, h, w), dtype=jnp.float32), 'weight': jax.random.normal(ks[1], (1, g, 1, 1), dtype=jnp.float32), 'bias': jnp.ones((1, g, 1, 1), dtype=jnp.float32), 'one': jnp.ones((1, g, 1), dtype=jnp.float32), 'zero': jax.random.normal(ks[2], (1, g, 1), dtype=jnp.float32), 'theta': jax.random.uniform(ks[3], (1, 2, 1, 1), dtype=jnp.float32), 'scale': jnp.ones((1,), dtype=jnp.float32)}
    _L2_conv_all = _L2_conv_setup()
    _L2_conv_in = {k: v for k, v in _L2_conv_all.items() if k in ('weight', 'bias', 'one', 'zero', 'theta', 'scale')}
    del _L2_conv_all

    def _L3_conv_setup():
        import jax, jax.numpy as jnp
        import numpy as np
        B, C, H, W = (4, 256, 32, 32)
        CK = C // 8
        key = jax.random.key(seed)
        k1, k2, k3, k4, k5 = jax.random.split(key, 5)
        x = jax.random.normal(k1, (B, C, H, W), dtype=jnp.float32)
        Wq = jax.random.normal(k2, (CK, C), dtype=jnp.float32) * (1.0 / np.sqrt(C))
        Wk = jax.random.normal(k3, (CK, C), dtype=jnp.float32) * (1.0 / np.sqrt(C))
        Wv = jax.random.normal(k4, (C, C), dtype=jnp.float32) * (1.0 / np.sqrt(C))
        gamma = jax.random.normal(k5, (1,), dtype=jnp.float32)
        return {'x': x, 'Wq': Wq, 'Wk': Wk, 'Wv': Wv, 'gamma': gamma}
    _L3_conv_all = _L3_conv_setup()
    _L3_conv_in = {k: v for k, v in _L3_conv_all.items() if k in ('Wq', 'Wk', 'Wv', 'gamma')}
    del _L3_conv_all
    return {'x': x, 'L0_conv_labels': _L0_conv_in['labels'], 'L0_conv_weight': _L0_conv_in['weight'], 'L0_conv_bias': _L0_conv_in['bias'], 'L1_conv_w_qkv': _L1_conv_in['w_qkv'], 'L1_conv_w_dw': _L1_conv_in['w_dw'], 'L1_conv_w_pw': _L1_conv_in['w_pw'], 'L1_conv_w_proj': _L1_conv_in['w_proj'], 'L1_conv_bn_gamma': _L1_conv_in['bn_gamma'], 'L1_conv_bn_beta': _L1_conv_in['bn_beta'], 'L1_conv_bn_mean': _L1_conv_in['bn_mean'], 'L1_conv_bn_var': _L1_conv_in['bn_var'], 'L2_conv_weight': _L2_conv_in['weight'], 'L2_conv_bias': _L2_conv_in['bias'], 'L2_conv_one': _L2_conv_in['one'], 'L2_conv_zero': _L2_conv_in['zero'], 'L2_conv_theta': _L2_conv_in['theta'], 'L2_conv_scale': _L2_conv_in['scale'], 'L3_conv_Wq': _L3_conv_in['Wq'], 'L3_conv_Wk': _L3_conv_in['Wk'], 'L3_conv_Wv': _L3_conv_in['Wv'], 'L3_conv_gamma': _L3_conv_in['gamma']}

def reference(x, L0_conv_labels, L0_conv_weight, L0_conv_bias, L1_conv_w_qkv, L1_conv_w_dw, L1_conv_w_pw, L1_conv_w_proj, L1_conv_bn_gamma, L1_conv_bn_beta, L1_conv_bn_mean, L1_conv_bn_var, L2_conv_weight, L2_conv_bias, L2_conv_one, L2_conv_zero, L2_conv_theta, L2_conv_scale, L3_conv_Wq, L3_conv_Wk, L3_conv_Wv, L3_conv_gamma):
    import jax
    import jax.numpy as jnp

    def _L0_conv_ref(x, labels, weight, bias):
        import jax, jax.numpy as jnp
        from jax import lax
        import numpy as np
        NUM_CLASSES = 42871
        C = 256
        KH = KW = 1
        B = 256
        H = W = 7
        labels_unique = jnp.unique(labels, size=labels.shape[0], fill_value=0)
        w_sub = weight[labels_unique]
        b_sub = bias[labels_unique]
        logits = lax.conv_general_dilated(x, w_sub, window_strides=(1, 1), padding='VALID', dimension_numbers=('NCHW', 'OIHW', 'NCHW'))
        return logits + b_sub[None, :, None, None]

    def _L1_conv_ref(x, w_qkv, w_dw, w_pw, w_proj, bn_gamma, bn_beta, bn_mean, bn_var):
        import jax, jax.numpy as jnp
        import numpy as np
        DIM = 16
        EPS = 1e-15
        BN_EPS = 1e-05

        def _conv(x, w, groups=1):
            return jax.lax.conv_general_dilated(x, w, window_strides=(1, 1), padding='SAME', feature_group_count=groups, dimension_numbers=('NCHW', 'OIHW', 'NCHW'))
        qkv = _conv(x, w_qkv)
        C3 = qkv.shape[1]
        agg = _conv(_conv(qkv, w_dw, groups=C3), w_pw, groups=3 * DIM)
        qkv = jnp.concatenate([qkv, agg], axis=1)
        B, _, H, W = qkv.shape
        S = H * W
        qkv = qkv.reshape(B, -1, 3 * DIM, S)
        q, k, v = jnp.split(qkv, 3, axis=2)
        q = jax.nn.relu(q)
        k = jax.nn.relu(k)
        v = jnp.concatenate([v, jnp.ones_like(v[:, :, :1])], axis=2)
        vk = jnp.einsum('bhds,bhes->bhde', v, k)
        out = jnp.einsum('bhde,bhes->bhds', vk, q)
        out = out[:, :, :-1] / (out[:, :, -1:] + EPS)
        out = out.reshape(B, -1, H, W)
        y = _conv(out, w_proj)
        inv = bn_gamma / jnp.sqrt(bn_var + BN_EPS)
        y = y * inv[:, None, None] + (bn_beta - bn_mean * inv)[:, None, None]
        return y

    def _L2_conv_ref(x, weight, bias, one, zero, theta, scale):
        import jax, jax.numpy as jnp
        import numpy as np
        GROUPS = 32
        LOG_2PI = float(np.log(2.0 * np.pi))
        b, c, h, w = x.shape
        g = GROUPS
        cg = c // g
        hw = h * w
        bg = b * g
        v = x.reshape(bg, cg, hw)
        s = v.sum(axis=1)
        idx = jnp.argmax(s, axis=1)
        q_row = idx // w
        q_col = idx % w
        q_val = jnp.take_along_axis(v, idx[:, None, None], axis=2)[..., 0]
        sim_max = jnp.einsum('nc,ncs->ns', q_val, v)
        gap = v.mean(axis=2)
        sim_gap = jnp.einsum('nc,ncs->ns', gap, v)
        rows = jnp.arange(h, dtype=x.dtype)[:, None] * jnp.ones((1, w), dtype=x.dtype)
        cols = jnp.ones((h, 1), dtype=x.dtype) * jnp.arange(w, dtype=x.dtype)[None, :]
        pos = jnp.stack([rows, cols], axis=0)
        q_pos = jnp.stack([q_row, q_col], axis=1).astype(x.dtype)
        dist = jnp.abs(pos[None] - q_pos[:, :, None, None]) * theta
        sc = scale[0]
        gauss = jnp.exp(-0.5 * (dist / sc) ** 2 - jnp.log(sc) - 0.5 * LOG_2PI)
        D = gauss.mean(axis=1).reshape(b, g, hw)
        sim = sim_max.reshape(b, g, hw) * D * zero + sim_gap.reshape(b, g, hw) * one
        ctx = sim - sim.mean(axis=2, keepdims=True)
        std = jnp.std(sim, axis=2, keepdims=True, ddof=1) + 1e-05
        ctx = (ctx / std).reshape(b, g, h, w) * weight + bias
        gate = jax.nn.sigmoid(ctx)[:, :, None, :, :]
        gate = jnp.broadcast_to(gate, (b, g, cg, h, w)).reshape(b, c, h, w)
        return x * gate

    def _L3_conv_ref(x, Wq, Wk, Wv, gamma):
        import jax, jax.numpy as jnp
        import numpy as np
        B, C, H, W = (4, 256, 32, 32)
        CK = C // 8
        b, c, h, w = x.shape
        xf = x.reshape(b, c, h * w)
        f = jnp.einsum('oc,bcn->bon', Wq, xf)
        g = jnp.einsum('oc,bcn->bon', Wk, xf)
        hh = jnp.einsum('oc,bcn->bon', Wv, xf)
        scores = jnp.einsum('bki,bkj->bij', f, g)
        beta = jax.nn.softmax(scores, axis=1)
        o = jnp.einsum('bci,bij->bcj', hh, beta)
        out = gamma[0] * o + xf
        return out.reshape(b, c, h, w)

    def _gn(v, G=32, eps=1e-05):
        B_, C_, H_, W_ = v.shape
        g = v.reshape(B_, G, C_ // G, H_, W_)
        m = jnp.mean(g, axis=(2, 3, 4), keepdims=True)
        s = jnp.var(g, axis=(2, 3, 4), keepdims=True)
        return ((g - m) / jnp.sqrt(s + eps)).reshape(v.shape)

    def _ln_c(v, eps=1e-06):
        m = jnp.mean(v, axis=1, keepdims=True)
        s = jnp.var(v, axis=1, keepdims=True)
        return (v - m) / jnp.sqrt(s + eps)

    def _ln_t(v, eps=1e-05):
        m = jnp.mean(v, axis=-1, keepdims=True)
        s = jnp.var(v, axis=-1, keepdims=True)
        return (v - m) / jnp.sqrt(s + eps)

    def _to_tokens(v):
        B_, C_, H_, W_ = v.shape
        return v.reshape(B_, C_, H_ * W_).transpose(0, 2, 1)

    def _from_tokens(t, like):
        B_, C_, H_, W_ = like.shape
        return t.transpose(0, 2, 1).reshape(B_, C_, H_, W_)
    x = x + _L0_conv_ref(_gn(x), L0_conv_labels, L0_conv_weight, L0_conv_bias)
    x = x + _L1_conv_ref(_gn(x), L1_conv_w_qkv, L1_conv_w_dw, L1_conv_w_pw, L1_conv_w_proj, L1_conv_bn_gamma, L1_conv_bn_beta, L1_conv_bn_mean, L1_conv_bn_var)
    x = x + _L2_conv_ref(_gn(x), L2_conv_weight, L2_conv_bias, L2_conv_one, L2_conv_zero, L2_conv_theta, L2_conv_scale)
    x = x + _L3_conv_ref(_gn(x), L3_conv_Wq, L3_conv_Wk, L3_conv_Wv, L3_conv_gamma)
    return x

_drawn_inputs = setup_inputs


def setup_inputs(seed=0):
    import zlib

    import numpy as np

    out = dict(_drawn_inputs(seed))
    spreads = {'L0_conv_bias': (0.0, 0.1),
     'L1_conv_bn_gamma': (1.0, 0.6),
     'L1_conv_bn_beta': (0.0, 0.1),
     'L1_conv_bn_mean': (0.0, 0.1),
     'L1_conv_bn_var': (1.0, 0.6),
     'L2_conv_bias': (1.0, 0.6),
     'L2_conv_one': (1.0, 0.6)}
    factors = {'L1_conv_w_dw': 28.992, 'L1_conv_w_pw': 27.904, 'L2_conv_theta': 88.44}
    for name, (base, spread) in spreads.items():
        noise = np.random.default_rng([zlib.crc32(name.encode()), seed]).standard_normal(out[name].shape)
        drawn = base * np.exp(spread * noise) if base else spread * noise
        out[name] = jnp.asarray(drawn.astype(out[name].dtype))
    for name, factor in factors.items():
        out[name] = (out[name] * factor).astype(out[name].dtype)
    return out
```

```python
C = 256
HW = 7
S = HW * HW
NB = 16
YB = HW * NB
COLS = S * NB
HALF = COLS // 2
KT = C // 128
GS = 8
D = 16
MT = 6
TAPS = 5
PR = 2 * S
VO = 128 + 8
QP = NB // 4
XC = HW * D
BIG = 1e30


def pair_of(ap, b):
    return ap.rearrange("p (r b) -> p b r", b=8)[:, b, :]


def settle(eng, met):
    eng.sem_inc(met, 1)


def setup_phase(nc, bass, mybir, ins, W, n_classes):
    from contextlib import ExitStack
    f32, i32 = mybir.dt.float32, mybir.dt.int32
    ALU = mybir.AluOpType
    AX = mybir.AxisListType
    ctx = ExitStack()
    with ctx:
        def sb(name, shape, dt=f32):
            return ctx.enter_context(nc.sbuf_tensor(name, shape, dt))

        def ps(name, shape):
            return ctx.enter_context(nc.psum_tensor(name, shape, f32))

        def sem(name):
            return ctx.enter_context(nc.semaphore(name))

        lab_row_i = sb("lab_row_i", [128, C], i32)
        lab_col_i = sb("lab_col_i", [128, KT], i32)
        lab_row = sb("lab_row", [128, C])
        lab_col = sb("lab_col", [128, KT])
        earlier = sb("earlier", [128, KT, C])
        same = sb("same", [128, KT, C])
        greater = sb("greater", [128, KT, C])
        place = sb("place", [128, KT, C])
        iota = sb("iota", [128, C])
        dups = sb("dups", [128, KT])
        first = sb("first", [128, KT])
        rank = sb("rank", [128, KT])
        uniq = sb("uniq", [128, KT])
        wrapped = sb("wrapped", [128, KT])
        negative = sb("negative", [128, KT])
        index = sb("index", [128, KT], i32)
        rows = sb("rows", [128, KT, C])
        pw = sb("pw", [XC, 48, D])
        dw = sb("dw", [XC, 48 * TAPS, TAPS])
        dwx = sb("dwx", [XC, 48 * TAPS, HW])
        taps = sb("taps", [XC, TAPS * HW])
        bn = sb("bn", [128, 4, KT])
        bn_std = sb("bn_std", [128, KT])
        bn_t = sb("bn_t", [128, KT])
        p_rank = ps("p_rank", [128, KT])
        p_uniq = ps("p_uniq", [128, KT])
        p_w = ps("p_w", [128, KT, C])

        loaded, labels_in = sem("loaded"), sem("labels_in")
        step = sem("step_v")
        ranked, found, turned = sem("ranked"), sem("found"), sem("turned")
        first_ok, place_ok, index_ok = sem("first_ok"), sem("place_ok"), sem("index_ok")
        gathered = sem("gathered")
        bn_rooted, bn_eps = sem("bn_rooted"), sem("bn_eps")

        loads = [
            (W["w_qkv"][:, :, :], ins["w_qkv"]), (W["w_proj"][:, :, :], ins["w_proj"]),
            (W["wv"][:, :, :], ins["wv"]), (W["wqk"][:, :, :], ins["wqk"]),
            (W["mask8"][:, :], ins["c_mask8"]), (W["mask_vo"][:, :], ins["c_mask_vo"]),
            (W["ident"][:, :], ins["c_ident"]), (W["image_of"][:, :], ins["c_image_of"]),
            (taps[:, :], ins["c_taps"]), (earlier[:, :, :], ins["c_earlier"]),
            (iota[:, :], ins["c_iota"]),
            *[(pw[D * x:D * x + D, :, :], ins["w_pw"]) for x in range(HW)],
            *[(dw[D * x:D * x + D, :, :], ins["w_dw"]) for x in range(HW)],
            (bn[:, :, :], ins["bn"]),
            (W["g_par"][:, :], ins["g_par"]),
            (W["theta"][:, :], ins["theta"].partition_broadcast(32)),
            (W["gamma"][:, :], ins["gamma"].partition_broadcast(128)),
        ]
        block = ctx.enter_context(nc.Block())

        @block.sync
        def _(sp):
            sp.dma_start(lab_row_i[:, :], ins["labels"].partition_broadcast(128)).then_inc(labels_in, 16)
            sp.dma_start(lab_col_i[:, :], ins["labels_by_row"]).then_inc(labels_in, 16)
            for dst, src in loads:
                sp.dma_start(dst, src).then_inc(loaded, 16)
            sp.wait_ge(loaded, 16 * len(loads))

        @block.vector
        def _(v):
            done = [0]

            def link(ins_):
                done[0] += 1
                ins_.then_inc(step, 1)
                v.wait_ge(step, done[0])

            v.wait_ge(labels_in, 32)
            link(v.tensor_copy(lab_row[:, :], lab_row_i[:, :]))
            link(v.tensor_copy(lab_col[:, :], lab_col_i[:, :]))
            v.wait_ge(loaded, 16 * len(loads))
            for t in range(KT):
                link(v.tensor_scalar(same[:, t, :], lab_row[:, :], lab_col[:, t:t + 1], None, ALU.is_equal))
                link(v.tensor_scalar(greater[:, t, :], lab_row[:, :], lab_col[:, t:t + 1], None, ALU.is_gt))
            link(v.tensor_tensor(same[:, :, :], same[:, :, :], earlier[:, :, :], ALU.mult))
            link(v.tensor_reduce(dups[:, :], same[:, :, :], AX.X, ALU.add))
            v.tensor_scalar(first[:, :], dups[:, :], 0.0, None, ALU.is_equal).then_inc(first_ok, 1)
            v.wait_ge(ranked, 1)
            link(v.tensor_copy(rank[:, :], p_rank[:, :]))
            for t in range(KT):
                v.tensor_scalar(place[:, t, :], iota[:, :], rank[:, t:t + 1], first[:, t:t + 1],
                                ALU.is_equal, ALU.mult).then_inc(place_ok, 1)
            v.wait_ge(found, 1)
            link(v.tensor_copy(uniq[:, :], p_uniq[:, :]))
            link(v.tensor_scalar(negative[:, :], uniq[:, :], 0.0, float(n_classes), ALU.is_lt, ALU.mult))
            link(v.tensor_tensor(wrapped[:, :], uniq[:, :], negative[:, :], ALU.add))
            link(v.tensor_scalar(wrapped[:, :], wrapped[:, :], 0.0, float(n_classes - 1), ALU.max, ALU.min))
            v.tensor_copy(index[:, :], wrapped[:, :]).then_inc(index_ok, 1)
            v.wait_ge(bn_rooted, 1)
            link(v.tensor_tensor(W["bn_scale"][:, :], bn_std[:, :], bn[:, 0, :], ALU.mult))
            link(v.tensor_tensor(bn_t[:, :], bn[:, 2, :], W["bn_scale"][:, :], ALU.mult))
            link(v.tensor_tensor(W["bn_shift"][:, :], bn[:, 1, :], bn_t[:, :], ALU.subtract))
            for xo in range(HW):
                for d in range(TAPS):
                    flag = taps[:, d * HW + xo:d * HW + xo + 1]
                    if d == 0:
                        link(v.tensor_scalar(dwx[:, :, xo], dw[:, :, d], flag, None, ALU.mult))
                    else:
                        link(v.scalar_tensor_tensor(dwx[:, :, xo], dw[:, :, d], flag, dwx[:, :, xo],
                                                    ALU.mult, ALU.add))
            v4 = dwx[:, :, :].rearrange("p (g y) x -> p g (y x)", g=48)
            for g in range(0, 48, 8):
                link(v.tensor_tensor(
                    W["conv"][:, g:g + 8, :].rearrange("p g (k o) -> p g k o", o=D),
                    v4[:, g:g + 8, :].unsqueeze(3).to_broadcast([XC, 8, TAPS * HW, D]),
                    pw[:, g:g + 8, :].unsqueeze(2).to_broadcast([XC, 8, TAPS * HW, D]), ALU.mult))
            v.wait_ge(turned, 1)
            link(v.tensor_copy(W["w_sub"][:, :, :], p_w[:, :, :]))

        @block.tensor
        def _(pe):
            pe.wait_ge(first_ok, 1)
            for u in range(KT):
                for t in range(KT):
                    mm = pe.matmul(p_rank[:, u:u + 1], greater[:, t, 128 * u:128 * u + 128],
                                   first[:, t:t + 1], start=(t == 0), stop=(t == KT - 1))
            mm.then_inc(ranked, 1)
            pe.wait_ge(place_ok, KT)
            for u in range(KT):
                for t in range(KT):
                    mm = pe.matmul(p_uniq[:, u:u + 1], place[:, t, 128 * u:128 * u + 128],
                                   lab_col[:, t:t + 1], start=(t == 0), stop=(t == KT - 1))
            mm.then_inc(found, 1)
            pe.wait_ge(gathered, 64)
            for u in range(KT):
                for t in range(KT):
                    mm = pe.transpose(p_w[:, t, 128 * u:128 * u + 128],
                                      rows[:, u, 128 * t:128 * t + 128], W["ident"][:, :])
            mm.then_inc(turned, 1)

        @block.gpsimd
        def _(pool):
            pool.wait_ge(loaded, 16 * len(loads))
            pool.tensor_scalar(bn_t[:, :], bn[:, 3, :], 1e-5, None, ALU.add).then_inc(bn_eps, 1)
            pool.memset(W["minus_half"][:, :], -0.5).then_inc(bn_eps, 1)
            pool.memset(W["plus_half"][:, :], 0.5)
            pool.wait_ge(bn_eps, 2)
            pool.tensor_tensor(bn_std[:, :], bn_t[:, :], W["minus_half"][:, 0:KT], ALU.pow).then_inc(bn_rooted, 1)
            pool.wait_ge(index_ok, 1)
            for u in range(KT):
                at = bass.IndirectOffsetOnAxis(ap=index[:, u:u + 1], axis=0)
                pool.indirect_dma_start(rows[:, u, :], None, ins["weight"], at).then_inc(gathered, 16)
                pool.indirect_dma_start(W["b_sub"][:, u:u + 1], None, ins["bias"], at).then_inc(gathered, 16)
            pool.wait_ge(gathered, 64)


def layer_one_phase(nc, bass, mybir, ins, W, x2_out, fwd, back, chunks):
    from contextlib import ExitStack
    f32 = mybir.dt.float32
    ALU = mybir.AluOpType
    ACT = mybir.ActivationFunctionType
    AX = mybir.AxisListType
    ctx = ExitStack()
    with ctx:
        def sb(name, shape):
            return ctx.enter_context(nc.sbuf_tensor(name, shape, f32))

        def ps(name, shape):
            return ctx.enter_context(nc.psum_tensor(name, shape, f32))

        def sem(name):
            return ctx.enter_context(nc.semaphore(name))

        xa = sb("xa", [128, KT, COLS])
        xb = sb("xb", [128, KT, COLS])
        z = sb("z", [128, KT, COLS])
        sq = sb("sq", [128, KT, COLS])
        qkv = sb("qkv", [128, MT, COLS])
        qr = sb("qr", [128, 2, COLS])
        cx = sb("cx", [XC, 2, 8, YB])
        cy = sb("cy", [XC, 2, 8, YB])
        kT = sb("kT", [PR, 2, 2, 128])
        vT = sb("vT", [PR, 2, 2, 2, VO])
        vk = sb("vk", [128, 2, 2, 2, VO])
        rden = sb("rden", [128, 2, 8])
        den = sb("den", [128, 2, 8])
        oN = sb("oN", [128, 2, 2, 128])
        o = sb("o", [128, COLS])
        stat = sb("stat", [128, KT * NB])
        mean = sb("mean", [128, KT, NB])
        var = sb("var", [128, KT * NB])
        rstd = sb("rstd", [128, KT, NB])

        p_stream = [ps("p_s0", [128, 512]), ps("p_s1", [128, 512])]
        p_t = ps("p_t", [128, 2, 256])
        p_vk = ps("p_vk", [128, 2, 512])
        p_out = ps("p_out", [128, 2, 256])
        p_ot = ps("p_ot", [128, 2, 256])
        p_g = ps("p_g", [128, 512])

        x_in, xa_free = sem("x_in"), sem("xa_free")
        summed, g_mm, mean_ok, centred, squared = sem("summed"), sem("g_mm"), sem("mean_ok"), sem("centred"), sem("squared")
        var_ok, rstd_ok, z_ok = sem("var_ok"), sem("rstd_ok"), sem("z_ok")
        l0_mm, x1_ok = sem("l0_mm"), sem("x1_ok")
        qkv_mm, qkv_ev, conv_mm, conv_ev = sem("qkv_mm"), sem("qkv_ev"), sem("conv_mm"), sem("conv_ev")
        qr_ok = sem("qr_ok")
        xb_ok = sem("xb_ok")
        fwd_w = [sem("fwd_w0"), sem("fwd_w1")]
        cx_in = [sem("cx_in0"), sem("cx_in1")]
        back_w = [sem("back_w0"), sem("back_w1")]
        agg_in = [sem("agg_in0"), sem("agg_in1")]
        t_mm, k_ev, v_ev = sem("t_mm"), sem("k_ev"), sem("v_ev")
        vk_mm, vk_ev, out_mm, den_ok, rden_ok, on_ok = sem("vk_mm"), sem("vk_ev"), sem("out_mm"), sem("den_ok"), sem("rden_ok"), sem("on_ok")
        ot_mm, o_ev, proj_mm, proj_ev = sem("ot_mm"), sem("o_ev"), sem("proj_mm"), sem("proj_ev")
        stored, ones_ok = sem("stored"), sem("ones_ok")
        met_g, met_sp = sem("met_g"), sem("met_sp")

        def by_image(ap):
            return ap.rearrange("p t (s b) -> p t b s", b=NB)

        def by_position(ap):
            return ap.rearrange("p t (s b) -> p t s b", b=NB)

        def over_positions(ap):
            return ap.unsqueeze(2).to_broadcast([128, KT, S, NB])

        def wait(eng, s, count):
            if not isinstance(count, int) or count > 0:
                eng.wait_ge(s, count)

        UN = 4 * QP

        def conv_order():
            return range(MT)

        def pe_stat(pe, it, k):
            pe.wait_ge(summed, 4 * it + k + 1)
            wait_g(pe, it, k)
            pe.matmul(p_g[:, 0:KT * NB], W["mask8"][:, :], stat[:, :], start=True, stop=True).then_inc(g_mm, 1)

        def wait_g(pe, it, k):
            if k == 0:
                wait(pe, var_ok, 2 * it)
            elif k == 1:
                pe.wait_ge(mean_ok, 2 * it + 1)
            elif k == 2:
                pe.wait_ge(x1_ok, 4 * it + 4)
            else:
                pe.wait_ge(mean_ok, 2 * it + 2)

        def pe_layer0(pe, it):
            pe.wait_ge(z_ok, 2 * it + 1)
            for m in range(KT):
                for h in range(2):
                    n = 2 * m + h
                    if n == 0:
                        pe.wait_ge(var_ok, 2 * it + 1)
                    else:
                        pe.wait_ge(x1_ok, 4 * it + n)
                    for t in range(KT):
                        mm = pe.matmul(p_g[:, 0:HALF], W["w_sub"][:, t, 128 * m:128 * m + 128],
                                       z[:, t, HALF * h:HALF * h + HALF], start=(t == 0), stop=(t == KT - 1))
                    mm.then_inc(l0_mm, 1)

        def pe_qkv(pe, it):
            pe.wait_ge(z_ok, 2 * it + 2)
            for m in range(MT):
                for h in range(2):
                    n = 2 * m + h
                    if n >= 2:
                        pe.wait_ge(qkv_ev, 12 * it + n - 1)
                    else:
                        wait(pe, proj_ev, 16 * it - 1 + n)
                    for t in range(KT):
                        mm = pe.matmul(p_stream[h][:, 0:HALF], W["w_qkv"][:, t, 128 * m:128 * m + 128],
                                       z[:, t, HALF * h:HALF * h + HALF], start=(t == 0), stop=(t == KT - 1))
                    mm.then_inc(qkv_mm, 1)

        def pe_conv(pe, it, m):
            pe.wait_ge(cx_in[m % 2], 16 * HW * (3 * it + m // 2 + 1))
            for f in range(2):
                n = 2 * m + f
                if m % 3 == 0:
                    if m == 0:
                        pe.wait_ge(proj_ev, 16 * it + 3 + f)
                    else:
                        pe.wait_ge(proj_ev, 16 * it + 7 + f)
                else:
                    pe.wait_ge(conv_ev, 12 * it + n - 1)
                for j4 in range(4):
                    j = 4 * f + j4
                    for i, dy in enumerate((2, 1, 3, 0, 4)):
                        s = dy - 2
                        y0, y1 = max(0, -s), min(HW, HW - s)
                        g = 8 * m + j
                        mm = pe.matmul(p_stream[f][0:XC, YB * j4 + NB * y0:YB * j4 + NB * y1],
                                       W["conv"][:, g, XC * dy:XC * dy + XC],
                                       cx[:, m % 2, j, NB * (y0 + s):NB * (y1 + s)],
                                       start=(i == 0), stop=(i == TAPS - 1))
                mm.then_inc(conv_mm, 1)

        def pe_turn(pe, it, u):
            q, w = u // QP, u % QP
            if q < 2:
                pe.wait_ge(qkv_ev, 12 * it + 6 * q + 6)
            elif w == 0:
                pe.wait_ge(agg_in[q - 2], 16 * 8 * 3 * (it + 1))
            wait(pe, k_ev, UN * it + u)
            wait(pe, v_ev, 2 * (UN * it + u))
            kt, vt = 3 * (q % 2) + 1, 3 * (q % 2) + 2
            for pr in range(2):
                for i, tile in enumerate((kt, vt)):
                    rows = pair_of(qkv[:, tile, :], 2 * w + pr)
                    mm = pe.transpose(p_t[0:PR, pr, 128 * i:128 * i + 128], rows, W["ident"][:, :])
            mm.then_inc(t_mm, 1)

        def pe_vk(pe, it, u):
            pe.wait_ge(k_ev, UN * it + u + 1)
            pe.wait_ge(v_ev, 2 * (UN * it + u + 1))
            wait(pe, vk_ev, UN * it + u)
            for pr in range(2):
                mm = pe.matmul(p_vk[:, pr, 0:2 * VO], kT[:, u % 2, pr, :],
                               vT[:, u % 2, pr, :, :].rearrange("p i n -> p (i n)"), start=True, stop=True)
            mm.then_inc(vk_mm, 1)

        def pe_out(pe, it, u):
            q, w = u // QP, u % QP
            pe.wait_ge(vk_ev, UN * it + u + 1)
            if q < 2:
                pe.wait_ge(qr_ok, 2 * it + q + 1)
            wait(pe, on_ok, UN * it + u)
            src = qr[:, q, :] if q < 2 else qkv[:, 3 * (q - 2), :]
            for pr in range(2):
                for i in range(2):
                    lhs = src.rearrange("p (s b) -> p b s", b=NB)[:, 2 * w + pr + 8 * i, :]
                    mm = pe.matmul(p_out[64 * i:64 * i + S, pr, 0:VO], lhs, vk[:, u % 2, pr, i, :],
                                   start=True, stop=True)
            mm.then_inc(out_mm, 1)

        def pe_out_turn(pe, it, u):
            pe.wait_ge(on_ok, UN * it + u + 1)
            wait(pe, o_ev, UN * it + u)
            for pr in range(2):
                mm = pe.transpose(p_ot[:, pr, 0:128], oN[:, u % 2, pr, :], W["ident"][:, :])
            mm.then_inc(ot_mm, 1)

        def pe_proj(pe, it, q):
            pe.wait_ge(o_ev, UN * it + QP * (q + 1))
            for m in range(KT):
                for h in range(2):
                    n = 2 * m + h
                    if n >= 2:
                        pe.wait_ge(proj_ev, 16 * it + 4 * q + n - 1)
                    elif q == 0:
                        pe.wait_ge(qkv_ev, 12 * it + 11 + n)
                    elif q == 3:
                        pe.wait_ge(proj_ev, 16 * it + 4 * q + n - 1)
                    else:
                        pe.wait_ge(conv_ev, 12 * it + 6 * q - 1 + n)
                    mm = pe.matmul(p_stream[h][:, 0:HALF], W["w_proj"][:, q, 128 * m:128 * m + 128],
                                   o[:, HALF * h:HALF * h + HALF], start=True, stop=True)
                    mm.then_inc(proj_mm, 1)

        def pe_octet(pe, it, q, between=lambda w: None):
            for w in range(QP + 3):
                if w < QP:
                    pe_turn(pe, it, QP * q + w)
                if 1 <= w <= QP:
                    pe_vk(pe, it, QP * q + w - 1)
                if 2 <= w <= QP + 1:
                    pe_out(pe, it, QP * q + w - 2)
                if w >= 3:
                    pe_out_turn(pe, it, QP * q + w - 3)
                between(w)
            pe_proj(pe, it, q)

        def pe_ahead(pe, it, part):
            if part == 0:
                pe_stat(pe, it, 0)
            elif part == 1:
                pe_stat(pe, it, 1)
            elif part == 2:
                pe_layer0(pe, it)
            elif part == 3:
                pe_stat(pe, it, 2)
            else:
                pe_stat(pe, it, 3)

        def pe_chunk(pe, it, ahead):
            pe_qkv(pe, it)
            pe_octet(pe, it, 0)
            pe_conv(pe, it, 0)
            if ahead is not None:
                pe_ahead(pe, ahead, 0)
            pe_conv(pe, it, 1)
            if ahead is not None:
                pe_ahead(pe, ahead, 1)
            pe_conv(pe, it, 2)
            if ahead is not None:
                pe_ahead(pe, ahead, 2)
            pe_octet(pe, it, 1)
            pe_conv(pe, it, 3)
            if ahead is not None:
                pe_ahead(pe, ahead, 3)
            pe_conv(pe, it, 4)
            if ahead is not None:
                pe_ahead(pe, ahead, 4)
            pe_conv(pe, it, 5)
            pe_octet(pe, it, 2)
            pe_octet(pe, it, 3)

        def v_norm(v, it, k, src, sub):
            n = 2 * it + k
            if sub == 0:
                if k == 0:
                    v.wait_ge(x_in, 16 * (it + 1))
                    wait(v, g_mm, 4 * it)
                else:
                    v.wait_ge(x1_ok, 4 * it + 4)
                    v.wait_ge(g_mm, 4 * it + 2)
                v.tensor_reduce(stat[:, :], by_image(src[:, :, :]), AX.X, ALU.add).then_inc(summed, 1)
            elif sub == 1:
                v.wait_ge(g_mm, 2 * n + 1)
                v.tensor_scalar(mean[:, :, :].rearrange("p t b -> p (t b)"), p_g[:, 0:KT * NB],
                                1.0 / (GS * S), None, ALU.mult).then_inc(mean_ok, 1)
                v.wait_ge(mean_ok, n + 1)
                if k == 0:
                    wait(v, qkv_mm, 12 * it)
                else:
                    v.wait_ge(l0_mm, 4 * it + 4)
                v.tensor_tensor(by_position(z[:, :, :]), by_position(src[:, :, :]),
                                over_positions(mean[:, :, :]), ALU.subtract).then_inc(centred, 1)
            elif sub == 2:
                v.wait_ge(squared, n + 1)
                v.tensor_reduce(stat[:, :], by_image(sq[:, :, :]), AX.X, ALU.add).then_inc(summed, 1)
            else:
                v.wait_ge(g_mm, 2 * n + 2)
                v.tensor_scalar(var[:, :], p_g[:, 0:KT * NB], 1.0 / (GS * S), 1e-5,
                                ALU.mult, ALU.add).then_inc(var_ok, 1)
                v.wait_ge(rstd_ok, n + 1)
                v.tensor_tensor(by_position(z[:, :, :]), by_position(z[:, :, :]),
                                over_positions(rstd[:, :, :]), ALU.mult).then_inc(z_ok, 1)

        def v_layer0(v, it):
            for m in range(KT):
                for h in range(2):
                    n = 2 * m + h
                    v.wait_ge(l0_mm, 4 * it + n + 1)
                    cols = xa[:, m, HALF * h:HALF * h + HALF]
                    v.scalar_tensor_tensor(cols, p_g[:, 0:HALF], W["b_sub"][:, m:m + 1], cols,
                                           ALU.add, ALU.add).then_inc(x1_ok, 1)

        def v_qkv(v, it):
            for m in range(MT):
                for h in range(2):
                    n = 2 * m + h
                    v.wait_ge(qkv_mm, 12 * it + n + 1)
                    if n == 0:
                        wait(v, out_mm, UN * it)
                    v.tensor_copy(qkv[:, m, HALF * h:HALF * h + HALF], p_stream[h][:, 0:HALF]).then_inc(qkv_ev, 1)

        def v_vk(v, it, u):
            v.wait_ge(vk_mm, UN * it + u + 1)
            wait(v, out_mm, UN * it + u - 1)
            v.tensor_tensor(vk[:, u % 2, :, :, :], p_vk[:, :, 0:2 * VO].rearrange("p r (i n) -> p r i n", i=2),
                            W["mask_vo"][:, :].unsqueeze(1).unsqueeze(1).to_broadcast([128, 2, 2, VO]),
                            ALU.mult).then_inc(vk_ev, 1)

        def v_norm_out(v, it, u):
            v.wait_ge(out_mm, UN * it + u + 1)
            v.tensor_scalar(den[:, :, :], p_out[:, :, 128:VO], 1e-15, None, ALU.add).then_inc(den_ok, 1)
            v.wait_ge(den_ok, UN * it + u + 1)
            v.reciprocal(rden[:, :, :], den[:, :, :]).then_inc(rden_ok, 1)
            v.wait_ge(rden_ok, UN * it + u + 1)
            wait(v, ot_mm, UN * it + u - 1)
            v.tensor_tensor(oN[:, u % 2, :, :].rearrange("p r (h d) -> p r h d", h=8),
                            p_out[:, :, 0:128].rearrange("p r (h d) -> p r h d", h=8),
                            rden[:, :, :].unsqueeze(3).to_broadcast([128, 2, 8, D]), ALU.mult).then_inc(on_ok, 1)

        def v_proj(v, it, q):
            for m in range(KT):
                for h in range(2):
                    n = 2 * m + h
                    v.wait_ge(proj_mm, 16 * it + 4 * q + n + 1)
                    if q == 0:
                        v.wait_ge(xb_ok, KT * it + m + 1)
                    else:
                        v.wait_ge(proj_ev, 16 * it + 4 * (q - 1) + n + 1)
                    cols = xb[:, m, HALF * h:HALF * h + HALF]
                    v.scalar_tensor_tensor(cols, p_stream[h][:, 0:HALF], W["bn_scale"][:, m:m + 1], cols,
                                           ALU.mult, ALU.add).then_inc(proj_ev, 1)

        def v_octet(v, it, q):
            for w in range(1, QP + 3):
                if w <= QP:
                    v_vk(v, it, QP * q + w - 1)
                if 2 <= w <= QP + 1:
                    v_norm_out(v, it, QP * q + w - 2)
            v_proj(v, it, q)

        def v_chunk(v, it, ahead):
            v_qkv(v, it)
            v_octet(v, it, 0)
            if ahead is not None:
                v_norm(v, ahead, 0, xa, 0)
                v_norm(v, ahead, 0, xa, 1)
                v_norm(v, ahead, 0, xa, 2)
                v_norm(v, ahead, 0, xa, 3)
                v_layer0(v, ahead)
            v_octet(v, it, 1)
            if ahead is not None:
                for sub in range(4):
                    v_norm(v, ahead, 1, xa, sub)
            v_octet(v, it, 2)
            v_octet(v, it, 3)

        def a_square(a, it, k):
            a.wait_ge(centred, 2 * it + k + 1)
            wait(a, summed, 4 * it + 2 * k)
            a.activation(sq[:, :, :], z[:, :, :], ACT.Square).then_inc(squared, 1)

        def a_turn(a, it, u):
            a.wait_ge(t_mm, UN * it + u + 1)
            wait(a, vk_mm, UN * it + u - 1)
            a.activation(kT[:, u % 2, :, :], p_t[0:PR, :, 0:128], ACT.Relu).then_inc(k_ev, 1)
            for i in range(2):
                a.activation(vT[:, u % 2, :, i, 0:128], p_t[0:PR, :, 128:256], ACT.Copy,
                             scale=W["image_of"][:, i:i + 1]).then_inc(v_ev, 1)

        def a_out(a, it, u):
            q, w = u // QP, u % QP
            a.wait_ge(ot_mm, UN * it + u + 1)
            if w == 0:
                wait(a, proj_mm, 16 * it + 4 * q)
            a.activation(o[:, :].rearrange("p (s i b) -> p b i s", i=2, b=8)[:, 2 * w:2 * w + 2, :, :],
                         p_ot[:, :, 0:128].rearrange("p r (i s) -> p r i s", i=2)[:, :, :, 0:S],
                         ACT.Copy).then_inc(o_ev, 1)

        def a_octet(a, it, q):
            for w in range(QP + 3):
                if w < QP:
                    a_turn(a, it, QP * q + w)
                if w >= 3:
                    a_out(a, it, QP * q + w - 3)

        def a_conv(a, it, m):
            for f in range(2):
                n = 2 * m + f
                a.wait_ge(conv_mm, 12 * it + n + 1)
                if f == 0:
                    wait(a, back_w[m % 2], 16 * (3 * it + m // 2))
                a.activation(cy[:, m % 2, 4 * f:4 * f + 4, :].rearrange("p j n -> p (j n)"),
                             p_stream[f][0:XC, 0:4 * YB],
                             ACT.Relu if m % 3 < 2 else ACT.Copy).then_inc(conv_ev, 1)

        def a_chunk(a, it, ahead):
            a_octet(a, it, 0)
            a_conv(a, it, 0)
            a_conv(a, it, 1)
            if ahead is not None:
                a_square(a, ahead, 0)
            a_conv(a, it, 2)
            a_octet(a, it, 1)
            a_conv(a, it, 3)
            a_conv(a, it, 4)
            if ahead is not None:
                a_square(a, ahead, 1)
            a_conv(a, it, 5)
            a_octet(a, it, 2)
            a_octet(a, it, 3)

        def sp_write(sp, it, m):
            sp.wait_ge(qkv_ev, 12 * it + 2 * m + 2)
            settle(sp, met_sp)
            sp.dma_start(fwd[m], qkv[:, m, :]).then_inc(fwd_w[m % 2], 16)

        def sp_read(sp, it, m):
            sp.wait_ge(fwd_w[m % 2], 16 * (3 * it + m // 2 + 1))
            settle(sp, met_sp)
            wait(sp, conv_mm, 12 * it + 2 * m - 2)
            for x in range(HW):
                sp.dma_start(cx[D * x:D * x + D, m % 2, :, :],
                             fwd[m].rearrange("(j c) (x n) -> x c j n", c=D, x=HW)[x]).then_inc(cx_in[m % 2], 16)

        def sp_chunk(sp, it, ahead):
            if ahead is not None:
                sp.wait_ge(xb_ok, KT * it + KT)
                settle(sp, met_sp)
                sp.dma_start(xa[:, :, :], ins["x"][ahead]).then_inc(x_in, 16)
            sp_write(sp, it, 0)
            for m in range(MT):
                if m + 1 < MT:
                    sp_write(sp, it, m + 1)
                sp_read(sp, it, m)

        def g_start(g, it):
            g.wait_ge(x1_ok, 4 * it + 4)
            wait(g, stored, 16 * it)
            g.wait_ge(centred, 2 * it + 2)
            settle(g, met_g)
            for m in range(KT):
                g.tensor_scalar(xb[:, m, :], xa[:, m, :], W["bn_shift"][:, m:m + 1], None, ALU.add).then_inc(xb_ok, 1)
            wait(g, out_mm, UN * it - 2 * QP)
            for h in range(2):
                g.wait_ge(qkv_ev, 12 * it + 6 * h + 2)
                settle(g, met_g)
                g.tensor_scalar(qr[:, h, :], qkv[:, 3 * h, :], 0.0, None, ALU.max).then_inc(qr_ok, 1)

        def g_root(g, it, k):
            g.wait_ge(var_ok, 2 * it + k + 1)
            settle(g, met_g)
            g.tensor_tensor(rstd[:, :, :].rearrange("p t b -> p (t b)"), var[:, :], W["minus_half"][:, :],
                            ALU.pow).then_inc(rstd_ok, 1)

        def g_write(g, it, m):
            g.wait_ge(conv_ev, 12 * it + 2 * m + 2)
            settle(g, met_g)
            g.dma_start(back[m], cy[:, m % 2, :, :]).then_inc(back_w[m % 2], 16)

        def g_read(g, it, m):
            g.wait_ge(back_w[m % 2], 16 * (3 * it + m // 2 + 1))
            if m % 3 == 0:
                g.wait_ge(t_mm, UN * it + QP * (m // 3 + 1))
                for n in (m + 1, m + 2):
                    g.wait_ge(fwd_w[n % 2], 16 * (3 * it + n // 2 + 1))
                g.wait_ge(qr_ok, 2 * it + m // 3 + 1)
            settle(g, met_g)
            for j in range(8):
                g.dma_start(qkv[D * j:D * j + D, m, :].rearrange("o (x n) -> o x n", x=HW),
                            back[m].rearrange("(x o) j n -> j o x n", o=D)[j]).then_inc(agg_in[m // 3], 16)

        def g_chunk(g, it, ahead):
            g_start(g, it)
            for m in range(MT):
                g_write(g, it, m)
                if ahead is not None and m in (2, 5):
                    g_root(g, ahead, m // 3)
                if m >= 1:
                    g_read(g, it, m - 1)
            g_read(g, it, MT - 1)
            g.wait_ge(proj_ev, 16 * it + 16)
            settle(g, met_g)
            g.dma_start(x2_out[it], xb[:, :, :]).then_inc(stored, 16)

        block = ctx.enter_context(nc.Block())

        @block.sync
        def _(sp):
            sp.dma_start(xa[:, :, :], ins["x"][0]).then_inc(x_in, 16)
            sp_chunk(sp, 0, 1)
            with sp.Fori(1, chunks - 1) as it:
                sp_chunk(sp, it, it + 1)
            sp_chunk(sp, chunks - 1, None)

        @block.tensor
        def _(pe):
            pe.wait_ge(ones_ok, 4)
            for part in range(5):
                pe_ahead(pe, 0, part)
            pe_chunk(pe, 0, 1)
            with pe.Fori(1, chunks - 1) as it:
                pe_chunk(pe, it, it + 1)
            pe_chunk(pe, chunks - 1, None)

        @block.vector
        def _(v):
            for n in range(2):
                v.tensor_copy(vT[:, n, :, :, 128:VO].rearrange("p r i h -> p r i h"),
                              W["image_of"][:, :].unsqueeze(1).unsqueeze(3).to_broadcast([PR, 2, 2, 8])).then_inc(ones_ok, 1)
            v.memset(p_out[:, :, :], 1.0).then_inc(ones_ok, 1)
            v.memset(p_ot[:, :, :], 0.0).then_inc(ones_ok, 1)
            v.wait_ge(ones_ok, 4)
            for sub in range(4):
                v_norm(v, 0, 0, xa, sub)
            v_layer0(v, 0)
            for sub in range(4):
                v_norm(v, 0, 1, xa, sub)
            v_chunk(v, 0, 1)
            with v.Fori(1, chunks - 1) as it:
                v_chunk(v, it, it + 1)
            v_chunk(v, chunks - 1, None)

        @block.scalar
        def _(a):
            for k in range(2):
                a_square(a, 0, k)
            a_chunk(a, 0, 1)
            with a.Fori(1, chunks - 1) as it:
                a_chunk(a, it, it + 1)
            a_chunk(a, chunks - 1, None)

        @block.gpsimd
        def _(g):
            for k in range(2):
                g_root(g, 0, k)
            g_chunk(g, 0, 1)
            with g.Fori(1, chunks - 1) as it:
                g_chunk(g, it, it + 1)
            g_chunk(g, chunks - 1, None)
            g.wait_ge(stored, 16 * chunks)


def gate_and_attention_phase(nc, bass, mybir, W, x2, out, ins, chunks):
    from contextlib import ExitStack
    f32 = mybir.dt.float32
    ALU = mybir.AluOpType
    ACT = mybir.ActivationFunctionType
    AX = mybir.AxisListType
    ctx = ExitStack()
    G = 32
    with ctx:
        def sb(name, shape):
            return ctx.enter_context(nc.sbuf_tensor(name, shape, f32))

        def ps(name, shape):
            return ctx.enter_context(nc.psum_tensor(name, shape, f32))

        def sem(name):
            return ctx.enter_context(nc.semaphore(name))

        x = sb("x2_x", [128, 2, KT, COLS])
        z = sb("x2_z", [128, KT, COLS])
        sq = sb("x2_sq", [128, KT, COLS])
        prod = sb("prod", [128, KT, COLS])
        gapped = sb("gapped", [128, KT, COLS])
        stat = sb("stat2", [128, KT * NB])
        mean = sb("mean2", [128, KT, NB])
        var = sb("var2", [128, KT * NB])
        rstd = sb("rstd2", [128, KT, NB])
        sel = sb("sel", [128, KT, G])
        spread = sb("spread", [G, KT, 128])
        countdown = sb("countdown", [G, COLS])
        ruler = sb("ruler", [G, YB])
        pair_a = sb("pair_a", [2, PR])
        pair_b = sb("pair_b", [2, PR])
        s_sb = sb("s_sb", [G, COLS])
        hot = sb("hot", [G, COLS])
        best = sb("best", [G, NB])
        last = sb("last", [G, NB])
        idx = sb("idx", [G, NB])
        row = sb("row", [G, NB])
        col = sb("col", [G, NB])
        dist = sb("dist", [G, 2, YB])
        dist2 = sb("dist2", [G, 2, YB])
        gauss = sb("gauss", [G, 2, YB])
        dsum = sb("dsum", [G, COLS])
        sim = sb("sim", [G, COLS])
        simsq = sb("simsq", [G, COLS])
        gate = sb("gate", [G, COLS])
        ssum = sb("ssum", [G, NB])
        smean = sb("smean", [G, NB])
        svar = sb("svar", [G, NB])
        ssq = sb("ssq", [G, NB])
        sstd = sb("sstd", [G, NB])
        sinv = sb("sinv", [G, NB])
        qv = sb("qv", [128, KT, NB])
        gap = sb("gap", [128, KT, NB])
        gapm = sb("gapm", [128, KT, NB])
        neg = sb("neg", [G, 2])
        half_zero = sb("half_zero", [G, 1])
        inv_scale = sb("inv_scale", [G, 1])
        log_norm = sb("log_norm", [G, 1])
        f_sb = sb("f_sb", [G, COLS])
        g_sb = sb("g_sb", [G, COLS])
        hh = sb("hh", [PR, 8, C])
        sc = sb("sc", [PR, 2, 4, PR])
        smx = sb("smx", [PR, 2, 4])
        ssm = sb("ssm", [PR, 2, 4])
        srec = sb("srec", [PR, 2, 4])
        beta = sb("beta", [PR, 2, 4, PR])
        pa = ps("pa", [128, 2, 512])
        pb = ps("pb", [128, 4, 512])
        pc = ps("pc", [128, 2, 512])

        sems = {}

        def S(name):
            if name not in sems:
                sems[name] = sem("p2_" + name)
            return sems[name]

        def wait(eng, name, count):
            if not isinstance(count, int) or count > 0:
                eng.wait_ge(S(name), count)

        def by_image(ap):
            return ap.rearrange("p t (s b) -> p t b s", b=NB)

        def by_position(ap):
            return ap.rearrange("p t (s b) -> p t s b", b=NB)

        def over_positions(ap):
            return ap.unsqueeze(2).to_broadcast([128, KT, S_, NB])

        S_ = HW * HW

        def g_image(ap):
            return ap.rearrange("g (s b) -> g b s", b=NB)

        def g_position(ap):
            return ap.rearrange("g (s b) -> g s b", b=NB)

        def g_over(ap):
            return ap.unsqueeze(1).to_broadcast([G, S_, NB])

        def halves(ap):
            return ap.rearrange("p (h n) -> p h n", h=2)

        for name in ("consts", "x_in", "stored"):
            S(name)
        x_in = [sem("p2_x_in0"), sem("p2_x_in1")]
        stored = [sem("p2_stored0"), sem("p2_stored1")]
        loads = [(sel[:, :, :], ins["c_sel"]), (spread[:, :, :], ins["c_spread"]),
                 (countdown[:, :], ins["c_countdown"]), (ruler[:, :], ins["c_ruler"]),
                 (pair_a[:, :], ins["c_pair_a"]), (pair_b[:, :], ins["c_pair_b"])]


        def v_norm(v, it, p, k):
            n = 2 * it + k
            src = x[:, p, :, :]
            if k == 0:
                v.wait_ge(x_in[p], it_load(it, p))
                wait(v, "g_mm", 4 * it)
            else:
                v.wait_ge(S("x3"), it + 1)
                v.wait_ge(S("g_mm"), 4 * it + 2)
            v.tensor_reduce(stat[:, :], by_image(src), AX.X, ALU.add).then_inc(S("summed"), 1)
            v.wait_ge(S("g_mm"), 2 * n + 1)
            v.tensor_scalar(mean[:, :, :].rearrange("p t b -> p (t b)"), pc[:, 0, 0:KT * NB],
                            1.0 / (GS * S_), None, ALU.mult).then_inc(S("mean"), 1)
            v.wait_ge(S("mean"), n + 1)
            if k == 0:
                wait(v, "hh_mm", 8 * it)
                wait(v, "fg_mm", it)
                wait(v, "x3z", it)
            else:
                v.wait_ge(S("s_mm"), it + 1)
                v.wait_ge(S("gapped"), it + 1)
            v.tensor_tensor(by_position(z[:, :, :]), by_position(src), over_positions(mean[:, :, :]),
                            ALU.subtract).then_inc(S("centred"), 1)
            v.wait_ge(S("squared"), n + 1)
            v.tensor_reduce(stat[:, :], by_image(sq[:, :, :]), AX.X, ALU.add).then_inc(S("summed"), 1)
            v.wait_ge(S("g_mm"), 2 * n + 2)
            v.tensor_scalar(var[:, :], pc[:, 0, 0:KT * NB], 1.0 / (GS * S_), 1e-5,
                            ALU.mult, ALU.add).then_inc(S("var"), 1)
            v.wait_ge(S("rstd"), n + 1)
            v.tensor_tensor(by_position(z[:, :, :]), by_position(z[:, :, :]),
                            over_positions(rstd[:, :, :]), ALU.mult).then_inc(S("z"), 1)

        def it_load(it, p):
            return 16 * (it // 2 + 1) if isinstance(it, int) else 8 * (it - p) + 16

        def v_gate(v, it, p):
            def link(ins_, name):
                ins_.then_inc(S(name), 1)
                v.wait_ge(S(name), it + 1)

            v.wait_ge(S("s_ev"), 2 * it + 2)
            link(v.tensor_reduce(best[:, :], g_image(s_sb[:, :]), AX.X, ALU.max), "best")
            link(v.tensor_tensor(g_position(hot[:, :]), g_position(s_sb[:, :]), g_over(best[:, :]),
                                 ALU.is_equal), "at_best")
            link(v.tensor_tensor(hot[:, :], hot[:, :], countdown[:, :], ALU.mult), "counted")
            link(v.tensor_reduce(last[:, :], g_image(hot[:, :]), AX.X, ALU.max), "last")
            link(v.tensor_tensor(g_position(hot[:, :]), g_position(hot[:, :]), g_over(last[:, :]),
                                 ALU.is_equal), "hot")
            link(v.tensor_reduce(gap[:, :, :], by_image(z[:, :, :]), AX.X, ALU.add), "gap")
            v.tensor_scalar(gapm[:, :, :], gap[:, :, :], 1.0 / S_, None, ALU.mult).then_inc(S("gapm"), 1)
            link(v.tensor_scalar(idx[:, :], last[:, :], -1.0, float(S_), ALU.mult, ALU.add), "idx")
            for r in range(1, HW):
                if r == 1:
                    i = v.tensor_scalar(row[:, :], idx[:, :], float(HW * r), None, ALU.is_ge)
                else:
                    i = v.scalar_tensor_tensor(row[:, :], idx[:, :], float(HW * r), row[:, :], ALU.is_ge, ALU.add)
                i.then_inc(S("row"), 1)
                v.wait_ge(S("row"), (HW - 1) * it + r)
            link(v.scalar_tensor_tensor(col[:, :], row[:, :], -float(HW), idx[:, :], ALU.mult, ALU.add), "col")
            for k, at in enumerate((row, col)):
                i = v.tensor_tensor(dist[:, k, :].rearrange("g (y b) -> g y b", b=NB),
                                    ruler[:, :].rearrange("g (y b) -> g y b", b=NB),
                                    at[:, :].unsqueeze(1).to_broadcast([G, HW, NB]), ALU.subtract)
                i.then_inc(S("apart"), 1)
            v.wait_ge(S("apart"), 2 * it + 2)
            for k in range(2):
                v.tensor_scalar(dist[:, k, :], dist[:, k, :], W["theta"][:, k:k + 1], None,
                                ALU.mult).then_inc(S("dist"), 1)
            v.wait_ge(S("hot_mm"), it + 1)
            for t in range(KT):
                v.tensor_tensor(halves(prod[:, t, :]), halves(z[:, t, :]),
                                pb[:, 2 * t:2 * t + 2, 0:HALF], ALU.mult).then_inc(S("picked"), 1)
            v.wait_ge(S("picked"), 2 * it + 2)
            link(v.tensor_reduce(qv[:, :, :], by_image(prod[:, :, :]), AX.X, ALU.add), "qv")
            v.tensor_tensor(by_position(prod[:, :, :]), by_position(z[:, :, :]), over_positions(qv[:, :, :]),
                            ALU.mult).then_inc(S("prod"), 1)
            v.wait_ge(S("gauss"), it + 1)
            link(v.tensor_tensor(
                dsum[:, :].rearrange("g (x y b) -> g x y b", x=HW, y=HW),
                gauss[:, 0, :].rearrange("g (y b) -> g y b", b=NB).unsqueeze(1).to_broadcast([G, HW, HW, NB]),
                gauss[:, 1, :].rearrange("g (x b) -> g x b", b=NB).unsqueeze(2).to_broadcast([G, HW, HW, NB]),
                ALU.add), "dsum")
            v.wait_ge(S("sim_mm"), it + 1)
            link(v.scalar_tensor_tensor(halves(sim[:, :]), pa[0:G, :, 0:HALF], half_zero[:, 0:1], halves(dsum[:, :]),
                                        ALU.mult, ALU.mult), "sim_max")
            v.wait_ge(S("gap_mm"), it + 1)
            link(v.scalar_tensor_tensor(halves(sim[:, :]), pc[0:G, :, 0:HALF], W["g_par"][:, 2:3], halves(sim[:, :]),
                                        ALU.mult, ALU.add), "sim")
            link(v.tensor_reduce(ssum[:, :], g_image(sim[:, :]), AX.X, ALU.add), "ssum")
            link(v.tensor_scalar(smean[:, :], ssum[:, :], 1.0 / S_, None, ALU.mult), "smean")
            v.tensor_tensor(g_position(sim[:, :]), g_position(sim[:, :]), g_over(smean[:, :]),
                            ALU.subtract).then_inc(S("sim_centred"), 1)
            v.wait_ge(S("sim_squared"), it + 1)
            link(v.tensor_reduce(ssq[:, :], g_image(simsq[:, :]), AX.X, ALU.add), "ssq")
            v.tensor_scalar(svar[:, :], ssq[:, :], 1.0 / (S_ - 1), None, ALU.mult).then_inc(S("svar"), 1)
            v.wait_ge(S("sstd"), it + 1)
            link(v.tensor_scalar(sstd[:, :], sstd[:, :], 1e-5, None, ALU.add), "sstd_eps")
            link(v.reciprocal(sinv[:, :], sstd[:, :]), "sinv")
            v.tensor_tensor(g_position(sim[:, :]), g_position(sim[:, :]), g_over(sinv[:, :]),
                            ALU.mult).then_inc(S("context"), 1)
            v.wait_ge(S("gate_exp"), it + 1)
            link(v.tensor_scalar(gate[:, :], gate[:, :], 1.0, None, ALU.add), "gate_sum")
            v.reciprocal(gate[:, :], gate[:, :]).then_inc(S("gate"), 1)
            v.wait_ge(S("gate_mm"), it + 1)
            for t in range(KT):
                v.tensor_tensor(halves(prod[:, t, :]), halves(z[:, t, :]),
                                pb[:, 2 * t:2 * t + 2, 0:HALF], ALU.mult).then_inc(S("gated"), 1)
            v.wait_ge(S("gated"), 2 * it + 2)
            v.tensor_tensor(x[:, p, :, :], x[:, p, :, :], prod[:, :, :], ALU.add).then_inc(S("x3"), 1)

        def v_attend(v, it, p):
            v.wait_ge(S("score_mm"), 2 * it + 2)
            scores = pa[0:PR, :, 0:4 * PR].rearrange("r h (q n) -> r h q n", q=4)

            def over(ap):
                return ap.unsqueeze(3).to_broadcast([PR, 2, 4, PR])
            v.tensor_reduce(smx[:, :, :], scores, AX.X, ALU.max).then_inc(S("smx"), 1)
            v.wait_ge(S("smx"), it + 1)
            v.tensor_tensor(sc[:, :, :, :], scores, over(smx[:, :, :]), ALU.subtract).then_inc(S("shifted"), 1)
            v.wait_ge(S("exp"), it + 1)
            v.tensor_reduce(ssm[:, :, :], sc[:, :, :, :], AX.X, ALU.add).then_inc(S("ssm"), 1)
            v.wait_ge(S("ssm"), it + 1)
            v.reciprocal(srec[:, :, :], ssm[:, :, :]).then_inc(S("srec"), 1)
            v.wait_ge(S("srec"), it + 1)
            v.tensor_tensor(sc[:, :, :, :], sc[:, :, :, :], over(srec[:, :, :]), ALU.mult).then_inc(S("probs"), 1)
            v.wait_ge(S("x3z"), it + 1)
            for m in range(KT):
                for h in range(2):
                    n = 2 * m + h
                    v.wait_ge(S("o_mm"), 4 * it + n + 1)
                    dst = x[:, p, m, :].rearrange("p (r b) -> p b r", b=8)[:, 4 * h:4 * h + 4, :]
                    v.scalar_tensor_tensor(dst, pb[:, n, 0:4 * PR].rearrange("p (b r) -> p b r", b=4),
                                           W["gamma"][:, 0:1], dst, ALU.mult, ALU.add).then_inc(S("x4"), 1)

        def v_chunk(v, it, p):
            v_norm(v, it, p, 0)
            v_gate(v, it, p)
            v_norm(v, it, p, 1)
            v_attend(v, it, p)

        def pe_stat(pe, it, k):
            pe.wait_ge(S("summed"), 4 * it + k + 1)
            if k == 0:
                wait(pe, "bt_ev", 2 * it)
            elif k in (1, 3):
                pe.wait_ge(S("mean"), 2 * it + k // 2 + 1)
            else:
                pe.wait_ge(S("sim"), it + 1)
            pe.matmul(pc[:, 0, 0:KT * NB], W["mask8"][:, :], stat[:, :], start=True, stop=True).then_inc(S("g_mm"), 1)

        def pe_group_sum(pe, dst, src, s, it):
            for h in range(2):
                for t in range(KT):
                    mm = pe.matmul(dst[0:G, h, 0:HALF], sel[:, t, :], src[:, t, HALF * h:HALF * h + HALF],
                                   start=(t == 0), stop=(t == KT - 1))
            mm.then_inc(S(s), 1)

        def pe_spread(pe, src, s):
            for t in range(KT):
                for h in range(2):
                    mm = pe.matmul(pb[:, 2 * t + h, 0:HALF], spread[:, t, :], src[:, HALF * h:HALF * h + HALF],
                                   start=True, stop=True)
            mm.then_inc(S(s), 1)

        def pe_chunk(pe, it, p):
            pe_stat(pe, it, 0)
            pe_stat(pe, it, 1)
            pe.wait_ge(S("z"), 2 * it + 1)
            wait(pe, "shifted", it)
            pe_group_sum(pe, pa, z, "s_mm", it)
            pe.wait_ge(S("hot"), it + 1)
            wait(pe, "x4", 4 * it)
            pe_spread(pe, hot, "hot_mm")
            pe.wait_ge(S("gapped"), it + 1)
            pe.wait_ge(S("var"), 2 * it + 1)
            pe_group_sum(pe, pc, gapped, "gap_mm", it)
            pe.wait_ge(S("prod"), it + 1)
            pe.wait_ge(S("s_ev"), 2 * it + 2)
            pe_group_sum(pe, pa, prod, "sim_mm", it)
            pe.wait_ge(S("gate"), it + 1)
            pe.wait_ge(S("picked"), 2 * it + 2)
            pe_spread(pe, gate, "gate_mm")
            pe_stat(pe, it, 2)
            pe_stat(pe, it, 3)
            pe.wait_ge(S("z"), 2 * it + 2)
            pe.wait_ge(S("gated"), 2 * it + 2)
            for k in range(2):
                for h in range(2):
                    for t in range(KT):
                        mm = pe.matmul(pb[0:G, 2 * k + h, 0:HALF], W["wqk"][:, t, G * k:G * k + G],
                                       z[:, t, HALF * h:HALF * h + HALF], start=(t == 0), stop=(t == KT - 1))
            mm.then_inc(S("fg_mm"), 1)
            pe.wait_ge(S("fg_ev"), 4 * it + 4)
            pe.wait_ge(S("sim_max"), it + 1)
            for h in range(2):
                for q in range(4):
                    pair = [pair_of(t[:, :], 4 * h + q) for t in (f_sb, g_sb)]
                    pe.matmul(pa[0:PR, h, PR * q:PR * q + PR], pair[1], pair[0], start=True, stop=False)
                    mm = pe.matmul(pa[0:PR, h, PR * q:PR * q + PR], pair_a[:, :], pair_b[:, :],
                                   start=False, stop=True)
                mm.then_inc(S("score_mm"), 1)
            for n in range(4):
                if n == 0:
                    pe.wait_ge(S("var"), 2 * it + 2)
                if n >= 2:
                    pe.wait_ge(S("hh_ev"), 4 * it + n - 1)
                for q in range(2):
                    for t in range(KT):
                        mm = pe.matmul(pc[0:PR, n % 2, C * q:C * q + C], pair_of(z[:, t, :], 2 * n + q),
                                       W["wv"][:, t, :],
                                       start=(t == 0), stop=(t == KT - 1))
                    mm.then_inc(S("hh_mm"), 1)
            pe.wait_ge(S("probs"), it + 1)
            for h in range(2):
                pe.wait_ge(S("hh_ev"), 4 * it + 3 + h)
                for q in range(4):
                    mm = pe.transpose(pc[0:PR, h, PR * q:PR * q + PR], sc[:, h, q, :], W["ident"][0:PR, 0:PR])
                mm.then_inc(S("bt_mm"), 1)
            for m in range(KT):
                for h in range(2):
                    if m == 0:
                        pe.wait_ge(S("bt_ev"), 2 * it + h + 1)
                    for q in range(4):
                        mm = pe.matmul(pb[:, 2 * m + h, PR * q:PR * q + PR], hh[:, 4 * h + q, 128 * m:128 * m + 128],
                                       beta[:, h, q, :], start=True, stop=True)
                    mm.then_inc(S("o_mm"), 1)

        def a_square(a, it, k):
            a.wait_ge(S("centred"), 2 * it + k + 1)
            wait(a, "summed", 4 * it + 2 * k)
            a.activation(sq[:, :, :], z[:, :, :], ACT.Square).then_inc(S("squared"), 1)

        def a_chunk(a, it, p):
            a_square(a, it, 0)
            a.wait_ge(S("s_mm"), it + 1)
            wait(a, "at_best", it)
            for h in range(2):
                a.activation(s_sb[:, HALF * h:HALF * h + HALF], pa[0:G, h, 0:HALF], ACT.Copy).then_inc(S("s_ev"), 1)
            a.wait_ge(S("dist"), 2 * it + 2)
            a.activation(dist2[:, :, :], dist[:, :, :], ACT.Square, scale=inv_scale[:, 0:1]).then_inc(S("dist2"), 1)
            a.wait_ge(S("dist2"), it + 1)
            wait(a, "dsum", it)
            a.activation(gauss[:, :, :], dist2[:, :, :], ACT.Exp, scale=-0.5, bias=log_norm[:, 0:1]).then_inc(S("gauss"), 1)
            a.wait_ge(S("sim_centred"), it + 1)
            a.activation(simsq[:, :], sim[:, :], ACT.Square).then_inc(S("sim_squared"), 1)
            a.wait_ge(S("context"), it + 1)
            wait(a, "gate_mm", it)
            a.activation(gate[:, :], sim[:, :], ACT.Exp, scale=neg[:, 0:1], bias=neg[:, 1:2]).then_inc(S("gate_exp"), 1)
            a_square(a, it, 1)
            a.wait_ge(S("fg_mm"), it + 1)
            for k, dst in enumerate((f_sb, g_sb)):
                for h in range(2):
                    a.activation(dst[:, HALF * h:HALF * h + HALF], pb[0:G, 2 * k + h, 0:HALF], ACT.Copy).then_inc(S("fg_ev"), 1)
            a.wait_ge(S("shifted"), it + 1)
            a.activation(sc[:, :, :, :], sc[:, :, :, :], ACT.Exp).then_inc(S("exp"), 1)
            for n in range(4):
                a.wait_ge(S("hh_mm"), 8 * it + 2 * n + 2)
                if n == 0:
                    wait(a, "o_mm", 4 * it)
                a.activation(hh[:, 2 * n:2 * n + 2, :], pc[0:PR, n % 2, :].rearrange("r (q c) -> r q c", q=2),
                             ACT.Copy).then_inc(S("hh_ev"), 1)
            for h in range(2):
                a.wait_ge(S("bt_mm"), 2 * it + h + 1)
                a.activation(beta[:, h, :, :], pc[0:PR, h, 0:4 * PR].rearrange("r (q n) -> r q n", q=4),
                             ACT.Copy).then_inc(S("bt_ev"), 1)

        def g_root(g, it, k):
            g.wait_ge(S("var"), 2 * it + k + 1)
            settle(g, S("met_g"))
            g.tensor_tensor(rstd[:, :, :].rearrange("p t b -> p (t b)"), var[:, :], W["minus_half"][:, :],
                            ALU.pow).then_inc(S("rstd"), 1)

        def g_chunk(g, it, p):
            g_root(g, it, 0)
            g.wait_ge(S("gapm"), it + 1)
            wait(g, "gap_mm", it)
            g.tensor_tensor(by_position(gapped[:, :, :]), by_position(z[:, :, :]), over_positions(gapm[:, :, :]),
                            ALU.mult).then_inc(S("gapped"), 1)
            g.wait_ge(S("svar"), it + 1)
            g.tensor_tensor(sstd[:, :], svar[:, :], W["plus_half"][:, :], ALU.pow).then_inc(S("sstd"), 1)
            g_root(g, it, 1)
            g.wait_ge(S("z"), 2 * it + 2)
            g.wait_ge(S("x3"), it + 1)
            g.wait_ge(S("centred"), 2 * it + 2)
            g.tensor_tensor(x[:, p, :, :], x[:, p, :, :], z[:, :, :], ALU.add).then_inc(S("x3z"), 1)

        def sp_load(sp, it, p, before):
            wait_stored(sp, p, before)
            settle(sp, S("met"))
            sp.dma_start(x[:, p, :, :], x2[it]).then_inc(x_in[p], 16)

        def wait_stored(sp, p, count):
            if not isinstance(count, int) or count > 0:
                sp.wait_ge(stored[p], count)

        def sp_store(sp, it, p):
            sp.wait_ge(S("x4"), 4 * it + 4)
            settle(sp, S("met"))
            sp.dma_start(out[it], x[:, p, :, :]).then_inc(stored[p], 16)

        block = ctx.enter_context(nc.Block())
        pairs = chunks // 2

        @block.sync
        def _(sp):
            for dst, src in loads:
                sp.dma_start(dst, src).then_inc(S("consts"), 16)
            sp_load(sp, 0, 0, 0)
            sp_load(sp, 1, 1, 0)
            with sp.Fori(1, pairs) as i:
                sp_store(sp, 2 * i - 2, 0)
                sp_load(sp, 2 * i, 0, 16 * i)
                sp_store(sp, 2 * i - 1, 1)
                sp_load(sp, 2 * i + 1, 1, 16 * i)
            sp_store(sp, chunks - 2, 0)
            sp_store(sp, chunks - 1, 1)
            for p in range(2):
                sp.wait_ge(stored[p], 16 * pairs)

        def both(eng, chunk):
            for p in range(2):
                chunk(eng, p, p)
            with eng.Fori(1, pairs) as i:
                for p in range(2):
                    chunk(eng, 2 * i + p, p)

        @block.tensor
        def _(pe):
            pe.wait_ge(S("consts"), 16 * len(loads))
            both(pe, pe_chunk)

        @block.vector
        def _(v):
            v.wait_ge(S("consts"), 16 * len(loads))
            v.tensor_scalar(neg[:, :], W["g_par"][:, 0:2], -1.0, None, ALU.mult).then_inc(S("params"), 1)
            v.tensor_scalar(half_zero[:, :], W["g_par"][:, 3:4], 0.5, None, ALU.mult).then_inc(S("params"), 1)
            v.reciprocal(inv_scale[:, :], W["theta"][:, 2:3]).then_inc(S("params"), 1)
            v.wait_ge(S("logged"), 1)
            v.tensor_scalar(log_norm[:, :], log_norm[:, :], -1.0, -0.9189385332046727,
                            ALU.mult, ALU.add).then_inc(S("params"), 1)
            v.wait_ge(S("params"), 4)
            both(v, v_chunk)

        @block.scalar
        def _(a):
            a.activation(log_norm[:, :], W["theta"][:, 2:3], ACT.Ln).then_inc(S("logged"), 1)
            a.wait_ge(S("params"), 4)
            both(a, a_chunk)

        @block.gpsimd
        def _(g):
            both(g, g_chunk)


def program(nc, ins, out, chunks, n_classes):
    import concourse.bass as bass
    from concourse import mybir
    from contextlib import ExitStack
    f32 = mybir.dt.float32
    x2 = nc.dram_tensor("x2_scratch", (chunks, 128, KT, COLS), f32, kind="Internal").ap()
    fwd = nc.dram_tensor("qkv_scratch", (MT, 128, COLS), f32, kind="Internal").ap()
    back = nc.dram_tensor("agg_scratch", (MT, XC, 8, YB), f32, kind="Internal").ap()
    ctx = ExitStack()
    with ctx:
        W = {}
        for name, shape in (
            ("w_qkv", [128, KT, 3 * C]), ("w_proj", [128, 4, C]), ("wv", [128, KT, C]), ("wqk", [128, KT, 64]),
            ("w_sub", [128, KT, C]), ("b_sub", [128, KT]), ("mask8", [128, 128]), ("mask_vo", [128, VO]),
            ("ident", [128, 128]), ("image_of", [PR, 2]), ("bn_scale", [128, KT]), ("bn_shift", [128, KT]),
            ("g_par", [32, 4]), ("theta", [32, 3]), ("gamma", [128, 1]),
            ("minus_half", [128, KT * NB]), ("plus_half", [32, NB]),
        ):
            W[name] = ctx.enter_context(nc.sbuf_tensor(name, shape, f32))
        with nc.sbuf_tensor("conv", [XC, 48, TAPS * XC], f32) as conv:
            W["conv"] = conv
            setup_phase(nc, bass, mybir, ins, W, n_classes)
            layer_one_phase(nc, bass, mybir, ins, W, x2, fwd, back, chunks)
        gate_and_attention_phase(nc, bass, mybir, W, x2, out, ins, chunks)


def constants():
    import numpy as np
    f = np.float32
    p = np.arange(128)
    xo = np.arange(XC) // D
    s = np.arange(PR) % 2
    xs, ys = np.divmod(np.arange(S), HW)
    g = np.arange(32)
    return {
        "c_mask8": (p[:, None] // GS == p[None] // GS).astype(f),
        "c_mask_vo": np.concatenate([p[:, None] // D == p[None] // D, p[:, None] // D == np.arange(8)[None]], 1).astype(f),
        "c_ident": np.eye(128, dtype=f),
        "c_image_of": (s[:, None] == np.arange(2)[None]).astype(f),
        "c_taps": (xo[:, None, None] - np.arange(HW)[None, None] + 2 == np.arange(TAPS)[None, :, None]).astype(f).reshape(XC, -1),
        "c_earlier": (np.arange(C)[None, None] < (128 * np.arange(KT)[None, :, None] + p[:, None, None])).astype(f),
        "c_iota": np.broadcast_to(np.arange(C, dtype=f), (128, C)).copy(),
        "c_sel": (16 * np.arange(KT)[None, :, None] + p[:, None, None] // GS == g[None, None]).astype(f),
        "c_spread": (16 * np.arange(KT)[None, :, None] + p[None, None] // GS == g[:, None, None]).astype(f),
        "c_countdown": np.broadcast_to((S - (ys * HW + xs)).astype(f)[None, :, None], (32, S, NB)).reshape(32, COLS).copy(),
        "c_ruler": np.broadcast_to(np.arange(HW, dtype=f)[None, :, None], (32, HW, NB)).reshape(32, YB).copy(),
        "c_pair_a": ((s[None] == np.arange(2)[:, None]) * -BIG).astype(f),
        "c_pair_b": (s[None] != np.arange(2)[:, None]).astype(f),
    }


def kernel(x, L0_conv_labels, L0_conv_weight, L0_conv_bias, L1_conv_w_qkv, L1_conv_w_dw, L1_conv_w_pw,
           L1_conv_w_proj, L1_conv_bn_gamma, L1_conv_bn_beta, L1_conv_bn_mean, L1_conv_bn_var, L2_conv_weight,
           L2_conv_bias, L2_conv_one, L2_conv_zero, L2_conv_theta, L2_conv_scale, L3_conv_Wq, L3_conv_Wk,
           L3_conv_Wv, L3_conv_gamma):
    import numpy as np
    import concourse.bacc as bacc
    from concourse import mybir
    from concourse.bass_utils import run_bass_kernel_spmd

    x = np.asarray(x)
    chunks = x.shape[0] // NB
    n_classes = L0_conv_weight.shape[0]

    def contiguous(a):
        return np.ascontiguousarray(a)

    def heads(a):
        a = np.asarray(a)
        r = a.reshape((2, 8, 3, D) + a.shape[1:])
        return np.moveaxis(r, 2, 1)

    wq = np.asarray(L1_conv_w_qkv).reshape(3 * C, C)
    w_qkv = heads(wq).reshape(3 * C, KT, 128).transpose(2, 1, 0)
    w_pw = heads(np.asarray(L1_conv_w_pw).reshape(3 * C, D)).reshape(48, D, D).transpose(2, 0, 1)
    w_dw = heads(np.asarray(L1_conv_w_dw).reshape(3 * C, TAPS, TAPS)).reshape(48, D, TAPS, TAPS)
    w_dw = w_dw.transpose(1, 0, 2, 3).reshape(D, 48 * TAPS, TAPS)
    w_proj = np.asarray(L1_conv_w_proj).reshape(C, 4, 128).transpose(2, 1, 0)
    wv = np.asarray(L3_conv_Wv).T.reshape(KT, 128, C).transpose(1, 0, 2)
    wqk = np.concatenate([np.asarray(L3_conv_Wq), np.asarray(L3_conv_Wk)], 0).T.reshape(KT, 128, 64).transpose(1, 0, 2)
    arrays = {
        "x": contiguous(x.reshape(chunks, NB, KT, 128, HW, HW).transpose(0, 3, 2, 5, 4, 1).reshape(chunks, 128, KT, COLS)),
        "labels": np.asarray(L0_conv_labels), "weight": np.asarray(L0_conv_weight).reshape(n_classes, C),
        "bias": np.asarray(L0_conv_bias).reshape(n_classes, 1),
        "w_qkv": contiguous(w_qkv), "w_pw": contiguous(w_pw), "w_dw": contiguous(w_dw), "w_proj": contiguous(w_proj),
        "wv": contiguous(wv), "wqk": contiguous(wqk),
        "labels_by_row": contiguous(np.asarray(L0_conv_labels).reshape(KT, 128).T),
        "bn": contiguous(np.stack([np.asarray(a).reshape(KT, 128) for a in (
            L1_conv_bn_gamma, L1_conv_bn_beta, L1_conv_bn_mean, L1_conv_bn_var)]).transpose(2, 0, 1)),
        "g_par": contiguous(np.stack([np.asarray(a).reshape(32) for a in (L2_conv_weight, L2_conv_bias, L2_conv_one, L2_conv_zero)], 1)),
        "theta": np.concatenate([np.asarray(L2_conv_theta).reshape(2), np.asarray(L2_conv_scale).reshape(1)]),
        "gamma": np.asarray(L3_conv_gamma).reshape(1),
        **constants(),
    }
    nc = bacc.Bacc("TRN2", target_bir_lowering=False, num_devices=1)
    ins = {n: nc.dram_tensor("in_" + n, a.shape, mybir.dt.from_np(a.dtype), kind="ExternalInput").ap()
           for n, a in arrays.items()}
    out = nc.dram_tensor("out", (chunks, 128, KT, COLS), mybir.dt.float32, kind="ExternalOutput").ap()
    program(nc, ins, out, chunks, n_classes)
    r = run_bass_kernel_spmd(nc, [{"in_" + n: a for n, a in arrays.items()}], core_ids=[0])
    got = r.results[0]["out"].reshape(chunks, 128, KT, HW, HW, NB)
    return contiguous(got.transpose(0, 5, 2, 1, 4, 3).reshape(x.shape))
```

```python
C = 256
HW = 7
S = HW * HW
NB = 16
YB = HW * NB
COLS = S * NB
HALF = COLS // 2
KT = C // 128
GS = 8
D = 16
MT = 6
TAPS = 5
PR = 2 * S
VO = 128 + 8
QP = NB // 4
XC = HW * D
BIG = 1e30


def pair_of(ap, b):
    return ap.rearrange("p (r b) -> p b r", b=8)[:, b, :]


def settle(eng, met):
    eng.sem_inc(met, 1)


def setup_phase(nc, bass, mybir, ins, W, n_classes):
    from contextlib import ExitStack
    f32, i32 = mybir.dt.float32, mybir.dt.int32
    ALU = mybir.AluOpType
    AX = mybir.AxisListType
    ctx = ExitStack()
    with ctx:
        def sb(name, shape, dt=f32):
            return ctx.enter_context(nc.sbuf_tensor(name, shape, dt))

        def ps(name, shape):
            return ctx.enter_context(nc.psum_tensor(name, shape, f32))

        def sem(name):
            return ctx.enter_context(nc.semaphore(name))

        lab_row_i = sb("lab_row_i", [128, C], i32)
        lab_col_i = sb("lab_col_i", [128, KT], i32)
        lab_row = sb("lab_row", [128, C])
        lab_col = sb("lab_col", [128, KT])
        earlier = sb("earlier", [128, KT, C])
        same = sb("same", [128, KT, C])
        greater = sb("greater", [128, KT, C])
        place = sb("place", [128, KT, C])
        iota = sb("iota", [128, C])
        dups = sb("dups", [128, KT])
        first = sb("first", [128, KT])
        rank = sb("rank", [128, KT])
        uniq = sb("uniq", [128, KT])
        wrapped = sb("wrapped", [128, KT])
        negative = sb("negative", [128, KT])
        index = sb("index", [128, KT], i32)
        rows = sb("rows", [128, KT, C])
        pw = sb("pw", [XC, 48, D])
        dw = sb("dw", [XC, 48 * TAPS, TAPS])
        dwx = sb("dwx", [XC, 48 * TAPS, HW])
        taps = sb("taps", [XC, TAPS * HW])
        bn = sb("bn", [128, 4, KT])
        bn_std = sb("bn_std", [128, KT])
        bn_t = sb("bn_t", [128, KT])
        p_rank = ps("p_rank", [128, KT])
        p_uniq = ps("p_uniq", [128, KT])
        p_w = ps("p_w", [128, KT, C])

        loaded, labels_in = sem("loaded"), sem("labels_in")
        step = sem("step_v")
        ranked, found, turned = sem("ranked"), sem("found"), sem("turned")
        first_ok, place_ok, index_ok = sem("first_ok"), sem("place_ok"), sem("index_ok")
        gathered = sem("gathered")
        bn_rooted, bn_eps = sem("bn_rooted"), sem("bn_eps")

        loads = [
            (W["w_qkv"][:, :, :], ins["w_qkv"]), (W["w_proj"][:, :, :], ins["w_proj"]),
            (W["wv"][:, :, :], ins["wv"]), (W["wqk"][:, :, :], ins["wqk"]),
            (W["mask8"][:, :], ins["c_mask8"]), (W["mask_vo"][:, :], ins["c_mask_vo"]),
            (W["ident"][:, :], ins["c_ident"]), (W["image_of"][:, :], ins["c_image_of"]),
            (taps[:, :], ins["c_taps"]), (earlier[:, :, :], ins["c_earlier"]),
            (iota[:, :], ins["c_iota"]),
            *[(pw[D * x:D * x + D, :, :], ins["w_pw"]) for x in range(HW)],
            *[(dw[D * x:D * x + D, :, :], ins["w_dw"]) for x in range(HW)],
            (bn[:, :, :], ins["bn"]),
            (W["g_par"][:, :], ins["g_par"]),
            (W["theta"][:, :], ins["theta"].partition_broadcast(32)),
            (W["gamma"][:, :], ins["gamma"].partition_broadcast(128)),
        ]
        block = ctx.enter_context(nc.Block())

        @block.sync
        def _(sp):
            sp.dma_start(lab_row_i[:, :], ins["labels"].partition_broadcast(128)).then_inc(labels_in, 16)
            sp.dma_start(lab_col_i[:, :], ins["labels_by_row"]).then_inc(labels_in, 16)
            for dst, src in loads:
                sp.dma_start(dst, src).then_inc(loaded, 16)
            sp.wait_ge(loaded, 16 * len(loads))

        @block.vector
        def _(v):
            done = [0]

            def link(ins_):
                done[0] += 1
                ins_.then_inc(step, 1)
                v.wait_ge(step, done[0])

            v.wait_ge(labels_in, 32)
            link(v.tensor_copy(lab_row[:, :], lab_row_i[:, :]))
            link(v.tensor_copy(lab_col[:, :], lab_col_i[:, :]))
            v.wait_ge(loaded, 16 * len(loads))
            for t in range(KT):
                link(v.tensor_scalar(same[:, t, :], lab_row[:, :], lab_col[:, t:t + 1], None, ALU.is_equal))
                link(v.tensor_scalar(greater[:, t, :], lab_row[:, :], lab_col[:, t:t + 1], None, ALU.is_gt))
            link(v.tensor_tensor(same[:, :, :], same[:, :, :], earlier[:, :, :], ALU.mult))
            link(v.tensor_reduce(dups[:, :], same[:, :, :], AX.X, ALU.add))
            v.tensor_scalar(first[:, :], dups[:, :], 0.0, None, ALU.is_equal).then_inc(first_ok, 1)
            v.wait_ge(ranked, 1)
            link(v.tensor_copy(rank[:, :], p_rank[:, :]))
            for t in range(KT):
                v.tensor_scalar(place[:, t, :], iota[:, :], rank[:, t:t + 1], first[:, t:t + 1],
                                ALU.is_equal, ALU.mult).then_inc(place_ok, 1)
            v.wait_ge(found, 1)
            link(v.tensor_copy(uniq[:, :], p_uniq[:, :]))
            link(v.tensor_scalar(negative[:, :], uniq[:, :], 0.0, float(n_classes), ALU.is_lt, ALU.mult))
            link(v.tensor_tensor(wrapped[:, :], uniq[:, :], negative[:, :], ALU.add))
            link(v.tensor_scalar(wrapped[:, :], wrapped[:, :], 0.0, float(n_classes - 1), ALU.max, ALU.min))
            v.tensor_copy(index[:, :], wrapped[:, :]).then_inc(index_ok, 1)
            v.wait_ge(bn_rooted, 1)
            link(v.tensor_tensor(W["bn_scale"][:, :], bn_std[:, :], bn[:, 0, :], ALU.mult))
            link(v.tensor_tensor(bn_t[:, :], bn[:, 2, :], W["bn_scale"][:, :], ALU.mult))
            link(v.tensor_tensor(W["bn_shift"][:, :], bn[:, 1, :], bn_t[:, :], ALU.subtract))
            for xo in range(HW):
                for d in range(TAPS):
                    flag = taps[:, d * HW + xo:d * HW + xo + 1]
                    if d == 0:
                        link(v.tensor_scalar(dwx[:, :, xo], dw[:, :, d], flag, None, ALU.mult))
                    else:
                        link(v.scalar_tensor_tensor(dwx[:, :, xo], dw[:, :, d], flag, dwx[:, :, xo],
                                                    ALU.mult, ALU.add))
            v4 = dwx[:, :, :].rearrange("p (g y) x -> p g (y x)", g=48)
            for g in range(0, 48, 8):
                link(v.tensor_tensor(
                    W["conv"][:, g:g + 8, :].rearrange("p g (k o) -> p g k o", o=D),
                    v4[:, g:g + 8, :].unsqueeze(3).to_broadcast([XC, 8, TAPS * HW, D]),
                    pw[:, g:g + 8, :].unsqueeze(2).to_broadcast([XC, 8, TAPS * HW, D]), ALU.mult))
            v.wait_ge(turned, 1)
            link(v.tensor_copy(W["w_sub"][:, :, :], p_w[:, :, :]))

        @block.tensor
        def _(pe):
            pe.wait_ge(first_ok, 1)
            for u in range(KT):
                for t in range(KT):
                    mm = pe.matmul(p_rank[:, u:u + 1], greater[:, t, 128 * u:128 * u + 128],
                                   first[:, t:t + 1], start=(t == 0), stop=(t == KT - 1))
            mm.then_inc(ranked, 1)
            pe.wait_ge(place_ok, KT)
            for u in range(KT):
                for t in range(KT):
                    mm = pe.matmul(p_uniq[:, u:u + 1], place[:, t, 128 * u:128 * u + 128],
                                   lab_col[:, t:t + 1], start=(t == 0), stop=(t == KT - 1))
            mm.then_inc(found, 1)
            pe.wait_ge(gathered, 64)
            for u in range(KT):
                for t in range(KT):
                    mm = pe.transpose(p_w[:, t, 128 * u:128 * u + 128],
                                      rows[:, u, 128 * t:128 * t + 128], W["ident"][:, :])
            mm.then_inc(turned, 1)

        @block.gpsimd
        def _(pool):
            pool.wait_ge(loaded, 16 * len(loads))
            pool.tensor_scalar(bn_t[:, :], bn[:, 3, :], 1e-5, None, ALU.add).then_inc(bn_eps, 1)
            pool.memset(W["minus_half"][:, :], -0.5).then_inc(bn_eps, 1)
            pool.memset(W["plus_half"][:, :], 0.5)
            pool.wait_ge(bn_eps, 2)
            pool.tensor_tensor(bn_std[:, :], bn_t[:, :], W["minus_half"][:, 0:KT], ALU.pow).then_inc(bn_rooted, 1)
            pool.wait_ge(index_ok, 1)
            for u in range(KT):
                at = bass.IndirectOffsetOnAxis(ap=index[:, u:u + 1], axis=0)
                pool.indirect_dma_start(rows[:, u, :], None, ins["weight"], at).then_inc(gathered, 16)
                pool.indirect_dma_start(W["b_sub"][:, u:u + 1], None, ins["bias"], at).then_inc(gathered, 16)
            pool.wait_ge(gathered, 64)


def layer_one_phase(nc, bass, mybir, ins, W, x2_out, fwd, back, chunks):
    from contextlib import ExitStack
    f32 = mybir.dt.float32
    ALU = mybir.AluOpType
    ACT = mybir.ActivationFunctionType
    AX = mybir.AxisListType
    ctx = ExitStack()
    with ctx:
        def sb(name, shape):
            return ctx.enter_context(nc.sbuf_tensor(name, shape, f32))

        def ps(name, shape):
            return ctx.enter_context(nc.psum_tensor(name, shape, f32))

        def sem(name):
            return ctx.enter_context(nc.semaphore(name))

        xa = sb("xa", [128, KT, COLS])
        xb = sb("xb", [128, KT, COLS])
        z = sb("z", [128, KT, COLS])
        sq = sb("sq", [128, KT, COLS])
        qkv = sb("qkv", [128, MT, COLS])
        qr = sb("qr", [128, 2, COLS])
        cx = sb("cx", [XC, 2, 8, YB])
        cy = sb("cy", [XC, 2, 8, YB])
        kT = sb("kT", [PR, 2, 2, 128])
        vT = sb("vT", [PR, 2, 2, 2, VO])
        vk = sb("vk", [128, 2, 2, 2, VO])
        rden = sb("rden", [128, 2, 8])
        den = sb("den", [128, 2, 8])
        oN = sb("oN", [128, 2, 2, 128])
        o = sb("o", [128, COLS])
        stat = sb("stat", [128, KT * NB])
        mean = sb("mean", [128, KT, NB])
        var = sb("var", [128, KT * NB])
        rstd = sb("rstd", [128, KT, NB])

        p_stream = [ps("p_s0", [128, 512]), ps("p_s1", [128, 512])]
        p_t = ps("p_t", [128, 2, 256])
        p_vk = ps("p_vk", [128, 2, 512])
        p_out = ps("p_out", [128, 2, 256])
        p_ot = ps("p_ot", [128, 2, 256])
        p_g = ps("p_g", [128, 512])

        x_in, xa_free = sem("x_in"), sem("xa_free")
        summed, g_mm, mean_ok, centred, squared = sem("summed"), sem("g_mm"), sem("mean_ok"), sem("centred"), sem("squared")
        var_ok, rstd_ok, z_ok = sem("var_ok"), sem("rstd_ok"), sem("z_ok")
        l0_mm, x1_ok = sem("l0_mm"), sem("x1_ok")
        qkv_mm, qkv_ev, conv_mm, conv_ev = sem("qkv_mm"), sem("qkv_ev"), sem("conv_mm"), sem("conv_ev")
        qr_ok = sem("qr_ok")
        xb_ok = sem("xb_ok")
        fwd_w = [sem("fwd_w0"), sem("fwd_w1")]
        cx_in = [sem("cx_in0"), sem("cx_in1")]
        back_w = [sem("back_w0"), sem("back_w1")]
        agg_in = [sem("agg_in0"), sem("agg_in1")]
        t_mm, k_ev, v_ev = sem("t_mm"), sem("k_ev"), sem("v_ev")
        vk_mm, vk_ev, out_mm, den_ok, rden_ok, on_ok = sem("vk_mm"), sem("vk_ev"), sem("out_mm"), sem("den_ok"), sem("rden_ok"), sem("on_ok")
        ot_mm, o_ev, proj_mm, proj_ev = sem("ot_mm"), sem("o_ev"), sem("proj_mm"), sem("proj_ev")
        stored, ones_ok = sem("stored"), sem("ones_ok")
        met_g, met_sp = sem("met_g"), sem("met_sp")

        def by_image(ap):
            return ap.rearrange("p t (s b) -> p t b s", b=NB)

        def by_position(ap):
            return ap.rearrange("p t (s b) -> p t s b", b=NB)

        def over_positions(ap):
            return ap.unsqueeze(2).to_broadcast([128, KT, S, NB])

        def wait(eng, s, count):
            if not isinstance(count, int) or count > 0:
                eng.wait_ge(s, count)

        UN = 4 * QP

        PE_AHEAD = {(0, 1): ("stat", 0), (0, 6): ("stat", 1), (1, 3): ("layer0", 0), (1, 4): ("layer0", 1),
                    (1, 5): ("layer0", 2), (1, 6): ("layer0", 3), (2, 1): ("stat", 2), (2, 5): ("stat", 3)}
        V_AHEAD = {(0, 0): ("sum", 0), (0, 3): ("centre", 0), (0, 5): ("square_sum", 0), (1, 0): ("var", 0),
                   (1, 2): ("scale", 0), (1, 4): ("layer0", 0), (1, 5): ("layer0", 1), (1, 6): ("layer0", 2),
                   (2, 0): ("layer0", 3), (2, 0.5): ("sum", 1), (2, 2): ("centre", 1), (2, 4): ("square_sum", 1),
                   (2, 6): ("var", 1), (3, 2): ("scale", 1)}
        A_AHEAD = {(0, 4): 0, (2, 3): 1}
        STEPS = QP + 3

        def pe_stat(pe, it, k):
            pe.wait_ge(summed, 4 * it + k + 1)
            wait_g(pe, it, k)
            pe.matmul(p_g[:, 0:KT * NB], W["mask8"][:, :], stat[:, :], start=True, stop=True).then_inc(g_mm, 1)

        def wait_g(pe, it, k):
            if k == 0:
                wait(pe, var_ok, 2 * it)
            elif k == 1:
                pe.wait_ge(mean_ok, 2 * it + 1)
            elif k == 2:
                pe.wait_ge(x1_ok, 4 * it + 4)
            else:
                pe.wait_ge(mean_ok, 2 * it + 2)

        def pe_layer0(pe, it, n):
            m, h = n // 2, n % 2
            if n == 0:
                pe.wait_ge(z_ok, 2 * it + 1)
                pe.wait_ge(var_ok, 2 * it + 1)
            else:
                pe.wait_ge(x1_ok, 4 * it + n)
            for t in range(KT):
                mm = pe.matmul(p_g[:, 0:HALF], W["w_sub"][:, t, 128 * m:128 * m + 128],
                               z[:, t, HALF * h:HALF * h + HALF], start=(t == 0), stop=(t == KT - 1))
            mm.then_inc(l0_mm, 1)

        def pe_qkv(pe, it):
            pe.wait_ge(z_ok, 2 * it + 2)
            for m in range(MT):
                for h in range(2):
                    n = 2 * m + h
                    if n >= 2:
                        pe.wait_ge(qkv_ev, 12 * it + n - 1)
                    else:
                        wait(pe, proj_ev, 16 * it - 1 + n)
                    for t in range(KT):
                        mm = pe.matmul(p_stream[h][:, 0:HALF], W["w_qkv"][:, t, 128 * m:128 * m + 128],
                                       z[:, t, HALF * h:HALF * h + HALF], start=(t == 0), stop=(t == KT - 1))
                    mm.then_inc(qkv_mm, 1)

        def pe_conv(pe, it, n):
            m, f = n // 2, n % 2
            if f == 0:
                pe.wait_ge(cx_in[m % 2], 16 * HW * (3 * it + m // 2 + 1))
            if m == 0:
                pe.wait_ge(qkv_ev, 12 * it + 11 + f)
            elif m == 3:
                pe.wait_ge(proj_ev, 16 * it + 3 + f)
            else:
                pe.wait_ge(conv_ev, 12 * it + n - 1)
            for j4 in range(4):
                j = 4 * f + j4
                for i, dy in enumerate((2, 1, 3, 0, 4)):
                    s = dy - 2
                    y0, y1 = max(0, -s), min(HW, HW - s)
                    mm = pe.matmul(p_stream[f][0:XC, YB * j4 + NB * y0:YB * j4 + NB * y1],
                                   W["conv"][:, 8 * m + j, XC * dy:XC * dy + XC],
                                   cx[:, m % 2, j, NB * (y0 + s):NB * (y1 + s)],
                                   start=(i == 0), stop=(i == TAPS - 1))
            mm.then_inc(conv_mm, 1)

        def pe_turn(pe, it, u):
            q, w = u // QP, u % QP
            if q < 2:
                pe.wait_ge(qkv_ev, 12 * it + 6 * q + 6)
            elif w == 0:
                pe.wait_ge(agg_in[q - 2], 16 * 8 * 3 * (it + 1))
            wait(pe, k_ev, UN * it + u)
            wait(pe, v_ev, 2 * (UN * it + u))
            kt, vt = 3 * (q % 2) + 1, 3 * (q % 2) + 2
            for pr in range(2):
                for i, tile in enumerate((kt, vt)):
                    rows = pair_of(qkv[:, tile, :], 2 * w + pr)
                    mm = pe.transpose(p_t[0:PR, pr, 128 * i:128 * i + 128], rows, W["ident"][:, :])
            mm.then_inc(t_mm, 1)

        def pe_vk(pe, it, u):
            pe.wait_ge(k_ev, UN * it + u + 1)
            pe.wait_ge(v_ev, 2 * (UN * it + u + 1))
            wait(pe, vk_ev, UN * it + u)
            for pr in range(2):
                mm = pe.matmul(p_vk[:, pr, 0:2 * VO], kT[:, u % 2, pr, :],
                               vT[:, u % 2, pr, :, :].rearrange("p i n -> p (i n)"), start=True, stop=True)
            mm.then_inc(vk_mm, 1)

        def pe_out(pe, it, u):
            q, w = u // QP, u % QP
            pe.wait_ge(vk_ev, UN * it + u + 1)
            if q < 2:
                pe.wait_ge(qr_ok, 2 * it + q + 1)
            wait(pe, on_ok, UN * it + u)
            src = qr[:, q, :] if q < 2 else qkv[:, 3 * (q - 2), :]
            for pr in range(2):
                for i in range(2):
                    lhs = src.rearrange("p (s b) -> p b s", b=NB)[:, 2 * w + pr + 8 * i, :]
                    mm = pe.matmul(p_out[64 * i:64 * i + S, pr, 0:VO], lhs, vk[:, u % 2, pr, i, :],
                                   start=True, stop=True)
            mm.then_inc(out_mm, 1)

        def pe_out_turn(pe, it, u):
            pe.wait_ge(on_ok, UN * it + u + 1)
            wait(pe, o_ev, UN * it + u)
            for pr in range(2):
                mm = pe.transpose(p_ot[:, pr, 0:128], oN[:, u % 2, pr, :], W["ident"][:, :])
            mm.then_inc(ot_mm, 1)

        def pe_proj(pe, it, q):
            pe.wait_ge(o_ev, UN * it + QP * (q + 1))
            for m in range(KT):
                for h in range(2):
                    n = 2 * m + h
                    if n >= 2:
                        pe.wait_ge(proj_ev, 16 * it + 4 * q + n - 1)
                    elif q < 2:
                        pe.wait_ge(conv_ev, 12 * it + 6 * q + 5 + n)
                    else:
                        pe.wait_ge(proj_ev, 16 * it + 4 * q + n - 1)
                    mm = pe.matmul(p_stream[h][:, 0:HALF], W["w_proj"][:, q, 128 * m:128 * m + 128],
                                   o[:, HALF * h:HALF * h + HALF], start=True, stop=True)
                    mm.then_inc(proj_mm, 1)

        def pe_ahead(pe, it, what, n):
            if what == "stat":
                pe_stat(pe, it, n)
            else:
                pe_layer0(pe, it, n)

        def pe_chunk(pe, it, ahead):
            pe_qkv(pe, it)
            for q in range(4):
                for w in range(STEPS):
                    if w < QP:
                        pe_turn(pe, it, QP * q + w)
                    if q < 2 and w < 6:
                        pe_conv(pe, it, 6 * q + w)
                    if 1 <= w <= QP:
                        pe_vk(pe, it, QP * q + w - 1)
                    if 2 <= w <= QP + 1:
                        pe_out(pe, it, QP * q + w - 2)
                    if w >= 3:
                        pe_out_turn(pe, it, QP * q + w - 3)
                    if ahead is not None and (q, w) in PE_AHEAD:
                        pe_ahead(pe, ahead, *PE_AHEAD[q, w])
                pe_proj(pe, it, q)

        def v_norm(v, it, k, what):
            n = 2 * it + k
            src = xa
            if what == "sum":
                if k == 0:
                    v.wait_ge(x_in, 16 * (it + 1))
                    wait(v, g_mm, 4 * it)
                else:
                    v.wait_ge(x1_ok, 4 * it + 4)
                    v.wait_ge(g_mm, 4 * it + 2)
                v.tensor_reduce(stat[:, :], by_image(src[:, :, :]), AX.X, ALU.add).then_inc(summed, 1)
            elif what == "centre":
                v.wait_ge(g_mm, 2 * n + 1)
                v.tensor_scalar(mean[:, :, :].rearrange("p t b -> p (t b)"), p_g[:, 0:KT * NB],
                                1.0 / (GS * S), None, ALU.mult).then_inc(mean_ok, 1)
                v.wait_ge(mean_ok, n + 1)
                if k == 0:
                    wait(v, qkv_mm, 12 * it)
                else:
                    v.wait_ge(l0_mm, 4 * it + 4)
                v.tensor_tensor(by_position(z[:, :, :]), by_position(src[:, :, :]),
                                over_positions(mean[:, :, :]), ALU.subtract).then_inc(centred, 1)
            elif what == "square_sum":
                v.wait_ge(squared, n + 1)
                v.tensor_reduce(stat[:, :], by_image(sq[:, :, :]), AX.X, ALU.add).then_inc(summed, 1)
            elif what == "var":
                v.wait_ge(g_mm, 2 * n + 2)
                v.tensor_scalar(var[:, :], p_g[:, 0:KT * NB], 1.0 / (GS * S), 1e-5,
                                ALU.mult, ALU.add).then_inc(var_ok, 1)
            else:
                v.wait_ge(rstd_ok, n + 1)
                v.tensor_tensor(by_position(z[:, :, :]), by_position(z[:, :, :]),
                                over_positions(rstd[:, :, :]), ALU.mult).then_inc(z_ok, 1)

        def v_layer0(v, it, n):
            m, h = n // 2, n % 2
            v.wait_ge(l0_mm, 4 * it + n + 1)
            cols = xa[:, m, HALF * h:HALF * h + HALF]
            v.scalar_tensor_tensor(cols, p_g[:, 0:HALF], W["b_sub"][:, m:m + 1], cols,
                                   ALU.add, ALU.add).then_inc(x1_ok, 1)

        def v_qkv(v, it):
            for m in range(MT):
                for h in range(2):
                    n = 2 * m + h
                    v.wait_ge(qkv_mm, 12 * it + n + 1)
                    if n == 0:
                        wait(v, out_mm, UN * it)
                    v.tensor_copy(qkv[:, m, HALF * h:HALF * h + HALF], p_stream[h][:, 0:HALF]).then_inc(qkv_ev, 1)

        def v_vk(v, it, u):
            v.wait_ge(vk_mm, UN * it + u + 1)
            wait(v, out_mm, UN * it + u - 1)
            v.tensor_tensor(vk[:, u % 2, :, :, :], p_vk[:, :, 0:2 * VO].rearrange("p r (i n) -> p r i n", i=2),
                            W["mask_vo"][:, :].unsqueeze(1).unsqueeze(1).to_broadcast([128, 2, 2, VO]),
                            ALU.mult).then_inc(vk_ev, 1)

        def v_norm_out(v, it, u):
            v.wait_ge(out_mm, UN * it + u + 1)
            v.tensor_scalar(den[:, :, :], p_out[:, :, 128:VO], 1e-15, None, ALU.add).then_inc(den_ok, 1)
            v.wait_ge(den_ok, UN * it + u + 1)
            v.reciprocal(rden[:, :, :], den[:, :, :]).then_inc(rden_ok, 1)
            v.wait_ge(rden_ok, UN * it + u + 1)
            wait(v, ot_mm, UN * it + u - 1)
            v.tensor_tensor(oN[:, u % 2, :, :].rearrange("p r (h d) -> p r h d", h=8),
                            p_out[:, :, 0:128].rearrange("p r (h d) -> p r h d", h=8),
                            rden[:, :, :].unsqueeze(3).to_broadcast([128, 2, 8, D]), ALU.mult).then_inc(on_ok, 1)

        def v_proj(v, it, q):
            for m in range(KT):
                for h in range(2):
                    n = 2 * m + h
                    v.wait_ge(proj_mm, 16 * it + 4 * q + n + 1)
                    if q == 0:
                        v.wait_ge(xb_ok, KT * it + m + 1)
                    else:
                        v.wait_ge(proj_ev, 16 * it + 4 * (q - 1) + n + 1)
                    cols = xb[:, m, HALF * h:HALF * h + HALF]
                    v.scalar_tensor_tensor(cols, p_stream[h][:, 0:HALF], W["bn_scale"][:, m:m + 1], cols,
                                           ALU.mult, ALU.add).then_inc(proj_ev, 1)

        def v_ahead(v, it, what, n):
            if what == "layer0":
                v_layer0(v, it, n)
            else:
                v_norm(v, it, n, what)

        def v_chunk(v, it, ahead):
            v_qkv(v, it)
            for q in range(4):
                for w in range(STEPS):
                    if 1 <= w <= QP:
                        v_vk(v, it, QP * q + w - 1)
                    if 2 <= w <= QP + 1:
                        v_norm_out(v, it, QP * q + w - 2)
                    for at in (w, w + 0.5):
                        if ahead is not None and (q, at) in V_AHEAD:
                            v_ahead(v, ahead, *V_AHEAD[q, at])
                v_proj(v, it, q)

        def a_square(a, it, k):
            a.wait_ge(centred, 2 * it + k + 1)
            wait(a, summed, 4 * it + 2 * k)
            a.activation(sq[:, :, :], z[:, :, :], ACT.Square).then_inc(squared, 1)

        def a_turn(a, it, u):
            a.wait_ge(t_mm, UN * it + u + 1)
            wait(a, vk_mm, UN * it + u - 1)
            a.activation(kT[:, u % 2, :, :], p_t[0:PR, :, 0:128], ACT.Relu).then_inc(k_ev, 1)
            for i in range(2):
                a.activation(vT[:, u % 2, :, i, 0:128], p_t[0:PR, :, 128:256], ACT.Copy,
                             scale=W["image_of"][:, i:i + 1]).then_inc(v_ev, 1)

        def a_out(a, it, u):
            q, w = u // QP, u % QP
            a.wait_ge(ot_mm, UN * it + u + 1)
            if w == 0:
                wait(a, proj_mm, 16 * it + 4 * q)
            a.activation(o[:, :].rearrange("p (s i b) -> p b i s", i=2, b=8)[:, 2 * w:2 * w + 2, :, :],
                         p_ot[:, :, 0:128].rearrange("p r (i s) -> p r i s", i=2)[:, :, :, 0:S],
                         ACT.Copy).then_inc(o_ev, 1)

        def a_conv(a, it, n):
            m, f = n // 2, n % 2
            a.wait_ge(conv_mm, 12 * it + n + 1)
            if f == 0:
                wait(a, back_w[m % 2], 16 * (3 * it + m // 2))
            a.activation(cy[:, m % 2, 4 * f:4 * f + 4, :].rearrange("p j n -> p (j n)"),
                         p_stream[f][0:XC, 0:4 * YB],
                         ACT.Relu if m % 3 < 2 else ACT.Copy).then_inc(conv_ev, 1)

        def a_chunk(a, it, ahead):
            for q in range(4):
                for w in range(STEPS):
                    if w < QP:
                        a_turn(a, it, QP * q + w)
                    if q < 2 and w < 6:
                        a_conv(a, it, 6 * q + w)
                    if w >= 3:
                        a_out(a, it, QP * q + w - 3)
                    if ahead is not None and (q, w) in A_AHEAD:
                        a_square(a, ahead, A_AHEAD[q, w])

        def sp_write(sp, it, m):
            sp.wait_ge(qkv_ev, 12 * it + 2 * m + 2)
            settle(sp, met_sp)
            sp.dma_start(fwd[m], qkv[:, m, :]).then_inc(fwd_w[m % 2], 16)

        def sp_read(sp, it, m):
            sp.wait_ge(fwd_w[m % 2], 16 * (3 * it + m // 2 + 1))
            settle(sp, met_sp)
            wait(sp, conv_mm, 12 * it + 2 * m - 2)
            for x in range(HW):
                sp.dma_start(cx[D * x:D * x + D, m % 2, :, :],
                             fwd[m].rearrange("(j c) (x n) -> x c j n", c=D, x=HW)[x]).then_inc(cx_in[m % 2], 16)

        def sp_back_write(sp, it, m):
            sp.wait_ge(conv_ev, 12 * it + 2 * m + 2)
            settle(sp, met_sp)
            sp.dma_start(back[m], cy[:, m % 2, :, :]).then_inc(back_w[m % 2], 16)

        def sp_back_read(sp, it, m):
            sp.wait_ge(back_w[m % 2], 16 * (3 * it + m // 2 + 1))
            settle(sp, met_sp)
            if m % 3 == 0:
                sp.wait_ge(t_mm, UN * it + QP * (m // 3 + 1))
                settle(sp, met_sp)
                for n in (m + 1, m + 2):
                    sp.wait_ge(fwd_w[n % 2], 16 * (3 * it + n // 2 + 1))
                    settle(sp, met_sp)
                sp.wait_ge(qr_ok, 2 * it + m // 3 + 1)
                settle(sp, met_sp)
            for j in range(8):
                sp.dma_start(qkv[D * j:D * j + D, m, :].rearrange("o (x n) -> o x n", x=HW),
                             back[m].rearrange("(x o) j n -> j o x n", o=D)[j]).then_inc(agg_in[m // 3], 16)

        def sp_chunk(sp, it, ahead):
            sp_write(sp, it, 0)
            sp_write(sp, it, 1)
            sp_read(sp, it, 0)
            sp_write(sp, it, 2)
            sp_read(sp, it, 1)
            if ahead is not None:
                sp.wait_ge(xb_ok, KT * it + KT)
                settle(sp, met_sp)
                sp.dma_start(xa[:, :, :], ins["x"][ahead]).then_inc(x_in, 16)
            for m in range(MT):
                if m + 3 < MT:
                    sp_write(sp, it, m + 3)
                if m + 2 < MT:
                    sp_read(sp, it, m + 2)
                sp_back_write(sp, it, m)
                if m >= 1:
                    sp_back_read(sp, it, m - 1)
            sp_back_read(sp, it, MT - 1)
            sp.wait_ge(proj_ev, 16 * it + 16)
            settle(sp, met_sp)
            sp.dma_start(x2_out[it], xb[:, :, :]).then_inc(stored, 16)

        def g_start(g, it):
            g.wait_ge(x1_ok, 4 * it + 4)
            wait(g, stored, 16 * it)
            g.wait_ge(centred, 2 * it + 2)
            settle(g, met_g)
            for m in range(KT):
                g.tensor_scalar(xb[:, m, :], xa[:, m, :], W["bn_shift"][:, m:m + 1], None, ALU.add).then_inc(xb_ok, 1)
            wait(g, out_mm, UN * it - 2 * QP)
            for h in range(2):
                g.wait_ge(qkv_ev, 12 * it + 6 * h + 2)
                settle(g, met_g)
                g.tensor_scalar(qr[:, h, :], qkv[:, 3 * h, :], 0.0, None, ALU.max).then_inc(qr_ok, 1)

        def g_root(g, it, k):
            g.wait_ge(var_ok, 2 * it + k + 1)
            settle(g, met_g)
            g.tensor_tensor(rstd[:, :, :].rearrange("p t b -> p (t b)"), var[:, :], W["minus_half"][:, :],
                            ALU.pow).then_inc(rstd_ok, 1)

        def g_chunk(g, it, ahead):
            g_start(g, it)
            if ahead is not None:
                for k in range(2):
                    g_root(g, ahead, k)

        block = ctx.enter_context(nc.Block())

        @block.sync
        def _(sp):
            sp.dma_start(xa[:, :, :], ins["x"][0]).then_inc(x_in, 16)
            sp_chunk(sp, 0, 1)
            with sp.Fori(1, chunks - 1) as it:
                sp_chunk(sp, it, it + 1)
            sp_chunk(sp, chunks - 1, None)
            sp.wait_ge(stored, 16 * chunks)

        @block.tensor
        def _(pe):
            pe.wait_ge(ones_ok, 4)
            for what in PE_AHEAD.values():
                pe_ahead(pe, 0, *what)
            pe_chunk(pe, 0, 1)
            with pe.Fori(1, chunks - 1) as it:
                pe_chunk(pe, it, it + 1)
            pe_chunk(pe, chunks - 1, None)

        @block.vector
        def _(v):
            for n in range(2):
                v.tensor_copy(vT[:, n, :, :, 128:VO].rearrange("p r i h -> p r i h"),
                              W["image_of"][:, :].unsqueeze(1).unsqueeze(3).to_broadcast([PR, 2, 2, 8])).then_inc(ones_ok, 1)
            v.memset(p_out[:, :, :], 1.0).then_inc(ones_ok, 1)
            v.memset(p_ot[:, :, :], 0.0).then_inc(ones_ok, 1)
            v.wait_ge(ones_ok, 4)
            for what in V_AHEAD.values():
                v_ahead(v, 0, *what)
            v_chunk(v, 0, 1)
            with v.Fori(1, chunks - 1) as it:
                v_chunk(v, it, it + 1)
            v_chunk(v, chunks - 1, None)

        @block.scalar
        def _(a):
            for k in range(2):
                a_square(a, 0, k)
            a_chunk(a, 0, 1)
            with a.Fori(1, chunks - 1) as it:
                a_chunk(a, it, it + 1)
            a_chunk(a, chunks - 1, None)

        @block.gpsimd
        def _(g):
            for k in range(2):
                g_root(g, 0, k)
            g_chunk(g, 0, 1)
            with g.Fori(1, chunks - 1) as it:
                g_chunk(g, it, it + 1)
            g_chunk(g, chunks - 1, None)


def gate_and_attention_phase(nc, bass, mybir, W, x2, out, ins, chunks):
    from contextlib import ExitStack
    f32 = mybir.dt.float32
    ALU = mybir.AluOpType
    ACT = mybir.ActivationFunctionType
    AX = mybir.AxisListType
    ctx = ExitStack()
    G = C // GS
    with ctx:
        def sb(name, shape):
            return ctx.enter_context(nc.sbuf_tensor(name, shape, f32))

        def ps(name, shape):
            return ctx.enter_context(nc.psum_tensor(name, shape, f32))

        def sem(name):
            return ctx.enter_context(nc.semaphore(name))

        x = [sb("x2", [128, KT, COLS]), sb("x3", [128, KT, COLS])]
        x4 = sb("x4", [128, KT, COLS])
        z = [sb("z2", [128, KT, COLS]), sb("z3", [128, KT, COLS])]
        sq = [sb("sq2", [128, KT, COLS]), sb("sq3", [128, KT, COLS])]
        stat = [sb("stat2", [128, KT * NB]), sb("stat3", [128, KT * NB])]
        mean = [sb("mean2", [128, KT, NB]), sb("mean3", [128, KT, NB])]
        var = [sb("var2", [128, KT * NB]), sb("var3", [128, KT * NB])]
        rstd = [sb("rstd2", [128, KT, NB]), sb("rstd3", [128, KT, NB])]
        prod = sb("prod", [128, KT, COLS])
        gapped = sb("gapped", [128, KT, COLS])
        sel = sb("sel", [128, KT, G])
        spread = sb("spread", [G, KT, 128])
        countdown = sb("countdown", [G, COLS])
        ruler = sb("ruler", [G, YB])
        pair_a = sb("pair_a", [2, PR])
        pair_b = sb("pair_b", [2, PR])
        s_sb = sb("s_sb", [G, COLS])
        hot = sb("hot", [G, COLS])
        best = sb("best", [G, NB])
        last = sb("last", [G, NB])
        idx = sb("idx", [G, NB])
        row = sb("row", [G, NB])
        col = sb("col", [G, NB])
        dist = sb("dist", [G, 2, YB])
        dist2 = sb("dist2", [G, 2, YB])
        gauss = sb("gauss", [G, 2, YB])
        dsum = sb("dsum", [G, COLS])
        gap_sim = sb("gap_sim", [G, COLS])
        sim = sb("sim", [G, COLS])
        simsq = sb("simsq", [G, COLS])
        gate = sb("gate", [G, COLS])
        ssum = sb("ssum", [G, NB])
        smean = sb("smean", [G, NB])
        ssq = sb("ssq", [G, NB])
        svar = sb("svar", [G, NB])
        sstd = sb("sstd", [G, NB])
        sinv = sb("sinv", [G, NB])
        qv = sb("qv", [128, KT, NB])
        gap = sb("gap", [128, KT, NB])
        gapm = sb("gapm", [128, KT, NB])
        half_par = sb("half_par", [G, 2])
        half_zero = sb("half_zero", [G, 1])
        inv_scale = sb("inv_scale", [G, 1])
        log_norm = sb("log_norm", [G, 1])
        f_sb = sb("f_sb", [G, COLS])
        g_sb = sb("g_sb", [G, COLS])
        hh = sb("hh", [PR, 8, C])
        sc = sb("sc", [PR, 2, 4, PR])
        smx = sb("smx", [PR, 2, 4])
        ssm = sb("ssm", [PR, 2, 4])
        srec = sb("srec", [PR, 2, 4])
        beta = sb("beta", [PR, 2, 4, PR])
        p_wide = ps("p_wide", [128, 2, 512])
        p_group = ps("p_group", [128, 2, 512])
        p_a = ps("p_a", [128, 2, 512])
        p_b = ps("p_b", [128, 2, 512])
        p_stat = [p_group, p_a]

        names = """x_in stored consts met_sp met_g params logged
            sum2 g_mm2 mean2 centred2 squared2 var2 rstd2 z2 sum3 g_mm3 mean3 centred3 squared3 var3 rstd3 z3
            s_mm s_ev best at_best counted last hot gap gapm gapped hot_mm idx row col apart dist dist2 gauss
            picked qv prod gap_mm gap_ev sim_mm dsum sim_max sim ssum smean sim_centred sim_squared ssq svar
            sstd sstd_eps sinv context tanh gate gate_mm gated x3
            f_mm g_mm fg_ev score_mm smx shifted exp hh_mm hh_ev ssm srec probs bt_mm bt_ev o_mm x3z x4_ok""".split()
        sems = {name: sem("p2_" + name) for name in names}

        def done(ins_, name):
            return ins_.then_inc(sems[name], 1)

        def wait(eng, name, count):
            if not isinstance(count, int) or count > 0:
                eng.wait_ge(sems[name], count)

        def by_image(ap):
            return ap.rearrange("p t (s b) -> p t b s", b=NB)

        def by_position(ap):
            return ap.rearrange("p t (s b) -> p t s b", b=NB)

        def over_positions(ap):
            return ap.unsqueeze(2).to_broadcast([128, KT, S, NB])

        def g_image(ap):
            return ap.rearrange("g (s b) -> g b s", b=NB)

        def g_position(ap):
            return ap.rearrange("g (s b) -> g s b", b=NB)

        def g_over(ap):
            return ap.unsqueeze(1).to_broadcast([G, S, NB])

        def halves(ap):
            return ap.rearrange("p (h n) -> p h n", h=2)

        loads = [(sel[:, :, :], ins["c_sel"]), (spread[:, :, :], ins["c_spread"]),
                 (countdown[:, :], ins["c_countdown"]), (ruler[:, :], ins["c_ruler"]),
                 (pair_a[:, :], ins["c_pair_a"]), (pair_b[:, :], ins["c_pair_b"])]

        def v_sum(v, it, k):
            if k == 0:
                v.wait_ge(sems["x_in"], 16 * (it + 1))
            else:
                wait(v, "x3", it + 1)
            wait(v, f"g_mm{k + 2}", 2 * it)
            done(v.tensor_reduce(stat[k][:, :], by_image(x[k][:, :, :]), AX.X, ALU.add), f"sum{k + 2}")

        def v_centre(v, it, k):
            wait(v, f"g_mm{k + 2}", 2 * it + 1)
            done(v.tensor_scalar(mean[k][:, :, :].rearrange("p t b -> p (t b)"), p_stat[k][:, 0, 0:KT * NB],
                                 1.0 / (GS * S), None, ALU.mult), f"mean{k + 2}")
            wait(v, f"mean{k + 2}", it + 1)
            if k == 1:
                wait(v, "hh_mm", 8 * it)
                wait(v, "g_mm", it)
                wait(v, "x3z", it)
            done(v.tensor_tensor(by_position(z[k][:, :, :]), by_position(x[k][:, :, :]),
                                 over_positions(mean[k][:, :, :]), ALU.subtract), f"centred{k + 2}")

        def v_square_sum(v, it, k):
            wait(v, f"squared{k + 2}", it + 1)
            done(v.tensor_reduce(stat[k][:, :], by_image(sq[k][:, :, :]), AX.X, ALU.add), f"sum{k + 2}")

        def v_var(v, it, k):
            wait(v, f"g_mm{k + 2}", 2 * it + 2)
            done(v.tensor_scalar(var[k][:, :], p_stat[k][:, 0, 0:KT * NB], 1.0 / (GS * S), 1e-5,
                                 ALU.mult, ALU.add), f"var{k + 2}")

        def v_scale(v, it, k):
            wait(v, f"rstd{k + 2}", it + 1)
            done(v.tensor_tensor(by_position(z[k][:, :, :]), by_position(z[k][:, :, :]),
                                 over_positions(rstd[k][:, :, :]), ALU.mult), f"z{k + 2}")

        def v_then(v, it, ins_, name):
            done(ins_, name)
            wait(v, name, it + 1)

        def v_gap(v, it):
            wait(v, "z2", it + 1)
            v_then(v, it, v.tensor_reduce(gap[:, :, :], by_image(z[0][:, :, :]), AX.X, ALU.add), "gap")
            done(v.tensor_scalar(gapm[:, :, :], gap[:, :, :], 1.0 / S, None, ALU.mult), "gapm")

        def v_hot(v, it):
            wait(v, "s_ev", 2 * it + 2)
            v_then(v, it, v.tensor_reduce(best[:, :], g_image(s_sb[:, :]), AX.X, ALU.max), "best")
            wait(v, "hot_mm", 2 * it)
            v_then(v, it, v.tensor_tensor(g_position(hot[:, :]), g_position(s_sb[:, :]), g_over(best[:, :]),
                                          ALU.is_equal), "at_best")
            v_then(v, it, v.tensor_tensor(hot[:, :], hot[:, :], countdown[:, :], ALU.mult), "counted")
            v_then(v, it, v.tensor_reduce(last[:, :], g_image(hot[:, :]), AX.X, ALU.max), "last")
            done(v.tensor_tensor(g_position(hot[:, :]), g_position(hot[:, :]), g_over(last[:, :]),
                                 ALU.is_equal), "hot")

        def v_dist(v, it):
            v_then(v, it, v.tensor_scalar(idx[:, :], last[:, :], -1.0, float(S), ALU.mult, ALU.add), "idx")
            for r in range(1, HW):
                if r == 1:
                    i = v.tensor_scalar(row[:, :], idx[:, :], float(HW * r), None, ALU.is_ge)
                else:
                    i = v.scalar_tensor_tensor(row[:, :], idx[:, :], float(HW * r), row[:, :], ALU.is_ge, ALU.add)
                done(i, "row")
                wait(v, "row", (HW - 1) * it + r)
            v_then(v, it, v.scalar_tensor_tensor(col[:, :], row[:, :], -float(HW), idx[:, :],
                                                 ALU.mult, ALU.add), "col")
            for k, at in enumerate((row, col)):
                done(v.tensor_tensor(dist[:, k, :].rearrange("g (y b) -> g y b", b=NB),
                                     ruler[:, :].rearrange("g (y b) -> g y b", b=NB),
                                     at[:, :].unsqueeze(1).to_broadcast([G, HW, NB]), ALU.subtract), "apart")
            wait(v, "apart", 2 * it + 2)
            for k in range(2):
                done(v.tensor_scalar(dist[:, k, :], dist[:, k, :], W["theta"][:, k:k + 1], None, ALU.mult), "dist")

        def v_picked(v, it):
            for t in range(KT):
                wait(v, "hot_mm", 2 * it + t + 1)
                done(v.tensor_tensor(halves(prod[:, t, :]), halves(z[0][:, t, :]), p_wide[:, :, 0:HALF],
                                     ALU.mult), "picked")
            wait(v, "picked", 2 * it + 2)
            v_then(v, it, v.tensor_reduce(qv[:, :, :], by_image(prod[:, :, :]), AX.X, ALU.add), "qv")
            done(v.tensor_tensor(by_position(prod[:, :, :]), by_position(z[0][:, :, :]),
                                 over_positions(qv[:, :, :]), ALU.mult), "prod")

        def v_dsum(v, it):
            wait(v, "gauss", it + 1)
            done(v.tensor_tensor(
                dsum[:, :].rearrange("g (x y b) -> g x y b", x=HW, y=HW),
                gauss[:, 0, :].rearrange("g (y b) -> g y b", b=NB).unsqueeze(1).to_broadcast([G, HW, HW, NB]),
                gauss[:, 1, :].rearrange("g (x b) -> g x b", b=NB).unsqueeze(2).to_broadcast([G, HW, HW, NB]),
                ALU.add), "dsum")

        def v_sim(v, it):
            wait(v, "dsum", it + 1)
            wait(v, "sim_mm", it + 1)
            v_then(v, it, v.scalar_tensor_tensor(halves(sim[:, :]), p_group[0:G, :, 0:HALF], half_zero[:, 0:1],
                                                 halves(dsum[:, :]), ALU.mult, ALU.mult), "sim_max")
            wait(v, "gap_ev", 2 * it + 2)
            v_then(v, it, v.tensor_tensor(sim[:, :], sim[:, :], gap_sim[:, :], ALU.add), "sim")
            v_then(v, it, v.tensor_reduce(ssum[:, :], g_image(sim[:, :]), AX.X, ALU.add), "ssum")
            v_then(v, it, v.tensor_scalar(smean[:, :], ssum[:, :], 1.0 / S, None, ALU.mult), "smean")
            done(v.tensor_tensor(g_position(sim[:, :]), g_position(sim[:, :]), g_over(smean[:, :]),
                                 ALU.subtract), "sim_centred")

        def v_spread_of_sim(v, it):
            wait(v, "sim_squared", it + 1)
            v_then(v, it, v.tensor_reduce(ssq[:, :], g_image(simsq[:, :]), AX.X, ALU.add), "ssq")
            done(v.tensor_scalar(svar[:, :], ssq[:, :], 1.0 / (S - 1), None, ALU.mult), "svar")

        def v_context(v, it):
            wait(v, "sstd", it + 1)
            v_then(v, it, v.tensor_scalar(sstd[:, :], sstd[:, :], 1e-5, None, ALU.add), "sstd_eps")
            v_then(v, it, v.reciprocal(sinv[:, :], sstd[:, :]), "sinv")
            done(v.tensor_tensor(g_position(sim[:, :]), g_position(sim[:, :]), g_over(sinv[:, :]),
                                 ALU.mult), "context")

        def v_gate(v, it):
            wait(v, "tanh", it + 1)
            done(v.tensor_scalar(gate[:, :], gate[:, :], 0.5, 0.5, ALU.mult, ALU.add), "gate")

        def v_x3(v, it):
            for t in range(KT):
                wait(v, "gate_mm", 2 * it + t + 1)
                if t == 0:
                    wait(v, "sim_mm", it + 1)
                done(v.tensor_tensor(halves(prod[:, t, :]), halves(z[0][:, t, :]), p_wide[:, :, 0:HALF],
                                     ALU.mult), "gated")
            wait(v, "gated", 2 * it + 2)
            wait(v, "x3z", it)
            done(v.tensor_tensor(x[1][:, :, :], x[0][:, :, :], prod[:, :, :], ALU.add), "x3")

        scores = p_a[0:PR, :, 0:4 * PR].rearrange("r h (q n) -> r h q n", q=4)

        def over(ap):
            return ap.unsqueeze(3).to_broadcast([PR, 2, 4, PR])

        def v_shift(v, it):
            wait(v, "score_mm", 2 * it + 2)
            v_then(v, it, v.tensor_reduce(smx[:, :, :], scores, AX.X, ALU.max), "smx")
            wait(v, "bt_mm", 2 * it)
            done(v.tensor_tensor(sc[:, :, :, :], scores, over(smx[:, :, :]), ALU.subtract), "shifted")

        def v_probs(v, it):
            wait(v, "exp", it + 1)
            v_then(v, it, v.tensor_reduce(ssm[:, :, :], sc[:, :, :, :], AX.X, ALU.add), "ssm")
            v_then(v, it, v.reciprocal(srec[:, :, :], ssm[:, :, :]), "srec")
            done(v.tensor_tensor(sc[:, :, :, :], sc[:, :, :, :], over(srec[:, :, :]), ALU.mult), "probs")

        def v_x4(v, it, m):
            wait(v, "x3z", it + 1)
            for h in range(2):
                wait(v, "o_mm", 4 * it + 2 * m + h + 1)
                dst = x4[:, m, :].rearrange("p (r b) -> p b r", b=8)[:, 4 * h:4 * h + 4, :]
                done(v.scalar_tensor_tensor(dst, (p_a, p_b)[m][:, h, 0:4 * PR].rearrange("p (b r) -> p b r", b=4),
                                            W["gamma"][:, 0:1], dst, ALU.mult, ALU.add), "x4_ok")

        def v_body(v, back, front):
            def b(step, *more):
                if back is not None:
                    step(v, back, *more)

            def f(step, *more):
                if front is not None:
                    step(v, front, *more)

            b(v_sum, 1), f(v_sum, 0)
            b(v_centre, 1), f(v_centre, 0)
            b(v_square_sum, 1), f(v_square_sum, 0)
            b(v_var, 1), f(v_var, 0)
            b(v_scale, 1), f(v_scale, 0)
            f(v_gap)
            f(v_hot)
            f(v_dist)
            b(v_shift)
            f(v_picked)
            f(v_dsum)
            b(v_probs)
            f(v_sim)
            b(v_x4, 0)
            f(v_spread_of_sim)
            b(v_x4, 1)
            f(v_context)
            f(v_gate)
            f(v_x3)

        def pe_stat(pe, it, k, n):
            wait(pe, f"sum{k + 2}", 2 * it + n + 1)
            if n == 1:
                wait(pe, f"mean{k + 2}", it + 1)
            elif k == 0:
                wait(pe, "sim_max", it)
            else:
                wait(pe, "x4_ok", 4 * it - 2)
            done(pe.matmul(p_stat[k][:, 0, 0:KT * NB], W["mask8"][:, :], stat[k][:, :], start=True, stop=True),
                 f"g_mm{k + 2}")

        def pe_group_sum(pe, src, name):
            for h in range(2):
                for t in range(KT):
                    mm = pe.matmul(p_group[0:G, h, 0:HALF], sel[:, t, :], src[:, t, HALF * h:HALF * h + HALF],
                                   start=(t == 0), stop=(t == KT - 1))
            done(mm, name)

        def pe_spread(pe, src, t, name):
            for h in range(2):
                mm = pe.matmul(p_wide[:, h, 0:HALF], spread[:, t, :], src[:, HALF * h:HALF * h + HALF],
                               start=True, stop=True)
            done(mm, name)

        def pe_sums(pe, it):
            wait(pe, "z2", it + 1)
            wait(pe, "var2", it + 1)
            pe_group_sum(pe, z[0], "s_mm")

        def pe_gap(pe, it):
            wait(pe, "gapped", it + 1)
            wait(pe, "s_ev", 2 * it + 2)
            pe_group_sum(pe, gapped, "gap_mm")

        def pe_hot(pe, it):
            wait(pe, "hot", it + 1)
            for t in range(KT):
                wait(pe, "gated", 2 * it) if t == 0 else wait(pe, "picked", 2 * it + 1)
                pe_spread(pe, hot, t, "hot_mm")

        def pe_sim(pe, it):
            wait(pe, "prod", it + 1)
            wait(pe, "gap_ev", 2 * it + 2)
            pe_group_sum(pe, prod, "sim_mm")

        def pe_gate(pe, it):
            wait(pe, "gate", it + 1)
            for t in range(KT):
                wait(pe, "picked", 2 * it + 2) if t == 0 else wait(pe, "gated", 2 * it + 1)
                pe_spread(pe, gate, t, "gate_mm")

        def pe_fg(pe, it):
            wait(pe, "z3", it + 1)
            for k, dst in enumerate((p_a, p_b)):
                if k == 0:
                    wait(pe, "var3", it + 1)
                else:
                    wait(pe, "x4_ok", 4 * it)
                for h in range(2):
                    for t in range(KT):
                        mm = pe.matmul(dst[0:G, h, 0:HALF], W["wqk"][:, t, G * k:G * k + G],
                                       z[1][:, t, HALF * h:HALF * h + HALF], start=(t == 0), stop=(t == KT - 1))
                done(mm, ("f_mm", "g_mm")[k])

        def pe_scores(pe, it):
            wait(pe, "fg_ev", 4 * it + 4)
            for h in range(2):
                for q in range(4):
                    f, g = (pair_of(t[:, :], 4 * h + q) for t in (f_sb, g_sb))
                    pe.matmul(p_a[0:PR, h, PR * q:PR * q + PR], g, f, start=True, stop=False)
                    mm = pe.matmul(p_a[0:PR, h, PR * q:PR * q + PR], pair_a[:, :], pair_b[:, :],
                                   start=False, stop=True)
                done(mm, "score_mm")

        def pe_hh(pe, it, n):
            if n < 2:
                wait(pe, "fg_ev", 4 * it + 4)
            else:
                wait(pe, "hh_ev", 4 * it + n - 1)
            for q in range(2):
                for t in range(KT):
                    mm = pe.matmul(p_b[0:PR, n % 2, C * q:C * q + C], pair_of(z[1][:, t, :], 2 * n + q),
                                   W["wv"][:, t, :], start=(t == 0), stop=(t == KT - 1))
                done(mm, "hh_mm")

        def pe_out(pe, it):
            wait(pe, "probs", it + 1)
            for h in range(2):
                wait(pe, "hh_ev", 4 * it + 3 + h)
                for q in range(4):
                    mm = pe.transpose(p_b[0:PR, h, PR * q:PR * q + PR], sc[:, h, q, :], W["ident"][0:PR, 0:PR])
                done(mm, "bt_mm")
            for m in range(KT):
                for h in range(2):
                    wait(pe, "bt_ev", 2 * it + h + 1)
                    for q in range(4):
                        mm = pe.matmul((p_a, p_b)[m][:, h, PR * q:PR * q + PR],
                                       hh[:, 4 * h + q, 128 * m:128 * m + 128], beta[:, h, q, :],
                                       start=True, stop=True)
                    done(mm, "o_mm")

        def pe_body(pe, back, front):
            def b(step, *more):
                if back is not None:
                    step(pe, back, *more)

            def f(step, *more):
                if front is not None:
                    step(pe, front, *more)

            b(pe_stat, 1, 0), f(pe_stat, 0, 0)
            b(pe_stat, 1, 1), f(pe_stat, 0, 1)
            b(pe_fg)
            f(pe_sums)
            b(pe_scores)
            f(pe_gap)
            for n in range(4):
                b(pe_hh, n)
            f(pe_hot)
            f(pe_sim)
            b(pe_out)
            f(pe_gate)

        def a_square(a, it, k):
            wait(a, f"centred{k + 2}", it + 1)
            done(a.activation(sq[k][:, :, :], z[k][:, :, :], ACT.Square), f"squared{k + 2}")

        def a_sums(a, it):
            wait(a, "s_mm", it + 1)
            for h in range(2):
                done(a.activation(s_sb[:, HALF * h:HALF * h + HALF], p_group[0:G, h, 0:HALF], ACT.Copy), "s_ev")

        def a_gap(a, it):
            wait(a, "gap_mm", it + 1)
            for h in range(2):
                done(a.activation(gap_sim[:, HALF * h:HALF * h + HALF], p_group[0:G, h, 0:HALF], ACT.Copy,
                                  scale=W["g_par"][:, 2:3]), "gap_ev")

        def a_gauss(a, it):
            wait(a, "dist", 2 * it + 2)
            done(a.activation(dist2[:, :, :], dist[:, :, :], ACT.Square, scale=inv_scale[:, 0:1]), "dist2")
            wait(a, "dist2", it + 1)
            done(a.activation(gauss[:, :, :], dist2[:, :, :], ACT.Exp, scale=-0.5, bias=log_norm[:, 0:1]), "gauss")

        def a_sim_square(a, it):
            wait(a, "sim_centred", it + 1)
            done(a.activation(simsq[:, :], sim[:, :], ACT.Square), "sim_squared")

        def a_tanh(a, it):
            wait(a, "context", it + 1)
            wait(a, "gate_mm", 2 * it)
            done(a.activation(gate[:, :], sim[:, :], ACT.Tanh, scale=half_par[:, 0:1], bias=half_par[:, 1:2]), "tanh")

        def a_fg(a, it):
            for k, (dst, src) in enumerate(((f_sb, p_a), (g_sb, p_b))):
                wait(a, ("f_mm", "g_mm")[k], it + 1)
                for h in range(2):
                    done(a.activation(dst[:, HALF * h:HALF * h + HALF], src[0:G, h, 0:HALF], ACT.Copy), "fg_ev")

        def a_exp(a, it):
            wait(a, "shifted", it + 1)
            done(a.activation(sc[:, :, :, :], sc[:, :, :, :], ACT.Exp), "exp")

        def a_hh(a, it):
            for n in range(4):
                wait(a, "hh_mm", 8 * it + 2 * n + 2)
                if n == 0:
                    wait(a, "o_mm", 4 * it)
                done(a.activation(hh[:, 2 * n:2 * n + 2, :], p_b[0:PR, n % 2, :].rearrange("r (q c) -> r q c", q=2),
                                  ACT.Copy), "hh_ev")

        def a_beta(a, it):
            for h in range(2):
                wait(a, "bt_mm", 2 * it + h + 1)
                done(a.activation(beta[:, h, :, :], p_b[0:PR, h, 0:4 * PR].rearrange("r (q n) -> r q n", q=4),
                                  ACT.Copy), "bt_ev")

        def a_body(a, back, front):
            def b(step, *more):
                if back is not None:
                    step(a, back, *more)

            def f(step, *more):
                if front is not None:
                    step(a, front, *more)

            b(a_square, 1), f(a_square, 0)
            b(a_fg)
            f(a_sums)
            f(a_gap)
            b(a_hh)
            f(a_gauss)
            b(a_exp)
            b(a_beta)
            f(a_sim_square)
            f(a_tanh)

        def g_root(g, it, k):
            wait(g, f"var{k + 2}", it + 1)
            settle(g, sems["met_g"])
            done(g.tensor_tensor(rstd[k][:, :, :].rearrange("p t b -> p (t b)"), var[k][:, :], W["minus_half"][:, :],
                                 ALU.pow), f"rstd{k + 2}")

        def g_gapped(g, it):
            wait(g, "gapm", it + 1)
            wait(g, "gap_mm", it)
            done(g.tensor_tensor(by_position(gapped[:, :, :]), by_position(z[0][:, :, :]),
                                 over_positions(gapm[:, :, :]), ALU.mult), "gapped")

        def g_x3z(g, it):
            wait(g, "z3", it + 1)
            wait(g, "stored", 16 * it)
            done(g.tensor_tensor(x4[:, :, :], x[1][:, :, :], z[1][:, :, :], ALU.add), "x3z")

        def g_deviation(g, it):
            wait(g, "svar", it + 1)
            done(g.tensor_tensor(sstd[:, :], svar[:, :], W["plus_half"][:, :], ALU.pow), "sstd")

        def g_body(g, back, front):
            def b(step, *more):
                if back is not None:
                    step(g, back, *more)

            def f(step, *more):
                if front is not None:
                    step(g, front, *more)

            b(g_root, 1), f(g_root, 0)
            b(g_x3z)
            f(g_gapped)
            f(g_deviation)

        def sp_load(sp, it):
            wait(sp, "x3", it)
            settle(sp, sems["met_sp"])
            sp.dma_start(x[0][:, :, :], x2[it]).then_inc(sems["x_in"], 16)

        def sp_store(sp, it):
            wait(sp, "x4_ok", 4 * it + 4)
            settle(sp, sems["met_sp"])
            sp.dma_start(out[it], x4[:, :, :]).then_inc(sems["stored"], 16)

        def bodies(eng, body):
            body(eng, None, 0)
            body(eng, 0, 1)
            with eng.Fori(1, chunks - 1) as it:
                body(eng, it, it + 1)
            body(eng, chunks - 1, None)

        block = ctx.enter_context(nc.Block())

        @block.sync
        def _(sp):
            for dst, src in loads:
                sp.dma_start(dst, src).then_inc(sems["consts"], 16)
            sp_load(sp, 0)
            sp_load(sp, 1)
            sp_store(sp, 0)
            with sp.Fori(1, chunks - 1) as it:
                sp_load(sp, it + 1)
                sp_store(sp, it)
            sp_store(sp, chunks - 1)
            sp.wait_ge(sems["stored"], 16 * chunks)

        @block.tensor
        def _(pe):
            pe.wait_ge(sems["consts"], 16 * len(loads))
            bodies(pe, pe_body)

        @block.vector
        def _(v):
            v.wait_ge(sems["consts"], 16 * len(loads))
            done(v.tensor_scalar(half_par[:, :], W["g_par"][:, 0:2], 0.5, None, ALU.mult), "params")
            done(v.tensor_scalar(half_zero[:, :], W["g_par"][:, 3:4], 0.5, None, ALU.mult), "params")
            done(v.reciprocal(inv_scale[:, :], W["theta"][:, 2:3]), "params")
            v.wait_ge(sems["logged"], 1)
            done(v.tensor_scalar(log_norm[:, :], log_norm[:, :], -1.0, -0.9189385332046727,
                                 ALU.mult, ALU.add), "params")
            v.wait_ge(sems["params"], 4)
            bodies(v, v_body)

        @block.scalar
        def _(a):
            done(a.activation(log_norm[:, :], W["theta"][:, 2:3], ACT.Ln), "logged")
            a.wait_ge(sems["params"], 4)
            bodies(a, a_body)

        @block.gpsimd
        def _(g):
            bodies(g, g_body)


def program(nc, ins, out, chunks, n_classes):
    import concourse.bass as bass
    from concourse import mybir
    from contextlib import ExitStack
    f32 = mybir.dt.float32
    x2 = nc.dram_tensor("x2_scratch", (chunks, 128, KT, COLS), f32, kind="Internal").ap()
    fwd = nc.dram_tensor("qkv_scratch", (MT, 128, COLS), f32, kind="Internal").ap()
    back = nc.dram_tensor("agg_scratch", (MT, XC, 8, YB), f32, kind="Internal").ap()
    ctx = ExitStack()
    with ctx:
        W = {}
        for name, shape in (
            ("w_qkv", [128, KT, 3 * C]), ("w_proj", [128, 4, C]), ("wv", [128, KT, C]), ("wqk", [128, KT, 64]),
            ("w_sub", [128, KT, C]), ("b_sub", [128, KT]), ("mask8", [128, 128]), ("mask_vo", [128, VO]),
            ("ident", [128, 128]), ("image_of", [PR, 2]), ("bn_scale", [128, KT]), ("bn_shift", [128, KT]),
            ("g_par", [32, 4]), ("theta", [32, 3]), ("gamma", [128, 1]),
            ("minus_half", [128, KT * NB]), ("plus_half", [32, NB]),
        ):
            W[name] = ctx.enter_context(nc.sbuf_tensor(name, shape, f32))
        with nc.sbuf_tensor("conv", [XC, 48, TAPS * XC], f32) as conv:
            W["conv"] = conv
            setup_phase(nc, bass, mybir, ins, W, n_classes)
            layer_one_phase(nc, bass, mybir, ins, W, x2, fwd, back, chunks)
        gate_and_attention_phase(nc, bass, mybir, W, x2, out, ins, chunks)


def constants():
    import numpy as np
    f = np.float32
    p = np.arange(128)
    xo = np.arange(XC) // D
    s = np.arange(PR) % 2
    xs, ys = np.divmod(np.arange(S), HW)
    g = np.arange(32)
    return {
        "c_mask8": (p[:, None] // GS == p[None] // GS).astype(f),
        "c_mask_vo": np.concatenate([p[:, None] // D == p[None] // D, p[:, None] // D == np.arange(8)[None]], 1).astype(f),
        "c_ident": np.eye(128, dtype=f),
        "c_image_of": (s[:, None] == np.arange(2)[None]).astype(f),
        "c_taps": (xo[:, None, None] - np.arange(HW)[None, None] + 2 == np.arange(TAPS)[None, :, None]).astype(f).reshape(XC, -1),
        "c_earlier": (np.arange(C)[None, None] < (128 * np.arange(KT)[None, :, None] + p[:, None, None])).astype(f),
        "c_iota": np.broadcast_to(np.arange(C, dtype=f), (128, C)).copy(),
        "c_sel": (16 * np.arange(KT)[None, :, None] + p[:, None, None] // GS == g[None, None]).astype(f),
        "c_spread": (16 * np.arange(KT)[None, :, None] + p[None, None] // GS == g[:, None, None]).astype(f),
        "c_countdown": np.broadcast_to((S - (ys * HW + xs)).astype(f)[None, :, None], (32, S, NB)).reshape(32, COLS).copy(),
        "c_ruler": np.broadcast_to(np.arange(HW, dtype=f)[None, :, None], (32, HW, NB)).reshape(32, YB).copy(),
        "c_pair_a": ((s[None] == np.arange(2)[:, None]) * -BIG).astype(f),
        "c_pair_b": (s[None] != np.arange(2)[:, None]).astype(f),
    }


def kernel(x, L0_conv_labels, L0_conv_weight, L0_conv_bias, L1_conv_w_qkv, L1_conv_w_dw, L1_conv_w_pw,
           L1_conv_w_proj, L1_conv_bn_gamma, L1_conv_bn_beta, L1_conv_bn_mean, L1_conv_bn_var, L2_conv_weight,
           L2_conv_bias, L2_conv_one, L2_conv_zero, L2_conv_theta, L2_conv_scale, L3_conv_Wq, L3_conv_Wk,
           L3_conv_Wv, L3_conv_gamma):
    import numpy as np
    import concourse.bacc as bacc
    from concourse import mybir
    from concourse.bass_utils import run_bass_kernel_spmd

    x = np.asarray(x)
    chunks = x.shape[0] // NB
    n_classes = L0_conv_weight.shape[0]

    def contiguous(a):
        return np.ascontiguousarray(a)

    def heads(a):
        a = np.asarray(a)
        r = a.reshape((2, 8, 3, D) + a.shape[1:])
        return np.moveaxis(r, 2, 1)

    wq = np.asarray(L1_conv_w_qkv).reshape(3 * C, C)
    w_qkv = heads(wq).reshape(3 * C, KT, 128).transpose(2, 1, 0)
    w_pw = heads(np.asarray(L1_conv_w_pw).reshape(3 * C, D)).reshape(48, D, D).transpose(2, 0, 1)
    w_dw = heads(np.asarray(L1_conv_w_dw).reshape(3 * C, TAPS, TAPS)).reshape(48, D, TAPS, TAPS)
    w_dw = w_dw.transpose(1, 0, 2, 3).reshape(D, 48 * TAPS, TAPS)
    w_proj = np.asarray(L1_conv_w_proj).reshape(C, 4, 128).transpose(2, 1, 0)
    wv = np.asarray(L3_conv_Wv).T.reshape(KT, 128, C).transpose(1, 0, 2)
    wqk = np.concatenate([np.asarray(L3_conv_Wq), np.asarray(L3_conv_Wk)], 0).T.reshape(KT, 128, 64).transpose(1, 0, 2)
    arrays = {
        "x": contiguous(x.reshape(chunks, NB, KT, 128, HW, HW).transpose(0, 3, 2, 5, 4, 1).reshape(chunks, 128, KT, COLS)),
        "labels": np.asarray(L0_conv_labels), "weight": np.asarray(L0_conv_weight).reshape(n_classes, C),
        "bias": np.asarray(L0_conv_bias).reshape(n_classes, 1),
        "w_qkv": contiguous(w_qkv), "w_pw": contiguous(w_pw), "w_dw": contiguous(w_dw), "w_proj": contiguous(w_proj),
        "wv": contiguous(wv), "wqk": contiguous(wqk),
        "labels_by_row": contiguous(np.asarray(L0_conv_labels).reshape(KT, 128).T),
        "bn": contiguous(np.stack([np.asarray(a).reshape(KT, 128) for a in (
            L1_conv_bn_gamma, L1_conv_bn_beta, L1_conv_bn_mean, L1_conv_bn_var)]).transpose(2, 0, 1)),
        "g_par": contiguous(np.stack([np.asarray(a).reshape(32) for a in (L2_conv_weight, L2_conv_bias, L2_conv_one, L2_conv_zero)], 1)),
        "theta": np.concatenate([np.asarray(L2_conv_theta).reshape(2), np.asarray(L2_conv_scale).reshape(1)]),
        "gamma": np.asarray(L3_conv_gamma).reshape(1),
        **constants(),
    }
    nc = bacc.Bacc("TRN2", target_bir_lowering=False, num_devices=1)
    ins = {n: nc.dram_tensor("in_" + n, a.shape, mybir.dt.from_np(a.dtype), kind="ExternalInput").ap()
           for n, a in arrays.items()}
    out = nc.dram_tensor("out", (chunks, 128, KT, COLS), mybir.dt.float32, kind="ExternalOutput").ap()
    program(nc, ins, out, chunks, n_classes)
    r = run_bass_kernel_spmd(nc, [{"in_" + n: a for n, a in arrays.items()}], core_ids=[0])
    got = r.results[0]["out"].reshape(chunks, 128, KT, HW, HW, NB)
    return contiguous(got.transpose(0, 5, 2, 1, 4, 3).reshape(x.shape))
```

```python
C = 256
HW = 7
S = HW * HW
NB = 16
YB = HW * NB
COLS = S * NB
HALF = COLS // 2
KT = C // 128
GS = 8
D = 16
MT = 6
TAPS = 5
PR = 2 * S
HC = 4
VC = 2 * D + 1
VO = 128 + 8
QP = NB // 4
XC = HW * D
BIG = 1e30


def pair_of(ap, b):
    return ap.rearrange("p (r b) -> p b r", b=8)[:, b, :]


def settle(eng, met):
    eng.sem_inc(met, 1)


def setup_phase(nc, bass, mybir, ins, W, n_classes):
    from contextlib import ExitStack
    f32, i32 = mybir.dt.float32, mybir.dt.int32
    ALU = mybir.AluOpType
    AX = mybir.AxisListType
    ctx = ExitStack()
    with ctx:
        def sb(name, shape, dt=f32):
            return ctx.enter_context(nc.sbuf_tensor(name, shape, dt))

        def ps(name, shape):
            return ctx.enter_context(nc.psum_tensor(name, shape, f32))

        def sem(name):
            return ctx.enter_context(nc.semaphore(name))

        lab_row_i = sb("lab_row_i", [128, C], i32)
        lab_col_i = sb("lab_col_i", [128, KT], i32)
        lab_row = sb("lab_row", [128, C])
        lab_col = sb("lab_col", [128, KT])
        earlier = sb("earlier", [128, KT, C])
        same = sb("same", [128, KT, C])
        greater = sb("greater", [128, KT, C])
        place = sb("place", [128, KT, C])
        iota = sb("iota", [128, C])
        dups = sb("dups", [128, KT])
        first = sb("first", [128, KT])
        rank = sb("rank", [128, KT])
        uniq = sb("uniq", [128, KT])
        wrapped = sb("wrapped", [128, KT])
        negative = sb("negative", [128, KT])
        index = sb("index", [128, KT], i32)
        rows = sb("rows", [128, KT, C])
        pw = sb("pw", [XC, 48, D])
        dw = sb("dw", [XC, 48 * TAPS, TAPS])
        dwx = sb("dwx", [XC, 48 * TAPS, HW])
        taps = sb("taps", [XC, TAPS * HW])
        bn = sb("bn", [128, 4, KT])
        bn_std = sb("bn_std", [128, KT])
        bn_t = sb("bn_t", [128, KT])
        p_rank = ps("p_rank", [128, KT])
        p_uniq = ps("p_uniq", [128, KT])
        p_w = ps("p_w", [128, KT, C])

        loaded, labels_in, conv_loaded = sem("loaded"), sem("labels_in"), sem("conv_loaded")
        tapped, conv_ok = sem("tapped"), sem("conv_ok")
        step = sem("step_v")
        ranked, found, turned = sem("ranked"), sem("found"), sem("turned")
        first_ok, place_ok, index_ok = sem("first_ok"), sem("place_ok"), sem("index_ok")
        gathered = sem("gathered")
        bn_rooted, bn_eps = sem("bn_rooted"), sem("bn_eps")

        conv_loads = [
            (taps[:, :], ins["c_taps"]),
            *[(dw[D * x:D * x + D, :, :], ins["w_dw"]) for x in range(HW)],
            *[(pw[D * x:D * x + D, :, :], ins["w_pw"]) for x in range(HW)],
        ]
        loads = [
            (W["w_qkv"][:, :, :], ins["w_qkv"]), (W["w_proj"][:, :, :], ins["w_proj"]),
            (W["wv"][:, :, :], ins["wv"]), (W["wqk"][:, :, :], ins["wqk"]),
            (W["mask8"][:, :], ins["c_mask8"]), (W["mask_vo"][:, :], ins["c_mask_vo"]),
            (W["ident"][:, :], ins["c_ident"]), (W["image_of"][:, :], ins["c_image_of"]),
            (earlier[:, :, :], ins["c_earlier"]),
            (iota[:, :], ins["c_iota"]),
            (bn[:, :, :], ins["bn"]),
            (W["g_par"][:, :], ins["g_par"]),
            (W["theta"][:, :], ins["theta"].partition_broadcast(64)),
            (W["gamma"][:, :], ins["gamma"].partition_broadcast(128)),
        ]
        conv_split = 32

        def conv_product(eng, g):
            v4 = dwx[:, :, :].rearrange("p (g y) x -> p g (y x)", g=48)
            eng.tensor_tensor(
                W["conv"][:, g:g + 8, :].rearrange("p g (k o) -> p g k o", o=D),
                v4[:, g:g + 8, :].unsqueeze(3).to_broadcast([XC, 8, TAPS * HW, D]),
                pw[:, g:g + 8, :].unsqueeze(2).to_broadcast([XC, 8, TAPS * HW, D]), ALU.mult).then_inc(conv_ok, 1)

        block = ctx.enter_context(nc.Block())

        @block.sync
        def _(sp):
            sp.dma_start(lab_row_i[:, :], ins["labels"].partition_broadcast(128)).then_inc(labels_in, 16)
            sp.dma_start(lab_col_i[:, :], ins["labels_by_row"]).then_inc(labels_in, 16)
            for dst, src in conv_loads:
                sp.dma_start(dst, src).then_inc(conv_loaded, 16)
            for dst, src in loads:
                sp.dma_start(dst, src).then_inc(loaded, 16)
            sp.wait_ge(loaded, 16 * len(loads))

        @block.vector
        def _(v):
            done = [0]

            def link(ins_):
                done[0] += 1
                ins_.then_inc(step, 1)
                v.wait_ge(step, done[0])

            v.wait_ge(labels_in, 32)
            link(v.tensor_copy(lab_row[:, :], lab_row_i[:, :]))
            link(v.tensor_copy(lab_col[:, :], lab_col_i[:, :]))
            v.wait_ge(conv_loaded, 16 * len(conv_loads))
            for d in range(TAPS):
                for xo in range(HW):
                    flag = taps[:, d * HW + xo:d * HW + xo + 1]
                    if d == 0:
                        v.tensor_scalar(dwx[:, :, xo], dw[:, :, d], flag, None, ALU.mult).then_inc(tapped, 1)
                    else:
                        v.wait_ge(tapped, HW * (d - 1) + xo + 1)
                        v.scalar_tensor_tensor(dwx[:, :, xo], dw[:, :, d], flag, dwx[:, :, xo],
                                               ALU.mult, ALU.add).then_inc(tapped, 1)
            v.wait_ge(tapped, HW * TAPS)
            v.wait_ge(loaded, 16 * len(loads))
            for t in range(KT):
                link(v.tensor_scalar(same[:, t, :], lab_row[:, :], lab_col[:, t:t + 1], None, ALU.is_equal))
                link(v.tensor_scalar(greater[:, t, :], lab_row[:, :], lab_col[:, t:t + 1], None, ALU.is_gt))
            link(v.tensor_tensor(same[:, :, :], same[:, :, :], earlier[:, :, :], ALU.mult))
            link(v.tensor_reduce(dups[:, :], same[:, :, :], AX.X, ALU.add))
            v.tensor_scalar(first[:, :], dups[:, :], 0.0, None, ALU.is_equal).then_inc(first_ok, 1)
            v.wait_ge(ranked, 1)
            link(v.tensor_copy(rank[:, :], p_rank[:, :]))
            for t in range(KT):
                v.tensor_scalar(place[:, t, :], iota[:, :], rank[:, t:t + 1], first[:, t:t + 1],
                                ALU.is_equal, ALU.mult).then_inc(place_ok, 1)
            v.wait_ge(found, 1)
            link(v.tensor_copy(uniq[:, :], p_uniq[:, :]))
            link(v.tensor_scalar(negative[:, :], uniq[:, :], 0.0, float(n_classes), ALU.is_lt, ALU.mult))
            link(v.tensor_tensor(wrapped[:, :], uniq[:, :], negative[:, :], ALU.add))
            link(v.tensor_scalar(wrapped[:, :], wrapped[:, :], 0.0, float(n_classes - 1), ALU.max, ALU.min))
            v.tensor_copy(index[:, :], wrapped[:, :]).then_inc(index_ok, 1)
            v.wait_ge(bn_rooted, 1)
            link(v.tensor_tensor(W["bn_scale"][:, :], bn_std[:, :], bn[:, 0, :], ALU.mult))
            link(v.tensor_tensor(bn_t[:, :], bn[:, 2, :], W["bn_scale"][:, :], ALU.mult))
            link(v.tensor_tensor(W["bn_shift"][:, :], bn[:, 1, :], bn_t[:, :], ALU.subtract))
            for g in range(0, conv_split, 8):
                conv_product(v, g)
            v.wait_ge(turned, 1)
            v.tensor_copy(W["w_sub"][:, :, :], p_w[:, :, :])

        @block.tensor
        def _(pe):
            pe.wait_ge(first_ok, 1)
            for u in range(KT):
                for t in range(KT):
                    mm = pe.matmul(p_rank[:, u:u + 1], greater[:, t, 128 * u:128 * u + 128],
                                   first[:, t:t + 1], start=(t == 0), stop=(t == KT - 1))
            mm.then_inc(ranked, 1)
            pe.wait_ge(place_ok, KT)
            for u in range(KT):
                for t in range(KT):
                    mm = pe.matmul(p_uniq[:, u:u + 1], place[:, t, 128 * u:128 * u + 128],
                                   lab_col[:, t:t + 1], start=(t == 0), stop=(t == KT - 1))
            mm.then_inc(found, 1)
            pe.wait_ge(gathered, 64)
            for u in range(KT):
                for t in range(KT):
                    mm = pe.transpose(p_w[:, t, 128 * u:128 * u + 128],
                                      rows[:, u, 128 * t:128 * t + 128], W["ident"][:, :])
            mm.then_inc(turned, 1)

        @block.gpsimd
        def _(pool):
            pool.wait_ge(loaded, 16 * len(loads))
            pool.tensor_scalar(bn_t[:, :], bn[:, 3, :], 1e-5, None, ALU.add).then_inc(bn_eps, 1)
            pool.memset(W["minus_half"][:, :], -0.5).then_inc(bn_eps, 1)
            pool.memset(W["plus_half"][:, :], 0.5)
            pool.wait_ge(bn_eps, 2)
            pool.tensor_tensor(bn_std[:, :], bn_t[:, :], W["minus_half"][:, 0:KT], ALU.pow).then_inc(bn_rooted, 1)
            pool.wait_ge(index_ok, 1)
            for u in range(KT):
                at = bass.IndirectOffsetOnAxis(ap=index[:, u:u + 1], axis=0)
                pool.indirect_dma_start(rows[:, u, :], None, ins["weight"], at).then_inc(gathered, 16)
                pool.indirect_dma_start(W["b_sub"][:, u:u + 1], None, ins["bias"], at).then_inc(gathered, 16)
            pool.wait_ge(tapped, HW * TAPS)
            for g in range(conv_split, 48, 8):
                conv_product(pool, g)
            pool.wait_ge(gathered, 64)


def layer_one_phase(nc, bass, mybir, ins, W, x2_out, fwd, back, chunks):
    from contextlib import ExitStack
    f32 = mybir.dt.float32
    ALU = mybir.AluOpType
    ACT = mybir.ActivationFunctionType
    AX = mybir.AxisListType
    ctx = ExitStack()
    with ctx:
        def sb(name, shape):
            return ctx.enter_context(nc.sbuf_tensor(name, shape, f32))

        def ps(name, shape):
            return ctx.enter_context(nc.psum_tensor(name, shape, f32))

        def sem(name):
            return ctx.enter_context(nc.semaphore(name))

        xa = sb("xa", [128, KT, COLS])
        xb = sb("xb", [128, KT, COLS])
        z = sb("z", [128, KT, COLS])
        sq = sb("sq", [128, KT, COLS])
        qkv = sb("qkv", [128, MT, COLS])
        qr = sb("qr", [128, 2, COLS])
        cx = sb("cx", [XC, 2, 8, YB])
        cy = sb("cy", [XC, 2, 8, YB])
        kT = sb("kT", [PR, 2, 2, 128])
        vT = sb("vT", [PR, 2, 2, 2, HC, VC])
        vk = sb("vk", [128, 2, 2, 2, VO])
        rden = sb("rden", [128, 2, 8])
        den = sb("den", [128, 2, 8])
        oN = sb("oN", [128, 2, 2, 128])
        o = sb("o", [128, COLS])
        stat = sb("stat", [128, KT * NB])
        mean = sb("mean", [128, KT, NB])
        var = sb("var", [128, KT * NB])
        rstd = sb("rstd", [128, KT, NB])

        p_stream = [ps("p_s0", [128, 512]), ps("p_s1", [128, 512])]
        p_t = ps("p_t", [128, 2, 256])
        p_vk = ps("p_vk", [128, 2, 512])
        p_out = ps("p_out", [128, 2, 256])
        p_ot = ps("p_ot", [128, 2, 256])
        p_g = ps("p_g", [128, 512])

        x_in, xa_free = sem("x_in"), sem("xa_free")
        summed, g_mm, mean_ok, centred, squared = sem("summed"), sem("g_mm"), sem("mean_ok"), sem("centred"), sem("squared")
        var_ok, rstd_ok, z_ok = sem("var_ok"), sem("rstd_ok"), sem("z_ok")
        l0_mm, x1_ok = sem("l0_mm"), sem("x1_ok")
        qkv_mm, qkv_ev, conv_mm, conv_ev = sem("qkv_mm"), sem("qkv_ev"), sem("conv_mm"), sem("conv_ev")
        qr_ok = sem("qr_ok")
        xb_ok = sem("xb_ok")
        fwd_w = [sem(f"fwd_w{j}") for j in range(MT)]
        cx_in = [sem("cx_in0"), sem("cx_in1")]
        back_w = [sem("back_w0"), sem("back_w1")]
        agg_kv, agg_q = [sem("agg_kv0"), sem("agg_kv1")], [sem("agg_q0"), sem("agg_q1")]
        t_mm, k_ev, v_ev = sem("t_mm"), sem("k_ev"), sem("v_ev")
        vk_mm, vk_ev, out_mm, den_ok, rden_ok, on_ok = sem("vk_mm"), sem("vk_ev"), sem("out_mm"), sem("den_ok"), sem("rden_ok"), sem("on_ok")
        ot_mm, o_ev, proj_mm, proj_ev = sem("ot_mm"), sem("o_ev"), sem("proj_mm"), sem("proj_ev")
        stored, ones_ok = sem("stored"), sem("ones_ok")
        met_g, met_sp = sem("met_g"), sem("met_sp")

        def by_image(ap):
            return ap.rearrange("p t (s b) -> p t b s", b=NB)

        def by_position(ap):
            return ap.rearrange("p t (s b) -> p t s b", b=NB)

        def over_positions(ap):
            return ap.unsqueeze(2).to_broadcast([128, KT, S, NB])

        def wait(eng, s, count):
            if not isinstance(count, int) or count > 0:
                eng.wait_ge(s, count)

        UN = 4 * QP

        ORDER = (1, 2, 0, 4, 5, 3)

        CONV_AT = {0: (0,), 1: (1,), 2: (2,), 3: (3,), 4: (4,), 5: (5,), 6: (6,), 8: (7,), 9: (8,), 10: (9,),
                   11: (10, 11)}
        PE_AHEAD = {3.25: [("stat", 0)], 5: [("stat", 1)], 7: [("layer0", 0)], 7.5: [("layer0", 1)],
                    8: [("layer0", 2)], 8.5: [("layer0", 3)], 9.5: [("stat", 2)], 11.25: [("stat", 3)]}
        V_AHEAD = {2: [("sum", 0)], 3.5: [("centre", 0)], 4: [("square_sum", 0)], 5: [("var", 0)],
                   6.5: [("scale", 0)], 7: [("layer0", 0)], 7.5: [("layer0", 1)], 8: [("layer0", 2)],
                   9: [("layer0", 3), ("sum", 1)], 10: [("centre", 1)], 10.5: [("square_sum", 1)],
                   11.5: [("var", 1)], 12.5: [("scale", 1)]}
        A_AHEAD = {3.5: 0, 10: 1}
        PROJ_AT = {7: 0, 12: 1, 15: 2}
        STEPS = UN + 3
        QKV_AT = {14: ((0, 1), ()), 15: ((), (2, 3)), 16: ((4, 5), (6, 7)), 17: ((8,), (9,)), 18: ((10,), (11,))}

        def pe_stat(pe, it, k):
            pe.wait_ge(summed, 4 * it + k + 1)
            wait_g(pe, it, k)
            pe.matmul(p_g[:, 0:KT * NB], W["mask8"][:, :], stat[:, :], start=True, stop=True).then_inc(g_mm, 1)

        def wait_g(pe, it, k):
            if k == 0:
                wait(pe, var_ok, 2 * it)
            elif k == 1:
                pe.wait_ge(mean_ok, 2 * it + 1)
            elif k == 2:
                pe.wait_ge(x1_ok, 4 * it + 4)
            else:
                pe.wait_ge(mean_ok, 2 * it + 2)

        def pe_layer0(pe, it, n):
            m, h = n // 2, n % 2
            if n == 0:
                pe.wait_ge(z_ok, 2 * it + 1)
                pe.wait_ge(var_ok, 2 * it + 1)
            else:
                pe.wait_ge(x1_ok, 4 * it + n)
            for t in range(KT):
                mm = pe.matmul(p_g[:, 0:HALF], W["w_sub"][:, t, 128 * m:128 * m + 128],
                               z[:, t, HALF * h:HALF * h + HALF], start=(t == 0), stop=(t == KT - 1))
            mm.then_inc(l0_mm, 1)

        def pe_qkv(pe, it, n):
            m, h = ORDER[n // 2], n % 2
            pe.wait_ge(z_ok, 2 * it + 2)
            if n < 2:
                wait(pe, proj_ev, 16 * (it - 1) + 7 + n)
            else:
                if n < 4:
                    wait(pe, proj_ev, 16 * (it - 1) + 9 + n)
                pe.wait_ge(qkv_ev, 12 * it + n - 1)
            for t in range(KT):
                mm = pe.matmul(p_stream[h][:, 0:HALF], W["w_qkv"][:, t, 128 * m:128 * m + 128],
                               z[:, t, HALF * h:HALF * h + HALF], start=(t == 0), stop=(t == KT - 1))
            mm.then_inc(qkv_mm, 1)

        def pe_conv(pe, it, n):
            k, f = n // 2, n % 2
            m = ORDER[k]
            if f == 0:
                pe.wait_ge(cx_in[k % 2], 16 * HW * (3 * it + k // 2 + 1))
            if n < 2:
                pe.wait_ge(qkv_ev, 12 * it + 11 + n)
                wait(pe, proj_ev, 16 * it - 1 + n)
            elif n in (7, 8):
                pe.wait_ge(proj_ev, 16 * it + n - 4)
            else:
                pe.wait_ge(conv_ev, 12 * it + n - 1)
            for j4 in range(4):
                j = 4 * f + j4
                for i, dy in enumerate((2, 1, 3, 0, 4)):
                    s = dy - 2
                    y0, y1 = max(0, -s), min(HW, HW - s)
                    mm = pe.matmul(p_stream[f][0:XC, YB * j4 + NB * y0:YB * j4 + NB * y1],
                                   W["conv"][:, 8 * m + j, XC * dy:XC * dy + XC],
                                   cx[:, k % 2, j, NB * (y0 + s):NB * (y1 + s)],
                                   start=(i == 0), stop=(i == TAPS - 1))
            mm.then_inc(conv_mm, 1)

        def pe_turn(pe, it, u):
            q, w = u // QP, u % QP
            if q < 2:
                pe.wait_ge(qkv_ev, 12 * it + 6 * q + 4)
            elif w == 0:
                pe.wait_ge(agg_kv[q - 2], 16 * 8 * 2 * (it + 1))
            wait(pe, k_ev, UN * it + u)
            wait(pe, v_ev, 2 * (UN * it + u))
            kt, vt = 3 * (q % 2) + 1, 3 * (q % 2) + 2
            for pr in range(2):
                for i, tile in enumerate((kt, vt)):
                    rows = pair_of(qkv[:, tile, :], 2 * w + pr)
                    mm = pe.transpose(p_t[0:PR, pr, 128 * i:128 * i + 128], rows, W["ident"][:, :])
            mm.then_inc(t_mm, 1)

        def pe_vk(pe, it, u):
            pe.wait_ge(k_ev, UN * it + u + 1)
            pe.wait_ge(v_ev, 2 * (UN * it + u + 1))
            wait(pe, vk_ev, 2 * (UN * it + u - 1))
            for pr in range(2):
                for c in range(HC):
                    mm = pe.matmul(p_vk[32 * c:32 * c + 32, u % 2, 2 * VC * pr:2 * VC * pr + 2 * VC],
                                   kT[:, u % 2, pr, 32 * c:32 * c + 32], vT[:, u % 2, pr, :, c, :],
                                   start=True, stop=True)
            mm.then_inc(vk_mm, 1)

        def pe_out(pe, it, u):
            q, w = u // QP, u % QP
            pe.wait_ge(vk_ev, 2 * (UN * it + u + 1))
            if q < 2:
                pe.wait_ge(qr_ok, 2 * it + q + 1)
            elif w == 0:
                pe.wait_ge(agg_q[q - 2], 16 * 8 * (it + 1))
            wait(pe, on_ok, UN * it + u)
            src = qr[:, q, :] if q < 2 else qkv[:, 3 * (q - 2), :]
            for pr in range(2):
                for i in range(2):
                    lhs = src.rearrange("p (s b) -> p b s", b=NB)[:, 2 * w + pr + 8 * i, :]
                    mm = pe.matmul(p_out[64 * i:64 * i + S, pr, 0:VO], lhs, vk[:, u % 2, pr, i, :],
                                   start=True, stop=True)
            mm.then_inc(out_mm, 1)

        def pe_out_turn(pe, it, u):
            pe.wait_ge(on_ok, UN * it + u + 1)
            wait(pe, o_ev, UN * it + u)
            for pr in range(2):
                mm = pe.transpose(p_ot[:, pr, 0:128], oN[:, u % 2, pr, :], W["ident"][:, :])
            mm.then_inc(ot_mm, 1)

        def proj_bank(q, n):
            return (n + 1) % 2 if q == 0 else n % 2

        def pe_proj(pe, it, q, n, ahead):
            m, h = n // 2, n % 2
            if n == 0:
                pe.wait_ge(o_ev, UN * it + QP * (q + 1))
            if n >= 2:
                pe.wait_ge(proj_ev, 16 * it + 4 * q + n - 1)
            elif q < 2:
                pe.wait_ge(conv_ev, 12 * it + (6, 11)[q] + n)
            elif ahead is None:
                pe.wait_ge(proj_ev, 16 * it + 4 * q - 1 + n)
            else:
                pe.wait_ge(qkv_ev, 12 * ahead + (1, 11)[q - 2] + n)
            pe.matmul(p_stream[proj_bank(q, n)][:, 0:HALF], W["w_proj"][:, q, 128 * m:128 * m + 128],
                      o[:, HALF * h:HALF * h + HALF], start=True, stop=True).then_inc(proj_mm, 1)

        def pe_ahead(pe, it, what, n):
            if what == "stat":
                pe_stat(pe, it, n)
            else:
                pe_layer0(pe, it, n)

        def pe_chunk(pe, it, ahead):
            def do_ahead(at):
                if ahead is not None:
                    for what in PE_AHEAD.get(at, ()):
                        pe_ahead(pe, ahead, *what)

            def do_qkv(w, part):
                if ahead is not None:
                    for n in QKV_AT.get(w, ((), ()))[part]:
                        pe_qkv(pe, ahead, n)

            for w in range(STEPS):
                q = PROJ_AT.get(w)
                if w < UN:
                    pe_turn(pe, it, w)
                if 1 <= w <= UN:
                    pe_vk(pe, it, w - 1)
                if q is not None:
                    pe_proj(pe, it, q, 0, ahead)
                    pe_proj(pe, it, q, 1, ahead)
                do_ahead(w)
                if q is not None:
                    pe_proj(pe, it, q, 2, ahead)
                    pe_proj(pe, it, q, 3, ahead)
                for i, n in enumerate(CONV_AT.get(w, ())):
                    pe_conv(pe, it, n)
                    do_ahead(w + 0.25 + 0.125 * i)
                do_qkv(w, 0)
                if 2 <= w <= UN + 1:
                    pe_out(pe, it, w - 2)
                if w >= 3:
                    pe_out_turn(pe, it, w - 3)
                do_qkv(w, 1)
                do_ahead(w + 0.5)
            for n in range(4):
                pe_proj(pe, it, 3, n, ahead)

        def v_norm(v, it, k, what):
            n = 2 * it + k
            src = xa
            if what == "sum":
                if k == 0:
                    v.wait_ge(x_in, 16 * KT * (it + 1))
                    wait(v, g_mm, 4 * it)
                else:
                    v.wait_ge(x1_ok, 4 * it + 4)
                    v.wait_ge(g_mm, 4 * it + 2)
                v.tensor_reduce(stat[:, :], by_image(src[:, :, :]), AX.X, ALU.add).then_inc(summed, 1)
            elif what == "centre":
                v.wait_ge(g_mm, 2 * n + 1)
                v.tensor_scalar(mean[:, :, :].rearrange("p t b -> p (t b)"), p_g[:, 0:KT * NB],
                                1.0 / (GS * S), None, ALU.mult).then_inc(mean_ok, 1)
                v.wait_ge(mean_ok, n + 1)
                if k == 0:
                    wait(v, qkv_mm, 12 * it)
                else:
                    v.wait_ge(l0_mm, 4 * it + 4)
                v.tensor_tensor(by_position(z[:, :, :]), by_position(src[:, :, :]),
                                over_positions(mean[:, :, :]), ALU.subtract).then_inc(centred, 1)
            elif what == "square_sum":
                v.wait_ge(squared, n + 1)
                v.tensor_reduce(stat[:, :], by_image(sq[:, :, :]), AX.X, ALU.add).then_inc(summed, 1)
            elif what == "var":
                v.wait_ge(g_mm, 2 * n + 2)
                v.tensor_scalar(var[:, :], p_g[:, 0:KT * NB], 1.0 / (GS * S), 1e-5,
                                ALU.mult, ALU.add).then_inc(var_ok, 1)
            else:
                v.wait_ge(rstd_ok, n + 1)
                v.tensor_tensor(by_position(z[:, :, :]), by_position(z[:, :, :]),
                                over_positions(rstd[:, :, :]), ALU.mult).then_inc(z_ok, 1)

        def v_layer0(v, it, n):
            m, h = n // 2, n % 2
            v.wait_ge(l0_mm, 4 * it + n + 1)
            cols = xa[:, m, HALF * h:HALF * h + HALF]
            v.scalar_tensor_tensor(cols, p_g[:, 0:HALF], W["b_sub"][:, m:m + 1], cols,
                                   ALU.add, ALU.add).then_inc(x1_ok, 1)

        def v_qkv(v, it, n):
            k, h = n // 2, n % 2
            m = ORDER[k]
            v.wait_ge(qkv_mm, 12 * it + n + 1)
            if h == 0:
                wait(v, out_mm if m % 3 == 0 else t_mm, UN * (it - 1) + (12 if m < 3 else 16))
            v.tensor_copy(qkv[:, m, HALF * h:HALF * h + HALF], p_stream[h][:, 0:HALF]).then_inc(qkv_ev, 1)

        def v_vk(v, it, u):
            v.wait_ge(vk_mm, UN * it + u + 1)
            wait(v, out_mm, UN * it + u - 1)
            dst = vk[:, u % 2, :, :, :].rearrange("p r i n -> p (r i) n")
            src = p_vk[:, u % 2, 0:4 * VC].rearrange("p (k n) -> p k n", k=4)
            v.tensor_tensor(dst[:, :, 0:128].rearrange("p k (c n) -> p k c n", c=HC),
                            src[:, :, 0:2 * D].unsqueeze(2).to_broadcast([128, 4, HC, 2 * D]),
                            W["mask_vo"][:, 0:128].rearrange("p (c n) -> p c n", c=HC).unsqueeze(1).to_broadcast([128, 4, HC, 2 * D]),
                            ALU.mult).then_inc(vk_ev, 1)
            v.tensor_tensor(dst[:, :, 128:VO], src[:, :, 2 * D:VC].to_broadcast([128, 4, 8]),
                            W["mask_vo"][:, 128:VO].unsqueeze(1).to_broadcast([128, 4, 8]),
                            ALU.mult).then_inc(vk_ev, 1)

        def v_norm_out(v, it, u):
            v.wait_ge(out_mm, UN * it + u + 1)
            v.tensor_scalar(den[:, :, :], p_out[:, :, 128:VO], 1e-15, None, ALU.add).then_inc(den_ok, 1)
            v.wait_ge(den_ok, UN * it + u + 1)
            v.reciprocal(rden[:, :, :], den[:, :, :]).then_inc(rden_ok, 1)
            v.wait_ge(rden_ok, UN * it + u + 1)
            wait(v, ot_mm, UN * it + u - 1)
            v.tensor_tensor(oN[:, u % 2, :, :].rearrange("p r (h d) -> p r h d", h=8),
                            p_out[:, :, 0:128].rearrange("p r (h d) -> p r h d", h=8),
                            rden[:, :, :].unsqueeze(3).to_broadcast([128, 2, 8, D]), ALU.mult).then_inc(on_ok, 1)

        def v_proj(v, it, q):
            for n in range(4):
                m, h = n // 2, n % 2
                v.wait_ge(proj_mm, 16 * it + 4 * q + n + 1)
                if q == 0:
                    v.wait_ge(xb_ok, KT * it + m + 1)
                else:
                    v.wait_ge(proj_ev, 16 * it + 4 * (q - 1) + n + 1)
                cols = xb[:, m, HALF * h:HALF * h + HALF]
                v.scalar_tensor_tensor(cols, p_stream[proj_bank(q, n)][:, 0:HALF], W["bn_scale"][:, m:m + 1], cols,
                                       ALU.mult, ALU.add).then_inc(proj_ev, 1)

        def v_ahead(v, it, what, n):
            if what == "layer0":
                v_layer0(v, it, n)
            else:
                v_norm(v, it, n, what)

        def v_chunk(v, it, ahead):
            def do_ahead(at):
                if ahead is not None:
                    for what in V_AHEAD.get(at, ()):
                        v_ahead(v, ahead, *what)

            def do_qkv(w, part):
                if ahead is not None:
                    for n in QKV_AT.get(w, ((), ()))[part]:
                        v_qkv(v, ahead, n)

            for w in range(STEPS):
                if 1 <= w <= UN:
                    v_vk(v, it, w - 1)
                if w in PROJ_AT:
                    v_proj(v, it, PROJ_AT[w])
                do_ahead(w)
                do_qkv(w, 0)
                if 2 <= w <= UN + 1:
                    v_norm_out(v, it, w - 2)
                do_ahead(w + 0.5)
                do_qkv(w, 1)
            v_proj(v, it, 3)

        def a_square(a, it, k):
            a.wait_ge(centred, 2 * it + k + 1)
            wait(a, summed, 4 * it + 2 * k)
            a.activation(sq[:, :, :], z[:, :, :], ACT.Square).then_inc(squared, 1)

        def a_turn(a, it, u):
            a.wait_ge(t_mm, UN * it + u + 1)
            wait(a, vk_mm, UN * it + u - 1)
            a.activation(kT[:, u % 2, :, :], p_t[0:PR, :, 0:128], ACT.Relu).then_inc(k_ev, 1)
            for i in range(2):
                a.activation(vT[:, u % 2, :, i, :, 0:2 * D],
                             p_t[0:PR, :, 128:256].rearrange("r q (c n) -> r q c n", c=HC), ACT.Copy,
                             scale=W["image_of"][:, i:i + 1]).then_inc(v_ev, 1)

        def a_out(a, it, u):
            q, w = u // QP, u % QP
            a.wait_ge(ot_mm, UN * it + u + 1)
            if w == 0:
                wait(a, proj_mm, 16 * it + 4 * q)
            a.activation(o[:, :].rearrange("p (s i b) -> p b i s", i=2, b=8)[:, 2 * w:2 * w + 2, :, :],
                         p_ot[:, :, 0:128].rearrange("p r (i s) -> p r i s", i=2)[:, :, :, 0:S],
                         ACT.Copy).then_inc(o_ev, 1)

        def a_conv(a, it, n):
            k, f = n // 2, n % 2
            a.wait_ge(conv_mm, 12 * it + n + 1)
            if f == 0:
                wait(a, back_w[k % 2], 16 * (3 * it + k // 2))
            a.activation(cy[:, k % 2, 4 * f:4 * f + 4, :].rearrange("p j n -> p (j n)"),
                         p_stream[f][0:XC, 0:4 * YB],
                         ACT.Relu if ORDER[k] % 3 < 2 else ACT.Copy).then_inc(conv_ev, 1)

        def a_chunk(a, it, ahead):
            for w in range(STEPS):
                if w < UN:
                    a_turn(a, it, w)
                for n in CONV_AT.get(w, ()):
                    a_conv(a, it, n)
                if ahead is not None and w in A_AHEAD:
                    a_square(a, ahead, A_AHEAD[w])
                if w >= 3:
                    a_out(a, it, w - 3)
                if ahead is not None and w + 0.5 in A_AHEAD:
                    a_square(a, ahead, A_AHEAD[w + 0.5])

        def sp_write(sp, it, k):
            sp.wait_ge(qkv_ev, 12 * it + 2 * k + 2)
            settle(sp, met_sp)
            sp.dma_start(fwd[ORDER[k]], qkv[:, ORDER[k], :]).then_inc(fwd_w[k], 16)

        def sp_read(sp, it, k):
            sp.wait_ge(fwd_w[k], 16 * (it + 1))
            settle(sp, met_sp)
            wait(sp, conv_mm, 12 * it + 2 * k - 2)
            for x in range(HW):
                sp.dma_start(cx[D * x:D * x + D, k % 2, :, :],
                             fwd[ORDER[k]].rearrange("(j c) (x n) -> x c j n", c=D, x=HW)[x]).then_inc(cx_in[k % 2], 16)

        def sp_back_write(sp, it, k):
            sp.wait_ge(conv_ev, 12 * it + 2 * k + 2)
            settle(sp, met_sp)
            sp.dma_start(back[ORDER[k]], cy[:, k % 2, :, :]).then_inc(back_w[k % 2], 16)

        def sp_back_read(sp, it, k):
            m = ORDER[k]
            sp.wait_ge(back_w[k % 2], 16 * (3 * it + k // 2 + 1))
            settle(sp, met_sp)
            if m % 3 == 0:
                sp.wait_ge(qr_ok, 2 * it + m // 3 + 1)
            else:
                sp.wait_ge(t_mm, UN * it + QP * (m // 3 + 1))
            settle(sp, met_sp)
            arrived = agg_q[m // 3] if m % 3 == 0 else agg_kv[m // 3]
            for j in range(8):
                sp.dma_start(qkv[D * j:D * j + D, m, :].rearrange("o (x n) -> o x n", x=HW),
                             back[m].rearrange("(x o) j n -> j o x n", o=D)[j]).then_inc(arrived, 16)

        def sp_qkv(sp, it):
            for k in range(2):
                sp_write(sp, it, k)
                sp_read(sp, it, k)
            for k in range(2, MT):
                sp_write(sp, it, k)

        def sp_chunk(sp, it, ahead):
            if ahead is not None:
                for m in range(KT):
                    sp.wait_ge(xb_ok, KT * it + m + 1)
                    settle(sp, met_sp)
                    sp.dma_start(xa[:, m, :], ins["x"][ahead][:, m, :]).then_inc(x_in, 16)
            for k in range(MT):
                sp_back_write(sp, it, k)
                if k + 2 < MT:
                    sp_read(sp, it, k + 2)
                sp_back_read(sp, it, k)
            if ahead is not None:
                sp_qkv(sp, ahead)
            sp.wait_ge(proj_ev, 16 * it + 16)
            settle(sp, met_sp)
            sp.dma_start(x2_out[it], xb[:, :, :]).then_inc(stored, 16)

        def g_start(g, it):
            wait(g, out_mm, UN * it - 2 * QP)
            for h in range(2):
                g.wait_ge(qkv_ev, 12 * it + 6 * h + 6)
                settle(g, met_g)
                g.tensor_scalar(qr[:, h, :], qkv[:, 3 * h, :], 0.0, None, ALU.max).then_inc(qr_ok, 1)
            g.wait_ge(x1_ok, 4 * it + 4)
            wait(g, stored, 16 * it)
            g.wait_ge(centred, 2 * it + 2)
            settle(g, met_g)
            for m in range(KT):
                g.tensor_scalar(xb[:, m, :], xa[:, m, :], W["bn_shift"][:, m:m + 1], None, ALU.add).then_inc(xb_ok, 1)

        def g_root(g, it, k):
            g.wait_ge(var_ok, 2 * it + k + 1)
            settle(g, met_g)
            g.tensor_tensor(rstd[:, :, :].rearrange("p t b -> p (t b)"), var[:, :], W["minus_half"][:, :],
                            ALU.pow).then_inc(rstd_ok, 1)

        def g_chunk(g, it, ahead):
            g_start(g, it)
            if ahead is not None:
                for k in range(2):
                    g_root(g, ahead, k)

        block = ctx.enter_context(nc.Block())

        @block.sync
        def _(sp):
            for m in range(KT):
                sp.dma_start(xa[:, m, :], ins["x"][0][:, m, :]).then_inc(x_in, 16)
            sp_qkv(sp, 0)
            sp_chunk(sp, 0, 1)
            with sp.Fori(1, chunks - 1) as it:
                sp_chunk(sp, it, it + 1)
            sp_chunk(sp, chunks - 1, None)
            sp.wait_ge(stored, 16 * chunks)

        @block.tensor
        def _(pe):
            pe.wait_ge(ones_ok, 6)
            for step in PE_AHEAD.values():
                for what in step:
                    pe_ahead(pe, 0, *what)
            for n in range(2 * MT):
                pe_qkv(pe, 0, n)
            pe_chunk(pe, 0, 1)
            with pe.Fori(1, chunks - 1) as it:
                pe_chunk(pe, it, it + 1)
            pe_chunk(pe, chunks - 1, None)

        @block.vector
        def _(v):
            for n in range(2):
                for pr in range(2):
                    v.tensor_copy(vT[:, n, pr, :, :, 2 * D:VC].rearrange("p i c o -> p i (c o)"),
                                  W["image_of"][:, :].unsqueeze(2).to_broadcast([PR, 2, HC])).then_inc(ones_ok, 1)
            v.memset(p_out[:, :, :], 1.0).then_inc(ones_ok, 1)
            v.memset(p_ot[:, :, :], 0.0).then_inc(ones_ok, 1)
            v.wait_ge(ones_ok, 6)
            for step in V_AHEAD.values():
                for what in step:
                    v_ahead(v, 0, *what)
            for n in range(2 * MT):
                v_qkv(v, 0, n)
            v_chunk(v, 0, 1)
            with v.Fori(1, chunks - 1) as it:
                v_chunk(v, it, it + 1)
            v_chunk(v, chunks - 1, None)

        @block.scalar
        def _(a):
            for k in range(2):
                a_square(a, 0, k)
            a_chunk(a, 0, 1)
            with a.Fori(1, chunks - 1) as it:
                a_chunk(a, it, it + 1)
            a_chunk(a, chunks - 1, None)

        @block.gpsimd
        def _(g):
            for k in range(2):
                g_root(g, 0, k)
            g_chunk(g, 0, 1)
            with g.Fori(1, chunks - 1) as it:
                g_chunk(g, it, it + 1)
            g_chunk(g, chunks - 1, None)


def gate_and_attention_phase(nc, bass, mybir, W, x2, out, ins, chunks):
    from contextlib import ExitStack
    f32 = mybir.dt.float32
    ALU = mybir.AluOpType
    ACT = mybir.ActivationFunctionType
    AX = mybir.AxisListType
    ctx = ExitStack()
    G = C // GS
    GR = 2 * G
    BH = NB // 2
    with ctx:
        def sb(name, shape):
            return ctx.enter_context(nc.sbuf_tensor(name, shape, f32))

        def ps(name, shape):
            return ctx.enter_context(nc.psum_tensor(name, shape, f32))

        def sem(name):
            return ctx.enter_context(nc.semaphore(name))

        x = [sb("x2", [128, KT, COLS]), sb("x3", [128, KT, COLS])]
        x2_gate = sb("x2_gate", [128, KT, COLS])
        x3_attend = sb("x3_attend", [128, KT, COLS])
        x4 = sb("x4", [128, KT, COLS])
        zc = [sb("zc2", [128, KT, COLS]), sb("zc3", [128, KT, COLS])]
        z = [sb("z2", [128, KT, COLS]), sb("z3", [128, KT, COLS])]
        sq = [sb("sq2", [128, KT, COLS]), sb("sq3", [128, KT, COLS])]
        stat = [sb("stat2", [128, KT * NB]), sb("stat3", [128, KT * NB])]
        mean = [sb("mean2", [128, KT, NB]), sb("mean3", [128, KT, NB])]
        var = [sb("var2", [128, KT * NB]), sb("var3", [128, KT * NB])]
        rstd = [sb("rstd2", [128, KT, NB]), sb("rstd3", [128, KT, NB])]
        prod = sb("prod", [128, KT, COLS])
        gapped = sb("gapped", [128, KT, COLS])
        sel = sb("sel", [128, KT, G])
        spread = sb("spread", [GR, KT, 128])
        hot_exact = ctx.enter_context(nc.sbuf_tensor("hot_exact", [GR, HALF], mybir.dt.bfloat16))
        spread_exact = ctx.enter_context(nc.sbuf_tensor("spread_exact", [GR, KT, 128], mybir.dt.bfloat16))
        countdown = sb("countdown", [GR, HALF])
        ruler = sb("ruler", [GR, HW * BH])
        s_sb = sb("s_sb", [GR, HALF])
        hot = sb("hot", [GR, HALF])
        best = sb("best", [GR, BH])
        last = sb("last", [GR, BH])
        idx = sb("idx", [GR, BH])
        row = sb("row", [GR, BH])
        col = sb("col", [GR, BH])
        dist = sb("dist", [GR, 2, HW * BH])
        dist2 = sb("dist2", [GR, 2, HW * BH])
        gauss = sb("gauss", [GR, 2, HW * BH])
        dsum = sb("dsum", [GR, HALF])
        gap_sim = sb("gap_sim", [GR, HALF])
        sim = sb("sim", [GR, HALF])
        simsq = sb("simsq", [GR, HALF])
        gate = sb("gate", [GR, HALF])
        ssum = sb("ssum", [GR, BH])
        smean = sb("smean", [GR, BH])
        ssq = sb("ssq", [GR, BH])
        svar = sb("svar", [GR, BH])
        sstd = sb("sstd", [GR, BH])
        sinv = sb("sinv", [GR, BH])
        qv = sb("qv", [128, KT, NB])
        gapc = sb("gapc", [128, KT * NB])
        gapm = sb("gapm", [128, KT, NB])
        half_par = sb("half_par", [GR, 2])
        half_zero = sb("half_zero", [GR, 1])
        inv_scale = sb("inv_scale", [GR, 1])
        log_norm = sb("log_norm", [GR, 1])
        f_sb = sb("f_sb", [G + 2, COLS])
        g_sb = sb("g_sb", [G + 2, COLS])
        hh = sb("hh", [PR, 8, C])
        sc = sb("sc", [PR, 2, 4, PR])
        smx = sb("smx", [PR, 2, 4])
        neg_max = sb("neg_max", [PR, 2, 4])
        ssm = sb("ssm", [PR, 2, 4])
        srec = sb("srec", [PR, 2, 4])
        beta = sb("beta", [PR, 2, 4, PR])
        p_wide = ps("p_wide", [128, 2, 512])
        p_group = ps("p_group", [128, 2, 512])
        p_a = ps("p_a", [128, 2, 512])
        p_b = ps("p_b", [128, 2, 512])
        p_rows = [p_wide, p_group]

        names = """x_in xg_in stored consts met_sp met_g params logged
            sum2 g_mm2 mean2 centred2 squared2 var2 rstd2 z2 sum3 g_mm3 mean3 centred3 squared3 var3 rstd3 z3
            s_mm s_ev best at_best counted last hot gapc gapm gapped hot_mm idx row col apart dist dist2 gauss
            picked qv prod gap_mm gap_ev sim_mm dsum sim_max sim ssum smean sim_centred sim_squared ssq svar
            sstd sstd_eps sinv context tanh gate_mm gated x3
            fg_mm fg_ev score_mm smx neg_max exp hh_mm hh_ev ssm srec probs bt_mm bt_ev o_mm x3_kept x3z x4_ok""".split()
        sems = {name: sem("p2_" + name) for name in names}

        def done(ins_, name):
            return ins_.then_inc(sems[name], 1)

        def wait(eng, name, count):
            if not isinstance(count, int) or count > 0:
                eng.wait_ge(sems[name], count)

        def by_image(ap):
            return ap.rearrange("p t (s b) -> p t b s", b=NB)

        def by_position(ap):
            return ap.rearrange("p t (s b) -> p t s b", b=NB)

        def over_positions(ap):
            return ap.unsqueeze(2).to_broadcast([128, KT, S, NB])

        def g_image(ap):
            return ap.rearrange("g (s b) -> g b s", b=BH)

        def g_position(ap):
            return ap.rearrange("g (s b) -> g s b", b=BH)

        def g_over(ap):
            return ap.unsqueeze(1).to_broadcast([GR, S, BH])

        def by_half(ap):
            return ap.rearrange("p (s i b) -> p i s b", i=2, b=BH)

        def rows_by_half(t):
            return p_rows[t][:, :, 0:HALF].rearrange("p i (s b) -> p i s b", b=BH)

        loads = [(sel[:, :, :], ins["c_sel"]), (spread[:, :, :], ins["c_spread"]),
                 (countdown[:, :], ins["c_countdown"]), (ruler[:, :], ins["c_ruler"]),
                 (g_sb[G:G + 2, :], ins["c_pair_g"]), (f_sb[G:G + 2, :], ins["c_pair_f"])]

        def v_sum(v, it, k):
            if k == 0:
                v.wait_ge(sems["x_in"], 16 * (it + 1))
            else:
                wait(v, "x3", it + 1)
            wait(v, f"g_mm{k + 2}", 2 * it)
            done(v.tensor_reduce(stat[k][:, :], by_image(x[k][:, :, :]), AX.X, ALU.add), f"sum{k + 2}")

        def v_mean(v, it, k):
            wait(v, f"g_mm{k + 2}", 2 * it + 1)
            wait(v, f"centred{k + 2}", it)
            done(v.tensor_scalar(mean[k][:, :, :].rearrange("p t b -> p (t b)"), p_wide[:, k, 0:KT * NB],
                                 1.0 / (GS * S), None, ALU.mult), f"mean{k + 2}")

        def v_centre(v, it, k):
            wait(v, f"mean{k + 2}", it + 1)
            wait(v, f"z{k + 2}", it)
            done(v.tensor_tensor(by_position(zc[k][:, :, :]), by_position(x[k][:, :, :]),
                                 over_positions(mean[k][:, :, :]), ALU.subtract), f"centred{k + 2}")
            if k == 0:
                wait(v, "gapm", it)
                done(v.scalar_tensor_tensor(gapc[:, :], stat[0][:, :], 1.0 / S,
                                            mean[0][:, :, :].rearrange("p t b -> p (t b)"),
                                            ALU.mult, ALU.subtract), "gapc")

        def v_square_sum(v, it, k):
            wait(v, f"squared{k + 2}", it + 1)
            if k == 0:
                wait(v, "gapc", it + 1)
            done(v.tensor_reduce(stat[k][:, :], by_image(sq[k][:, :, :]), AX.X, ALU.add), f"sum{k + 2}")

        def v_var(v, it, k):
            wait(v, f"g_mm{k + 2}", 2 * it + 2)
            done(v.tensor_scalar(var[k][:, :], p_wide[:, k, 0:KT * NB], 1.0 / (GS * S), 1e-5,
                                 ALU.mult, ALU.add), f"var{k + 2}")

        def v_scale(v, it, k):
            wait(v, f"rstd{k + 2}", it + 1)
            if k == 0:
                wait(v, "gated", 4 * it)
            else:
                wait(v, "hh_mm", 8 * it)
                wait(v, "x3z", it)
            done(v.tensor_tensor(by_position(z[k][:, :, :]), by_position(zc[k][:, :, :]),
                                 over_positions(rstd[k][:, :, :]), ALU.mult), f"z{k + 2}")

        def v_then(v, it, ins_, name):
            done(ins_, name)
            wait(v, name, it + 1)

        def v_gap(v, it):
            wait(v, "rstd2", it + 1)
            wait(v, "gapc", it + 1)
            wait(v, "gapped", it)
            done(v.tensor_tensor(gapm[:, :, :].rearrange("p t b -> p (t b)"), gapc[:, :],
                                 rstd[0][:, :, :].rearrange("p t b -> p (t b)"), ALU.mult), "gapm")

        def v_hot(v, it):
            wait(v, "s_ev", it + 1)
            v_then(v, it, v.tensor_reduce(best[:, :], g_image(s_sb[:, :]), AX.X, ALU.max), "best")
            wait(v, "hot_mm", 2 * it)
            v_then(v, it, v.tensor_tensor(g_position(hot[:, :]), g_position(s_sb[:, :]), g_over(best[:, :]),
                                          ALU.is_equal), "at_best")
            v_then(v, it, v.tensor_tensor(hot[:, :], hot[:, :], countdown[:, :], ALU.mult), "counted")
            v_then(v, it, v.tensor_reduce(last[:, :], g_image(hot[:, :]), AX.X, ALU.max), "last")
            done(v.tensor_tensor(g_position(hot_exact[:, :]), g_position(hot[:, :]), g_over(last[:, :]),
                                 ALU.is_equal), "hot")

        def v_dist(v, it):
            v_then(v, it, v.tensor_scalar(idx[:, :], last[:, :], -1.0, float(S), ALU.mult, ALU.add), "idx")
            for r in range(1, HW):
                if r == 1:
                    i = v.tensor_scalar(row[:, :], idx[:, :], float(HW * r), None, ALU.is_ge)
                else:
                    i = v.scalar_tensor_tensor(row[:, :], idx[:, :], float(HW * r), row[:, :], ALU.is_ge, ALU.add)
                done(i, "row")
                wait(v, "row", (HW - 1) * it + r)
            v_then(v, it, v.scalar_tensor_tensor(col[:, :], row[:, :], -float(HW), idx[:, :],
                                                 ALU.mult, ALU.add), "col")
            for k, at in enumerate((row, col)):
                done(v.tensor_tensor(dist[:, k, :].rearrange("g (y b) -> g y b", b=BH),
                                     ruler[:, :].rearrange("g (y b) -> g y b", b=BH),
                                     at[:, :].unsqueeze(1).to_broadcast([GR, HW, BH]), ALU.subtract), "apart")
            wait(v, "apart", 2 * it + 2)
            for k in range(2):
                done(v.tensor_scalar(dist[:, k, :], dist[:, k, :], W["theta"][:, k:k + 1], None, ALU.mult), "dist")

        def v_picked(v, it):
            for t in range(KT):
                wait(v, "hot_mm", 2 * it + t + 1)
                done(v.tensor_tensor(by_half(prod[:, t, :]), by_half(z[0][:, t, :]), rows_by_half(t),
                                     ALU.mult), "picked")
            wait(v, "picked", 2 * it + 2)
            v_then(v, it, v.tensor_reduce(qv[:, :, :], by_image(prod[:, :, :]), AX.X, ALU.add), "qv")
            done(v.tensor_tensor(by_position(prod[:, :, :]), by_position(z[0][:, :, :]),
                                 over_positions(qv[:, :, :]), ALU.mult), "prod")

        def v_dsum(v, it):
            wait(v, "gauss", it + 1)
            done(v.tensor_tensor(
                dsum[:, :].rearrange("g (x y b) -> g x y b", x=HW, y=HW),
                gauss[:, 0, :].rearrange("g (y b) -> g y b", b=BH).unsqueeze(1).to_broadcast([GR, HW, HW, BH]),
                gauss[:, 1, :].rearrange("g (x b) -> g x b", b=BH).unsqueeze(2).to_broadcast([GR, HW, HW, BH]),
                ALU.add), "dsum")

        def v_sim(v, it):
            wait(v, "dsum", it + 1)
            wait(v, "sim_mm", it + 1)
            v_then(v, it, v.scalar_tensor_tensor(sim[:, :], p_group[0:GR, 0, 0:HALF], half_zero[:, 0:1],
                                                 dsum[:, :], ALU.mult, ALU.mult), "sim_max")
            wait(v, "gap_ev", it + 1)
            v_then(v, it, v.tensor_tensor(sim[:, :], sim[:, :], gap_sim[:, :], ALU.add), "sim")
            v_then(v, it, v.tensor_reduce(ssum[:, :], g_image(sim[:, :]), AX.X, ALU.add), "ssum")
            v_then(v, it, v.tensor_scalar(smean[:, :], ssum[:, :], 1.0 / S, None, ALU.mult), "smean")
            done(v.tensor_tensor(g_position(sim[:, :]), g_position(sim[:, :]), g_over(smean[:, :]),
                                 ALU.subtract), "sim_centred")

        def v_spread_of_sim(v, it):
            wait(v, "sim_squared", it + 1)
            v_then(v, it, v.tensor_reduce(ssq[:, :], g_image(simsq[:, :]), AX.X, ALU.add), "ssq")
            done(v.tensor_scalar(svar[:, :], ssq[:, :], 1.0 / (S - 1), None, ALU.mult), "svar")

        def v_context(v, it):
            wait(v, "sstd", it + 1)
            v_then(v, it, v.tensor_scalar(sstd[:, :], sstd[:, :], 1e-5, None, ALU.add), "sstd_eps")
            v_then(v, it, v.reciprocal(sinv[:, :], sstd[:, :]), "sinv")
            done(v.tensor_tensor(g_position(sim[:, :]), g_position(sim[:, :]), g_over(sinv[:, :]),
                                 ALU.mult), "context")

        def v_x3(v, it):
            for t in range(KT):
                wait(v, "gate_mm", 2 * it + t + 1)
                if t == 0:
                    wait(v, "sim_mm", it + 1)
                for i in range(2):
                    done(v.scalar_tensor_tensor(by_half(prod[:, t, :])[:, i], rows_by_half(t)[:, i], 1.0,
                                                by_half(z[0][:, t, :])[:, i], ALU.add, ALU.mult), "gated")
            wait(v, "gated", 4 * it + 4)
            v.wait_ge(sems["xg_in"], 16 * (it + 1))
            wait(v, "centred3", it)
            wait(v, "x3_kept", it)
            done(v.scalar_tensor_tensor(x[1][:, :, :], prod[:, :, :], 0.5, x2_gate[:, :, :],
                                        ALU.mult, ALU.add), "x3")

        scores = p_a[0:PR, :, 0:4 * PR].rearrange("r h (q n) -> r h q n", q=4)

        def over(ap):
            return ap.unsqueeze(3).to_broadcast([PR, 2, 4, PR])

        def v_max(v, it):
            wait(v, "score_mm", 2 * it + 2)
            v_then(v, it, v.tensor_reduce(smx[:, :, :], scores, AX.X, ALU.max), "smx")
            wait(v, "exp", 8 * it)
            done(v.tensor_scalar(neg_max[:, :, :], smx[:, :, :], -1.0, None, ALU.mult), "neg_max")

        def v_probs(v, it):
            wait(v, "exp", 8 * it + 8)
            v_then(v, it, v.tensor_reduce(ssm[:, :, :], sc[:, :, :, :], AX.X, ALU.add), "ssm")
            v_then(v, it, v.reciprocal(srec[:, :, :], ssm[:, :, :]), "srec")
            done(v.tensor_tensor(sc[:, :, :, :], sc[:, :, :, :], over(srec[:, :, :]), ALU.mult), "probs")

        def v_x4(v, it, m):
            wait(v, "x3z", it + 1)
            for h in range(2):
                wait(v, "o_mm", 4 * it + 2 * m + h + 1)
                dst = x4[:, m, :].rearrange("p (r b) -> p b r", b=8)[:, 4 * h:4 * h + 4, :]
                done(v.scalar_tensor_tensor(dst, (p_a, p_b)[m][:, h, 0:4 * PR].rearrange("p (b r) -> p b r", b=4),
                                            W["gamma"][:, 0:1], dst, ALU.mult, ALU.add), "x4_ok")

        def v_body(v, intake, norm2, gate, norm3, attend):
            def run(step, chunk, *more):
                if chunk is not None:
                    step(v, chunk, *more)

            run(v_sum, norm3, 1)
            run(v_hot, gate)
            run(v_mean, norm3, 1)
            run(v_mean, norm2, 0)
            run(v_centre, norm3, 1)
            run(v_picked, gate)
            run(v_centre, norm2, 0)
            run(v_square_sum, norm3, 1)
            run(v_dist, gate)
            run(v_var, norm3, 1)
            run(v_max, attend)
            run(v_dsum, gate)
            run(v_sim, gate)
            run(v_spread_of_sim, gate)
            run(v_square_sum, norm2, 0)
            run(v_context, gate)
            run(v_var, norm2, 0)
            run(v_probs, attend)
            run(v_sum, intake, 0)
            run(v_x3, gate)
            run(v_scale, norm2, 0)
            run(v_gap, norm2)
            run(v_scale, norm3, 1)
            run(v_x4, attend, 0)
            run(v_x4, attend, 1)

        def pe_stat(pe, it, k, n):
            wait(pe, f"sum{k + 2}", 2 * it + n + 1)
            if n == 1:
                wait(pe, f"mean{k + 2}", it + 1)
            else:
                wait(pe, f"var{k + 2}", it)
            done(pe.matmul(p_wide[:, k, 0:KT * NB], W["mask8"][:, :], stat[k][:, :], start=True, stop=True),
                 f"g_mm{k + 2}")

        def pe_rows_read(pe, it, name, count):
            wait(pe, name, KT * count * it + count)

        def pe_sums_read(pe, it, k, name):
            wait(pe, f"{name}{k + 2}", it + 1)

        def pe_group_sum(pe, src, name):
            for t in range(KT):
                for i in range(2):
                    mm = pe.matmul(p_group[G * i:G * i + G, 0, 0:HALF], sel[:, t, :], by_half(src[:, t, :])[:, i],
                                   start=(t == 0), stop=(t == KT - 1))
            done(mm, name)

        def pe_spread(pe, sel_rows, src, t, name):
            for i in range(2):
                mm = pe.matmul(p_rows[t][:, i, 0:HALF], sel_rows[G * i:G * i + G, t, :],
                               src[G * i:G * i + G, :], start=True, stop=True)
            done(mm, name)

        def pe_sums(pe, it):
            wait(pe, "z2", it + 1)
            wait(pe, "gated", 4 * it)
            pe_group_sum(pe, z[0], "s_mm")

        def pe_gap(pe, it):
            wait(pe, "gapped", it + 1)
            wait(pe, "s_ev", it + 1)
            pe_group_sum(pe, gapped, "gap_mm")

        def pe_hot(pe, it):
            wait(pe, "hot", it + 1)
            for t in range(KT):
                if t == 1:
                    wait(pe, "gap_ev", it + 1)
                pe_spread(pe, spread_exact, hot_exact, t, "hot_mm")

        def pe_sim(pe, it):
            wait(pe, "prod", it + 1)
            pe_group_sum(pe, prod, "sim_mm")

        def pe_gate(pe, it):
            wait(pe, "tanh", it + 1)
            for t in range(KT):
                if t == 1:
                    wait(pe, "sim_max", it + 1)
                pe_spread(pe, spread, gate, t, "gate_mm")

        def pe_fg(pe, it):
            wait(pe, "z3", it + 1)
            wait(pe, "x4_ok", 4 * it - 2)
            for t in range(KT):
                for h in range(2):
                    mm = pe.matmul(p_a[2 * G * h:2 * G * h + 2 * G, 0, 0:HALF], W["wqk"][:, t, :],
                                   z[1][:, t, HALF * h:HALF * h + HALF], start=(t == 0), stop=(t == KT - 1))
            done(mm, "fg_mm")

        def pe_scores(pe, it):
            wait(pe, "fg_ev", 4 * it + 4)
            for h in range(2):
                for q in range(4):
                    f, g = (pair_of(t[:, :], 4 * h + q) for t in (f_sb, g_sb))
                    mm = pe.matmul(p_a[0:PR, h, PR * q:PR * q + PR], g, f, start=True, stop=True)
                done(mm, "score_mm")

        def pe_hh(pe, it, n):
            wait(pe, "z3", it + 1)
            if n < 2:
                wait(pe, "x4_ok", 4 * it)
            else:
                wait(pe, "hh_ev", 4 * it + n - 1)
            for q in range(2):
                for t in range(KT):
                    mm = pe.matmul(p_b[0:PR, n % 2, C * q:C * q + C], pair_of(z[1][:, t, :], 2 * n + q),
                                   W["wv"][:, t, :], start=(t == 0), stop=(t == KT - 1))
                done(mm, "hh_mm")

        def pe_turn(pe, it):
            wait(pe, "probs", it + 1)
            for h in range(2):
                wait(pe, "hh_ev", 4 * it + 3 + h)
                for q in range(4):
                    mm = pe.transpose(p_b[0:PR, h, PR * q:PR * q + PR], sc[:, h, q, :], W["ident"][0:PR, 0:PR])
                done(mm, "bt_mm")

        def pe_out(pe, it, m):
            for h in range(2):
                wait(pe, "bt_ev", 2 * it + h + 1)
                for q in range(4):
                    mm = pe.matmul((p_a, p_b)[m][:, h, PR * q:PR * q + PR],
                                   hh[:, 4 * h + q, 128 * m:128 * m + 128], beta[:, h, q, :],
                                   start=True, stop=True)
                done(mm, "o_mm")

        def pe_body(pe, intake, norm2, gate, norm3, attend):
            def run(step, chunk, *more):
                if chunk is not None:
                    step(pe, chunk, *more)

            run(pe_fg, attend)
            run(pe_gap, gate)
            run(pe_stat, norm3, 1, 0)
            run(pe_stat, norm2, 0, 0)
            run(pe_sums_read, norm3, 1, "mean")
            run(pe_sums_read, norm2, 0, "mean")
            run(pe_hot, gate)
            run(pe_scores, attend)
            run(pe_hh, attend, 0)
            run(pe_sim, gate)
            run(pe_rows_read, gate, "picked", 1)
            run(pe_stat, norm3, 1, 1)
            run(pe_hh, attend, 1)
            run(pe_hh, attend, 2)
            run(pe_stat, norm2, 0, 1)
            run(pe_sums_read, norm3, 1, "var")
            run(pe_sums_read, norm2, 0, "var")
            run(pe_gate, gate)
            run(pe_hh, attend, 3)
            run(pe_turn, attend)
            run(pe_out, attend, 0)
            run(pe_sums, norm2)
            run(pe_out, attend, 1)
            run(pe_rows_read, gate, "gated", 2)

        def a_square(a, it, k):
            wait(a, f"centred{k + 2}", it + 1)
            done(a.activation(sq[k][:, :, :], zc[k][:, :, :], ACT.Square), f"squared{k + 2}")

        def a_keep(a, it):
            wait(a, "x3", it + 1)
            wait(a, "x3z", it)
            done(a.activation(x3_attend[:, :, :], x[1][:, :, :], ACT.Copy), "x3_kept")

        def a_sums(a, it):
            wait(a, "s_mm", it + 1)
            done(a.activation(s_sb[:, :], p_group[0:GR, 0, 0:HALF], ACT.Copy), "s_ev")

        def a_gap(a, it):
            wait(a, "gap_mm", it + 1)
            done(a.activation(gap_sim[:, :], p_group[0:GR, 0, 0:HALF], ACT.Copy,
                              scale=W["g_par"][:, 2:3]), "gap_ev")

        def a_gauss(a, it):
            wait(a, "dist", 2 * it + 2)
            done(a.activation(dist2[:, :, :], dist[:, :, :], ACT.Square, scale=inv_scale[:, 0:1]), "dist2")
            wait(a, "dist2", it + 1)
            done(a.activation(gauss[:, :, :], dist2[:, :, :], ACT.Exp, scale=-0.5, bias=log_norm[:, 0:1]), "gauss")

        def a_sim_square(a, it):
            wait(a, "sim_centred", it + 1)
            done(a.activation(simsq[:, :], sim[:, :], ACT.Square), "sim_squared")

        def a_tanh(a, it):
            wait(a, "context", it + 1)
            wait(a, "gate_mm", 2 * it)
            done(a.activation(gate[:, :], sim[:, :], ACT.Tanh, scale=half_par[:, 0:1], bias=half_par[:, 1:2]), "tanh")

        def a_fg(a, it):
            wait(a, "fg_mm", it + 1)
            wait(a, "score_mm", 2 * it)
            for h in range(2):
                for k, dst in enumerate((f_sb, g_sb)):
                    done(a.activation(dst[0:G, HALF * h:HALF * h + HALF], p_a[2 * G * h + G * k:2 * G * h + G * k + G, 0, 0:HALF],
                                      ACT.Copy), "fg_ev")

        def a_exp(a, it):
            wait(a, "neg_max", it + 1)
            wait(a, "bt_mm", 2 * it)
            for h in range(2):
                for q in range(4):
                    done(a.activation(sc[:, h, q, :], scores[:, h, q, :], ACT.Exp, bias=neg_max[:, h, q:q + 1]), "exp")

        def a_hh(a, it, n):
            wait(a, "hh_mm", 8 * it + 2 * n + 2)
            if n == 0:
                wait(a, "o_mm", 4 * it)
            done(a.activation(hh[:, 2 * n:2 * n + 2, :], p_b[0:PR, n % 2, :].rearrange("r (q c) -> r q c", q=2),
                              ACT.Copy), "hh_ev")

        def a_beta(a, it):
            for h in range(2):
                wait(a, "bt_mm", 2 * it + h + 1)
                done(a.activation(beta[:, h, :, :], p_b[0:PR, h, 0:4 * PR].rearrange("r (q n) -> r q n", q=4),
                                  ACT.Copy), "bt_ev")

        def a_body(a, intake, norm2, gate, norm3, attend):
            def run(step, chunk, *more):
                if chunk is not None:
                    step(a, chunk, *more)

            run(a_fg, attend)
            run(a_gap, gate)
            run(a_keep, norm3)
            run(a_square, norm3, 1)
            run(a_hh, attend, 0)
            run(a_square, norm2, 0)
            run(a_gauss, gate)
            run(a_exp, attend)
            run(a_hh, attend, 1)
            run(a_hh, attend, 2)
            run(a_sim_square, gate)
            run(a_tanh, gate)
            run(a_hh, attend, 3)
            run(a_beta, attend)
            run(a_sums, norm2)

        def g_root(g, it, k):
            wait(g, f"var{k + 2}", it + 1)
            wait(g, f"z{k + 2}", it)
            if k == 0:
                wait(g, "gapm", it)
            settle(g, sems["met_g"])
            done(g.tensor_tensor(rstd[k][:, :, :].rearrange("p t b -> p (t b)"), var[k][:, :], W["minus_half"][:, :],
                                 ALU.pow), f"rstd{k + 2}")

        def g_gapped(g, it):
            wait(g, "gapm", it + 1)
            wait(g, "gap_mm", it)
            done(g.tensor_tensor(by_position(gapped[:, :, :]), by_position(z[0][:, :, :]),
                                 over_positions(gapm[:, :, :]), ALU.mult), "gapped")

        def g_x3z(g, it):
            wait(g, "z3", it + 1)
            wait(g, "x3_kept", it + 1)
            wait(g, "stored", 16 * it)
            done(g.tensor_tensor(x4[:, :, :], x3_attend[:, :, :], z[1][:, :, :], ALU.add), "x3z")

        def g_deviation(g, it):
            wait(g, "svar", it + 1)
            done(g.tensor_tensor(sstd[:, :], svar[:, :], W["plus_half"][:, :], ALU.pow), "sstd")

        def g_body(g, intake, norm2, gate, norm3, attend):
            def run(step, chunk, *more):
                if chunk is not None:
                    step(g, chunk, *more)

            run(g_x3z, attend)
            run(g_root, norm3, 1)
            run(g_deviation, gate)
            run(g_root, norm2, 0)
            run(g_gapped, norm2)

        def sp_load(sp, it):
            wait(sp, "centred2", it)
            settle(sp, sems["met_sp"])
            sp.dma_start(x[0][:, :, :], x2[it]).then_inc(sems["x_in"], 16)

        def sp_load_gate(sp, it):
            wait(sp, "x3", it)
            settle(sp, sems["met_sp"])
            sp.dma_start(x2_gate[:, :, :], x2[it]).then_inc(sems["xg_in"], 16)

        def sp_store(sp, it):
            wait(sp, "x4_ok", 4 * it + 4)
            settle(sp, sems["met_sp"])
            sp.dma_start(out[it], x4[:, :, :]).then_inc(sems["stored"], 16)

        def sp_body(sp, intake, norm2, gate, norm3, attend):
            def run(step, chunk):
                if chunk is not None:
                    step(sp, chunk)

            run(sp_load_gate, gate)
            run(sp_load, intake)
            run(sp_store, attend)

        def bodies(eng, body):
            def peeled(first, end):
                for r in range(first, end):
                    body(eng, *[r - k if 0 <= r - k < chunks else None for k in range(5)])

            peeled(0, 5)
            with eng.Fori(5, chunks) as r:
                body(eng, r, r - 1, r - 2, r - 3, r - 4)
            peeled(chunks, chunks + 4)

        block = ctx.enter_context(nc.Block())

        @block.sync
        def _(sp):
            for dst, src in loads:
                sp.dma_start(dst, src).then_inc(sems["consts"], 16)
            bodies(sp, sp_body)
            sp.wait_ge(sems["stored"], 16 * chunks)

        @block.tensor
        def _(pe):
            pe.wait_ge(sems["consts"], 16 * len(loads))
            pe.wait_ge(sems["params"], 5)
            bodies(pe, pe_body)

        @block.vector
        def _(v):
            v.wait_ge(sems["consts"], 16 * len(loads))
            done(v.tensor_scalar(half_par[:, :], W["g_par"][:, 0:2], 0.5, None, ALU.mult), "params")
            done(v.tensor_scalar(half_zero[:, :], W["g_par"][:, 3:4], 0.5, None, ALU.mult), "params")
            done(v.reciprocal(inv_scale[:, :], W["theta"][:, 2:3]), "params")
            done(v.tensor_copy(spread_exact[:, :, :], spread[:, :, :]), "params")
            v.wait_ge(sems["logged"], 1)
            done(v.tensor_scalar(log_norm[:, :], log_norm[:, :], -1.0, -0.9189385332046727,
                                 ALU.mult, ALU.add), "params")
            v.wait_ge(sems["params"], 5)
            bodies(v, v_body)

        @block.scalar
        def _(a):
            done(a.activation(log_norm[:, :], W["theta"][:, 2:3], ACT.Ln), "logged")
            a.wait_ge(sems["params"], 5)
            bodies(a, a_body)

        @block.gpsimd
        def _(g):
            bodies(g, g_body)


def program(nc, ins, out, chunks, n_classes):
    import concourse.bass as bass
    from concourse import mybir
    from contextlib import ExitStack
    f32 = mybir.dt.float32
    x2 = nc.dram_tensor("x2_scratch", (chunks, 128, KT, COLS), f32, kind="Internal").ap()
    fwd = nc.dram_tensor("qkv_scratch", (MT, 128, COLS), f32, kind="Internal").ap()
    back = nc.dram_tensor("agg_scratch", (MT, XC, 8, YB), f32, kind="Internal").ap()
    ctx = ExitStack()
    with ctx:
        W = {}
        for name, shape in (
            ("w_qkv", [128, KT, 3 * C]), ("w_proj", [128, 4, C]), ("wv", [128, KT, C]), ("wqk", [128, KT, 64]),
            ("w_sub", [128, KT, C]), ("b_sub", [128, KT]), ("mask8", [128, 128]), ("mask_vo", [128, VO]),
            ("ident", [128, 128]), ("image_of", [PR, 2]), ("bn_scale", [128, KT]), ("bn_shift", [128, KT]),
            ("g_par", [64, 4]), ("theta", [64, 3]), ("gamma", [128, 1]),
            ("minus_half", [128, KT * NB]), ("plus_half", [64, NB // 2]),
        ):
            W[name] = ctx.enter_context(nc.sbuf_tensor(name, shape, f32))
        with nc.sbuf_tensor("conv", [XC, 48, TAPS * XC], f32) as conv:
            W["conv"] = conv
            setup_phase(nc, bass, mybir, ins, W, n_classes)
            layer_one_phase(nc, bass, mybir, ins, W, x2, fwd, back, chunks)
        gate_and_attention_phase(nc, bass, mybir, W, x2, out, ins, chunks)


def constants():
    import numpy as np
    f = np.float32
    p = np.arange(128)
    xo = np.arange(XC) // D
    s = np.arange(PR) % 2
    i = np.arange(COLS) % NB // 8
    xs, ys = np.divmod(np.arange(S), HW)
    g = np.arange(32)
    return {
        "c_mask8": (p[:, None] // GS == p[None] // GS).astype(f),
        "c_mask_vo": np.concatenate([p[:, None] // D == p[None] // D, p[:, None] // D == np.arange(8)[None]], 1).astype(f),
        "c_ident": np.eye(128, dtype=f),
        "c_image_of": (s[:, None] == np.arange(2)[None]).astype(f),
        "c_taps": (xo[:, None, None] - np.arange(HW)[None, None] + 2 == np.arange(TAPS)[None, :, None]).astype(f).reshape(XC, -1),
        "c_earlier": (np.arange(C)[None, None] < (128 * np.arange(KT)[None, :, None] + p[:, None, None])).astype(f),
        "c_iota": np.broadcast_to(np.arange(C, dtype=f), (128, C)).copy(),
        "c_sel": (16 * np.arange(KT)[None, :, None] + p[:, None, None] // GS == g[None, None]).astype(f),
        "c_spread": (16 * np.arange(KT)[None, :, None] + p[None, None] // GS == np.tile(g, 2)[:, None, None]).astype(f),
        "c_countdown": np.broadcast_to((S - (ys * HW + xs)).astype(f)[None, :, None], (64, S, NB // 2)).reshape(64, HALF).copy(),
        "c_ruler": np.broadcast_to(np.arange(HW, dtype=f)[None, :, None], (64, HW, NB // 2)).reshape(64, -1).copy(),
        "c_pair_g": ((i[None] == np.arange(2)[:, None]) * -BIG).astype(f),
        "c_pair_f": (i[None] != np.arange(2)[:, None]).astype(f),
    }


def kernel(x, L0_conv_labels, L0_conv_weight, L0_conv_bias, L1_conv_w_qkv, L1_conv_w_dw, L1_conv_w_pw,
           L1_conv_w_proj, L1_conv_bn_gamma, L1_conv_bn_beta, L1_conv_bn_mean, L1_conv_bn_var, L2_conv_weight,
           L2_conv_bias, L2_conv_one, L2_conv_zero, L2_conv_theta, L2_conv_scale, L3_conv_Wq, L3_conv_Wk,
           L3_conv_Wv, L3_conv_gamma):
    import numpy as np
    import concourse.bacc as bacc
    from concourse import mybir
    from concourse.bass_utils import run_bass_kernel_spmd

    x = np.asarray(x)
    chunks = x.shape[0] // NB
    n_classes = L0_conv_weight.shape[0]

    def contiguous(a):
        return np.ascontiguousarray(a)

    def heads(a):
        a = np.asarray(a)
        r = a.reshape((2, 8, 3, D) + a.shape[1:])
        return np.moveaxis(r, 2, 1)

    wq = np.asarray(L1_conv_w_qkv).reshape(3 * C, C)
    w_qkv = heads(wq).reshape(3 * C, KT, 128).transpose(2, 1, 0)
    w_pw = heads(np.asarray(L1_conv_w_pw).reshape(3 * C, D)).reshape(48, D, D).transpose(2, 0, 1)
    w_dw = heads(np.asarray(L1_conv_w_dw).reshape(3 * C, TAPS, TAPS)).reshape(48, D, TAPS, TAPS)
    w_dw = w_dw.transpose(1, 0, 2, 3).reshape(D, 48 * TAPS, TAPS)
    w_proj = np.asarray(L1_conv_w_proj).reshape(C, 4, 128).transpose(2, 1, 0)
    wv = np.asarray(L3_conv_Wv).T.reshape(KT, 128, C).transpose(1, 0, 2)
    wqk = np.concatenate([np.asarray(L3_conv_Wq), np.asarray(L3_conv_Wk)], 0).T.reshape(KT, 128, 64).transpose(1, 0, 2)
    arrays = {
        "x": contiguous(x.reshape(chunks, NB, KT, 128, HW, HW).transpose(0, 3, 2, 5, 4, 1).reshape(chunks, 128, KT, COLS)),
        "labels": np.asarray(L0_conv_labels), "weight": np.asarray(L0_conv_weight).reshape(n_classes, C),
        "bias": np.asarray(L0_conv_bias).reshape(n_classes, 1),
        "w_qkv": contiguous(w_qkv), "w_pw": contiguous(w_pw), "w_dw": contiguous(w_dw), "w_proj": contiguous(w_proj),
        "wv": contiguous(wv), "wqk": contiguous(wqk),
        "labels_by_row": contiguous(np.asarray(L0_conv_labels).reshape(KT, 128).T),
        "bn": contiguous(np.stack([np.asarray(a).reshape(KT, 128) for a in (
            L1_conv_bn_gamma, L1_conv_bn_beta, L1_conv_bn_mean, L1_conv_bn_var)]).transpose(2, 0, 1)),
        "g_par": contiguous(np.tile(np.stack([np.asarray(a).reshape(32) for a in (
            L2_conv_weight, L2_conv_bias, L2_conv_one, L2_conv_zero)], 1), (2, 1))),
        "theta": np.concatenate([np.asarray(L2_conv_theta).reshape(2), np.asarray(L2_conv_scale).reshape(1)]),
        "gamma": np.asarray(L3_conv_gamma).reshape(1),
        **constants(),
    }
    nc = bacc.Bacc("TRN2", target_bir_lowering=False, num_devices=1)
    ins = {n: nc.dram_tensor("in_" + n, a.shape, mybir.dt.from_np(a.dtype), kind="ExternalInput").ap()
           for n, a in arrays.items()}
    out = nc.dram_tensor("out", (chunks, 128, KT, COLS), mybir.dt.float32, kind="ExternalOutput").ap()
    program(nc, ins, out, chunks, n_classes)
    r = run_bass_kernel_spmd(nc, [{"in_" + n: a for n, a in arrays.items()}], core_ids=[0])
    got = r.results[0]["out"].reshape(chunks, 128, KT, HW, HW, NB)
    return contiguous(got.transpose(0, 5, 2, 1, 4, 3).reshape(x.shape))
```
